# Optimizing a Trainium2 kernel written in Bass

```python
import numpy as np
import jax
import jax.numpy as jnp

def _softmax(x, axis=-1):
    return jax.nn.softmax(x, axis=axis)

def _gelu(x):
    return jax.nn.gelu(x, approximate=True)

def _silu(x):
    return jax.nn.silu(x)

def _sigmoid(x):
    return jax.nn.sigmoid(x)

def _layernorm(x, axis=-1, eps=1e-05):
    m = jnp.mean(x, axis=axis, keepdims=True)
    v = jnp.var(x, axis=axis, keepdims=True)
    return (x - m) / jnp.sqrt(v + eps)

def _scatter_add(tgt, idx, src, axis=0):
    return tgt.at[idx].add(src)

def _segment_sum(src, seg, n):
    return jax.ops.segment_sum(src, seg, n)
kernel_name = 'mk_gnn_ffn_d2_gnn_r32_13c8d6'

def setup_inputs(seed: int=0):
    np.random.seed(seed)
    _w = jnp.asarray

    def _rec_inputs():
        import jax
        import jax.numpy as jnp
        _gk = jax.random.key(seed)
        x = -0.0006008 + 1.001 * jax.random.normal(jax.random.fold_in(_gk, 1), (3125, 256), jnp.float32)
        _s = jax.random.randint(jax.random.fold_in(_gk, 2), (25000,), 0, 3125, jnp.int32)
        _d = jax.random.randint(jax.random.fold_in(_gk, 3), (25000,), 0, 3125, jnp.int32)
        _loop = jnp.arange(3125, dtype=jnp.int32)
        src = jnp.concatenate([_s, _d, _loop])
        dst = jnp.concatenate([_d, _s, _loop])
        _o = jnp.argsort(dst, stable=True)
        src = src[_o]
        dst = dst[_o]
        edge_attr_16 = 0.000130101 + 1.00012 * jax.random.normal(jax.random.fold_in(_gk, 11), (53125, 16), jnp.float32)
        return (x, src, dst, edge_attr_16)
    x, src, dst, edge_attr_16 = _rec_inputs()

    def _L0_gnn_setup():
        import jax, jax.numpy as jnp
        import numpy as np
        N, NODE_DIM, EDGE_DIM, HIDDEN, E = (10000, 256, 16, 512, 10000)
        key = jax.random.key(seed)
        ks = jax.random.split(key, 12)

        def lin(kw, kb, fan_in, fan_out):
            bound = 1.0 / np.sqrt(fan_in)
            W = jax.random.uniform(kw, (fan_in, fan_out), jnp.float32, -bound, bound)
            b = jax.random.uniform(kb, (fan_out,), jnp.float32, -bound, bound)
            return (W, b)
        node_features = jax.random.normal(ks[0], (N, NODE_DIM), jnp.float32)
        edge_index = jax.random.randint(ks[1], (2, E), 0, N, jnp.int32)
        edge_features = jax.random.normal(ks[2], (E, EDGE_DIM), jnp.float32)
        mW1, mb1 = lin(ks[3], ks[4], 2 * NODE_DIM + EDGE_DIM, HIDDEN)
        mW2, mb2 = lin(ks[5], ks[6], HIDDEN, NODE_DIM)
        uW1, ub1 = lin(ks[7], ks[8], 2 * NODE_DIM, HIDDEN)
        uW2, ub2 = lin(ks[9], ks[10], HIDDEN, NODE_DIM)
        return {'node_features': node_features, 'edge_index': edge_index, 'edge_features': edge_features, 'mW1': mW1, 'mb1': mb1, 'mW2': mW2, 'mb2': mb2, 'uW1': uW1, 'ub1': ub1, 'uW2': uW2, 'ub2': ub2}
    _L0_gnn_all = _L0_gnn_setup()
    _L0_gnn_in = {k: v for k, v in _L0_gnn_all.items() if k in ('mW1', 'mb1', 'mW2', 'mb2', 'uW1', 'ub1', 'uW2', 'ub2')}
    del _L0_gnn_all

    def _L0_ffn_setup():
        import jax, jax.numpy as jnp
        import numpy as np
        B, A = (128, 8)
        IN, OUT = (256, 256)
        SH1, SH2 = (256, 128)
        EH1, EH2 = (128, 64)
        E, TOPK = (4, 2)

        def _shared_mlp(x, W1, b1, W2, b2, W3, b3):
            h = jax.nn.relu(x @ W1 + b1)
            h = jax.nn.relu(h @ W2 + b2)
            return h @ W3 + b3

        def _experts_mlp(x, eW1, eb1, eW2, eb2, eW3, eb3):
            h = jax.nn.relu(jnp.einsum('baf,efh->ebah', x, eW1) + eb1[:, None, None, :])
            h = jax.nn.relu(jnp.einsum('ebah,ehg->ebag', h, eW2) + eb2[:, None, None, :])
            o = jnp.einsum('ebag,ego->ebao', h, eW3) + eb3[:, None, None, :]
            return jnp.moveaxis(o, 0, -1)
        key = jax.random.key(seed)
        ks = jax.random.split(key, 16)
        s = 0.05
        return {'x': jax.random.normal(ks[0], (B, A, IN), jnp.float32), 'sW1': jax.random.normal(ks[1], (IN, SH1), jnp.float32) * s, 'sb1': jnp.zeros((SH1,), jnp.float32), 'sW2': jax.random.normal(ks[2], (SH1, SH2), jnp.float32) * s, 'sb2': jnp.zeros((SH2,), jnp.float32), 'sW3': jax.random.normal(ks[3], (SH2, OUT), jnp.float32) * s, 'sb3': jnp.zeros((OUT,), jnp.float32), 'eW1': jax.random.normal(ks[4], (E, IN, EH1), jnp.float32) * s, 'eb1': jnp.zeros((E, EH1), jnp.float32), 'eW2': jax.random.normal(ks[5], (E, EH1, EH2), jnp.float32) * s, 'eb2': jnp.zeros((E, EH2), jnp.float32), 'eW3': jax.random.normal(ks[6], (E, EH2, OUT), jnp.float32) * s, 'eb3': jnp.zeros((E, OUT), jnp.float32), 'gW': jax.random.normal(ks[7], (IN, E), jnp.float32) * s, 'gb': jnp.zeros((E,), jnp.float32)}
    _L0_ffn_all = _L0_ffn_setup()
    _L0_ffn_in = {k: v for k, v in _L0_ffn_all.items() if k in ('sW1', 'sb1', 'sW2', 'sb2', 'sW3', 'sb3', 'eW1', 'eb1', 'eW2', 'eb2', 'eW3', 'eb3', 'gW', 'gb')}
    del _L0_ffn_all

    def _L1_gnn_setup():
        import jax, jax.numpy as jnp
        import numpy as np
        N_NODES = 3125
        N_EDGES = 100000
        D_IN = 256
        D_HID = 256
        D_OUT = 256

        def _sage_conv(x, src, tgt, W_l, b_l, W_r):
            n = x.shape[0]
            msgs = x[src]
            agg = jax.ops.segment_sum(msgs, tgt, num_segments=n)
            deg = jax.ops.segment_sum(jnp.ones((src.shape[0],), x.dtype), tgt, num_segments=n)
            agg = agg / jnp.maximum(deg, 1.0)[:, None]
            return agg @ W_l + b_l + x @ W_r
        key = jax.random.key(seed)
        ks = jax.random.split(key, 8)
        x = jax.random.normal(ks[0], (N_NODES, D_IN), dtype=jnp.float32)
        edge_index = jax.random.randint(ks[1], (2, N_EDGES), 0, N_NODES, dtype=jnp.int64)
        s1 = 1.0 / np.sqrt(D_IN)
        s2 = 1.0 / np.sqrt(D_HID)
        return {'x': x, 'edge_index': edge_index, 'W_l1': jax.random.uniform(ks[2], (D_IN, D_HID), jnp.float32, -s1, s1), 'b1': jnp.zeros((D_HID,), jnp.float32), 'W_r1': jax.random.uniform(ks[3], (D_IN, D_HID), jnp.float32, -s1, s1), 'W_l2': jax.random.uniform(ks[4], (D_HID, D_OUT), jnp.float32, -s2, s2), 'b2': jnp.zeros((D_OUT,), jnp.float32), 'W_r2': jax.random.uniform(ks[5], (D_HID, D_OUT), jnp.float32, -s2, s2)}
    _L1_gnn_all = _L1_gnn_setup()
    _L1_gnn_in = {k: v for k, v in _L1_gnn_all.items() if k in ('W_l1', 'b1', 'W_r1', 'W_l2', 'b2', 'W_r2')}
    del _L1_gnn_all

    def _L1_ffn_setup():
        import jax, jax.numpy as jnp
        import numpy as np
        B, S, D = (8, 128, 256)
        H = 4 * D
        CAPACITY = 0.5
        key = jax.random.key(seed)
        ks = jax.random.split(key, 6)
        x = jax.random.normal(ks[0], (B, S, D), dtype=jnp.float32)
        attention_mask = jnp.zeros((B, 1, 1, S), dtype=jnp.float32)
        wr = jax.random.normal(ks[1], (D, 1), dtype=jnp.float32) * 0.02
        br = jnp.zeros((1,), dtype=jnp.float32)
        w1 = jax.random.normal(ks[2], (D, H), dtype=jnp.float32) * 0.02
        b1 = jnp.zeros((H,), dtype=jnp.float32)
        w2 = jax.random.normal(ks[3], (H, D), dtype=jnp.float32) * 0.02
        b2 = jnp.zeros((D,), dtype=jnp.float32)
        return {'x': x, 'attention_mask': attention_mask, 'wr': wr, 'br': br, 'w1': w1, 'b1': b1, 'w2': w2, 'b2': b2}
    _L1_ffn_all = _L1_ffn_setup()
    _L1_ffn_in = {k: v for k, v in _L1_ffn_all.items() if k in ('attention_mask', 'wr', 'br', 'w1', 'b1', 'w2', 'b2')}
    del _L1_ffn_all
    return {'x': x, 'src': src, 'dst': dst, 'edge_attr_16': edge_attr_16, 'L0_gnn_mW1': _L0_gnn_in['mW1'], 'L0_gnn_mb1': _L0_gnn_in['mb1'], 'L0_gnn_mW2': _L0_gnn_in['mW2'], 'L0_gnn_mb2': _L0_gnn_in['mb2'], 'L0_gnn_uW1': _L0_gnn_in['uW1'], 'L0_gnn_ub1': _L0_gnn_in['ub1'], 'L0_gnn_uW2': _L0_gnn_in['uW2'], 'L0_gnn_ub2': _L0_gnn_in['ub2'], 'L0_ffn_sW1': _L0_ffn_in['sW1'], 'L0_ffn_sb1': _L0_ffn_in['sb1'], 'L0_ffn_sW2': _L0_ffn_in['sW2'], 'L0_ffn_sb2': _L0_ffn_in['sb2'], 'L0_ffn_sW3': _L0_ffn_in['sW3'], 'L0_ffn_sb3': _L0_ffn_in['sb3'], 'L0_ffn_eW1': _L0_ffn_in['eW1'], 'L0_ffn_eb1': _L0_ffn_in['eb1'], 'L0_ffn_eW2': _L0_ffn_in['eW2'], 'L0_ffn_eb2': _L0_ffn_in['eb2'], 'L0_ffn_eW3': _L0_ffn_in['eW3'], 'L0_ffn_eb3': _L0_ffn_in['eb3'], 'L0_ffn_gW': _L0_ffn_in['gW'], 'L0_ffn_gb': _L0_ffn_in['gb'], 'L1_gnn_W_l1': _L1_gnn_in['W_l1'], 'L1_gnn_b1': _L1_gnn_in['b1'], 'L1_gnn_W_r1': _L1_gnn_in['W_r1'], 'L1_gnn_W_l2': _L1_gnn_in['W_l2'], 'L1_gnn_b2': _L1_gnn_in['b2'], 'L1_gnn_W_r2': _L1_gnn_in['W_r2'], 'L1_ffn_attention_mask': _L1_ffn_in['attention_mask'], 'L1_ffn_wr': _L1_ffn_in['wr'], 'L1_ffn_br': _L1_ffn_in['br'], 'L1_ffn_w1': _L1_ffn_in['w1'], 'L1_ffn_b1': _L1_ffn_in['b1'], 'L1_ffn_w2': _L1_ffn_in['w2'], 'L1_ffn_b2': _L1_ffn_in['b2']}

def reference(x, src, dst, edge_attr_16, L0_gnn_mW1, L0_gnn_mb1, L0_gnn_mW2, L0_gnn_mb2, L0_gnn_uW1, L0_gnn_ub1, L0_gnn_uW2, L0_gnn_ub2, L0_ffn_sW1, L0_ffn_sb1, L0_ffn_sW2, L0_ffn_sb2, L0_ffn_sW3, L0_ffn_sb3, L0_ffn_eW1, L0_ffn_eb1, L0_ffn_eW2, L0_ffn_eb2, L0_ffn_eW3, L0_ffn_eb3, L0_ffn_gW, L0_ffn_gb, L1_gnn_W_l1, L1_gnn_b1, L1_gnn_W_r1, L1_gnn_W_l2, L1_gnn_b2, L1_gnn_W_r2, L1_ffn_attention_mask, L1_ffn_wr, L1_ffn_br, L1_ffn_w1, L1_ffn_b1, L1_ffn_w2, L1_ffn_b2):
    import jax
    import jax.numpy as jnp

    def _L0_gnn_ref(node_features, edge_index, edge_features, mW1, mb1, mW2, mb2, uW1, ub1, uW2, ub2):
        import jax, jax.numpy as jnp
        import numpy as np
        N, NODE_DIM, EDGE_DIM, HIDDEN, E = (10000, 256, 16, 512, 10000)
        i_idx = edge_index[0]
        j_idx = edge_index[1]
        node_i = node_features[i_idx]
        node_j = node_features[j_idx]
        msg_input = jnp.concatenate([node_i, node_j, edge_features], axis=-1)
        h = jax.nn.relu(msg_input @ mW1 + mb1)
        messages = h @ mW2 + mb2
        aggregated = jax.ops.segment_sum(messages, i_idx, num_segments=node_features.shape[0])
        update_input = jnp.concatenate([node_features, aggregated], axis=-1)
        u = jax.nn.relu(update_input @ uW1 + ub1)
        updated = u @ uW2 + ub2
        return node_features + updated

    def _L0_ffn_ref(x, sW1, sb1, sW2, sb2, sW3, sb3, eW1, eb1, eW2, eb2, eW3, eb3, gW, gb):
        import jax, jax.numpy as jnp
        import numpy as np
        B, A = (128, 8)
        IN, OUT = (256, 256)
        SH1, SH2 = (256, 128)
        EH1, EH2 = (128, 64)
        E, TOPK = (4, 2)

        def _shared_mlp(x, W1, b1, W2, b2, W3, b3):
            h = jax.nn.relu(x @ W1 + b1)
            h = jax.nn.relu(h @ W2 + b2)
            return h @ W3 + b3

        def _experts_mlp(x, eW1, eb1, eW2, eb2, eW3, eb3):
            h = jax.nn.relu(jnp.einsum('baf,efh->ebah', x, eW1) + eb1[:, None, None, :])
            h = jax.nn.relu(jnp.einsum('ebah,ehg->ebag', h, eW2) + eb2[:, None, None, :])
            o = jnp.einsum('ebag,ego->ebao', h, eW3) + eb3[:, None, None, :]
            return jnp.moveaxis(o, 0, -1)
        all_out = _experts_mlp(x, eW1, eb1, eW2, eb2, eW3, eb3)
        shared = _shared_mlp(x, sW1, sb1, sW2, sb2, sW3, sb3)
        gates = jax.nn.softmax(x @ gW + gb, axis=-1)
        topv, topi = jax.lax.top_k(gates, TOPK)
        topw = jax.nn.softmax(topv, axis=-1)
        sel = jnp.take_along_axis(all_out, topi[:, :, None, :], axis=-1)
        gated = jnp.sum(sel * topw[:, :, None, :], axis=-1)
        return shared + gated

    def _L1_gnn_ref(x, edge_index, W_l1, b1, W_r1, W_l2, b2, W_r2):
        import jax, jax.numpy as jnp
        import numpy as np
        N_NODES = 3125
        N_EDGES = 100000
        D_IN = 256
        D_HID = 256
        D_OUT = 256

        def _sage_conv(x, src, tgt, W_l, b_l, W_r):
            n = x.shape[0]
            msgs = x[src]
            agg = jax.ops.segment_sum(msgs, tgt, num_segments=n)
            deg = jax.ops.segment_sum(jnp.ones((src.shape[0],), x.dtype), tgt, num_segments=n)
            agg = agg / jnp.maximum(deg, 1.0)[:, None]
            return agg @ W_l + b_l + x @ W_r
        src, tgt = (edge_index[0], edge_index[1])
        h = jax.nn.relu(_sage_conv(x, src, tgt, W_l1, b1, W_r1))
        logits = _sage_conv(h, src, tgt, W_l2, b2, W_r2)
        return logits

    def _L1_ffn_ref(x, attention_mask, wr, br, w1, b1, w2, b2):
        import jax, jax.numpy as jnp
        import numpy as np
        B, S, D = (8, 128, 256)
        H = 4 * D
        CAPACITY = 0.5
        b, s, d = x.shape
        weights = (jnp.einsum('bsd,do->bso', x, wr) + br)[..., 0]
        k = max(1, int(CAPACITY * s))
        kk = k - 1 if k > 1 else 1
        _, idx = jax.lax.top_k(weights, k)
        sel_idx = idx[:, :kk]
        sel = jnp.take_along_axis(x, sel_idx[:, :, None], axis=1)
        h = jax.nn.gelu(jnp.einsum('bkd,dh->bkh', sel, w1) + b1)
        y = jnp.einsum('bkh,hd->bkd', h, w2) + b2
        w_sel = jnp.take_along_axis(weights, sel_idx, axis=1)
        y = y * w_sel[..., None]
        batch_idx = jnp.arange(b)[:, None]
        processed = jnp.zeros_like(x).at[batch_idx, sel_idx].set(y)
        return processed + x
    edge_index = jnp.stack([src, dst])
    x = x + _L0_gnn_ref(_layernorm(x, axis=-1), edge_index, edge_attr_16, L0_gnn_mW1, L0_gnn_mb1, L0_gnn_mW2, L0_gnn_mb2, L0_gnn_uW1, L0_gnn_ub1, L0_gnn_uW2, L0_gnn_ub2)
    x = x + _L0_ffn_ref(_layernorm(x, axis=-1)[None], L0_ffn_sW1, L0_ffn_sb1, L0_ffn_sW2, L0_ffn_sb2, L0_ffn_sW3, L0_ffn_sb3, L0_ffn_eW1, L0_ffn_eb1, L0_ffn_eW2, L0_ffn_eb2, L0_ffn_eW3, L0_ffn_eb3, L0_ffn_gW, L0_ffn_gb)[0]
    x = x + _L1_gnn_ref(_layernorm(x, axis=-1), edge_index, L1_gnn_W_l1, L1_gnn_b1, L1_gnn_W_r1, L1_gnn_W_l2, L1_gnn_b2, L1_gnn_W_r2)
    x = x + _L1_ffn_ref(_layernorm(x, axis=-1)[None], L1_ffn_attention_mask, L1_ffn_wr, L1_ffn_br, L1_ffn_w1, L1_ffn_b1, L1_ffn_w2, L1_ffn_b2)[0]
    return x

_drawn_inputs = setup_inputs


def setup_inputs(seed=0):
    import zlib

    import numpy as np

    out = dict(_drawn_inputs(seed))
    spreads = {'L0_ffn_sb1': (0.0, 0.8),
     'L0_ffn_sb2': (0.0, 0.394),
     'L0_ffn_sb3': (0.0, 0.1),
     'L0_ffn_eb1': (0.0, 0.8),
     'L0_ffn_eb2': (0.0, 0.8),
     'L0_ffn_eb3': (0.0, 0.1),
     'L0_ffn_gb': (0.0, 0.701),
     'L1_gnn_b1': (0.0, 0.339),
     'L1_gnn_b2': (0.0, 0.1),
     'L1_ffn_b1': (0.0, 0.8),
     'L1_ffn_b2': (0.0, 0.8)}
    factors = {'edge_attr_16': 4.216,
     'L0_gnn_mb1': 5.108,
     'L0_gnn_ub1': 8.0,
     'L0_gnn_ub2': 4.384,
     'L0_ffn_eW1': 2.753,
     'L1_ffn_wr': 5.375,
     'L1_ffn_w1': 8.0,
     'L1_ffn_w2': 8.0}
    for name, (base, spread) in spreads.items():
        noise = np.random.default_rng([zlib.crc32(name.encode()), seed]).standard_normal(out[name].shape)
        drawn = base * np.exp(spread * noise) if base else spread * noise
        out[name] = jnp.asarray(drawn.astype(out[name].dtype))
    for name, factor in factors.items():
        out[name] = (out[name] * factor).astype(out[name].dtype)
    return out
```

```python
from contextlib import ExitStack

import concourse.bass as bass
from concourse import mybir

ALU = mybir.AluOpType
ACT = mybir.ActivationFunctionType
AX = mybir.AxisListType
F32 = mybir.dt.float32
F32R = mybir.dt.float32r
F16 = mybir.dt.float16
BF16 = mybir.dt.bfloat16
I32 = mybir.dt.int32
U32 = mybir.dt.uint32
I16 = mybir.dt.int16

P = 128
N_NODES = 3125
D = 256
KD = D // P
HID = 512
KH = HID // P
N_EDGES = 53125
EDGE_DIM = 16
NT = -(-N_NODES // P)
NPAD = NT * P
EC = -(-N_EDGES // P)
EPAD = EC * P
GROUP = 2 * P
NG = (N_EDGES + NT * (GROUP - 1)) // GROUP
NSLOT = NG * GROUP
NCOL = 2 * NG
REC = 2 + 2 * EDGE_DIM
CH = 5
NCH = NT // CH
EPS = 1e-5
HB = 4
TAB = EC // NT // HB * HB
BATCH = 8


class Names:
    pass


class Mem:

    def __init__(self, nc, ctx, prefix=""):
        self.nc, self.ctx, self.prefix, self.sems = nc, ctx, prefix, []

    def sb(self, name, shape, dt=F32):
        return self.ctx.enter_context(self.nc.sbuf_tensor(self.prefix + name, shape, dt))

    def ps(self, name, shape, dt=F32):
        return self.ctx.enter_context(self.nc.psum_tensor(self.prefix + name, shape, dt))

    def sem(self, name):
        self.sems.append(self.nc.alloc_semaphore(self.prefix + name))
        return self.sems[-1]

    def clear_sems(self):
        for sem in self.sems:
            self.nc.sync.sem_clear(sem)
            self.nc.release_semaphore(sem)


class Chain:

    def __init__(self, eng, sem):
        self.eng, self.sem, self.n = eng, sem, 0

    def link(self, ins):
        ins.then_inc(self.sem, 1)
        self.n += 1
        self.eng.wait_ge(self.sem, self.n)


def chunks(eng):
    yield 0
    with eng.Fori(1, NCH) as c:
        yield c


def wait_past(eng, sem, count):
    if not (isinstance(count, int) and count == 0):
        eng.wait_ge(sem, count)


def layer_norm_chunk(dve, done, at, x, xn, stats, small, std_ready, std_done, nth):
    for t in range(CH):
        dve.bn_stats(stats[:, t, :], x[:, t, :]).then_inc(done, 1)
    dve.wait_ge(done, at + CH)
    mean, var, std, rstd, diff, diff2 = (small[:, n, :] for n in range(6))
    dve.tensor_tensor(mean, stats[:, :, 1], stats[:, :, 4], ALU.add).then_inc(done, 1)
    dve.tensor_tensor(diff, stats[:, :, 1], stats[:, :, 4], ALU.subtract).then_inc(done, 1)
    dve.tensor_tensor(var, stats[:, :, 2], stats[:, :, 5], ALU.add).then_inc(done, 1)
    dve.wait_ge(done, at + CH + 3)
    dve.tensor_scalar(mean, mean, 0.5, None, ALU.mult).then_inc(done, 1)
    dve.tensor_tensor(diff2, diff, diff, ALU.mult).then_inc(done, 1)
    dve.tensor_scalar(var, var, 1.0 / D, EPS, ALU.mult, ALU.add).then_inc(done, 1)
    dve.wait_ge(done, at + CH + 6)
    dve.scalar_tensor_tensor(out=var, in0=diff2, scalar=0.25, in1=var, op0=ALU.mult,
                             op1=ALU.add).then_inc(std_ready, 1)
    dve.wait_ge(std_done, nth + 1)
    dve.reciprocal(rstd, std).then_inc(done, 1)
    dve.wait_ge(done, at + CH + 7)
    dve.tensor_tensor(diff, rstd, rstd, ALU.mult).then_inc(done, 1)
    dve.wait_ge(done, at + CH + 8)
    dve.tensor_tensor(diff, diff, var, ALU.mult).then_inc(done, 1)
    dve.wait_ge(done, at + CH + 9)
    dve.tensor_scalar(diff, diff, -0.5, 1.5, ALU.mult, ALU.add).then_inc(done, 1)
    dve.wait_ge(done, at + CH + 10)
    dve.tensor_tensor(rstd, rstd, diff, ALU.mult).then_inc(done, 1)
    dve.wait_ge(done, at + CH + 11)
    for t in range(CH):
        dve.tensor_scalar(xn[:, t, :], x[:, t, :], mean[:, t:t + 1], rstd[:, t:t + 1], ALU.subtract,
                          ALU.mult).then_inc(done, 1)


LN_STEPS = 2 * CH + 11


def square_root(act, small, std_ready, std_done, nth):
    act.wait_ge(std_ready, nth + 1)
    act.activation(small[:, 2, :], small[:, 1, :], ACT.Sqrt).then_inc(std_done, 1)


def stage_constants(nc, C):
    with ExitStack() as ctx:
        m = Mem(nc, ctx)
        s_iota, s_done = m.sem("s_iota"), m.sem("s_const")
        with nc.Block() as block:
            @block.gpsimd
            def _(pool):
                pool.iota(C.iota_i[:, :], [[1, P]], base=0, channel_multiplier=0).then_inc(s_iota, 1)
                pool.iota(C.iota_h[:, :], [[1, NCOL]], base=0, channel_multiplier=0,
                          allow_small_or_imprecise_dtypes=True).then_inc(s_iota, 1)
                pool.iota(C.part_i[:, :], [[0, 1]], base=0, channel_multiplier=1).then_inc(s_iota, 1)

            @block.vector
            def _(dve):
                step = Chain(dve, s_done)
                dve.wait_ge(s_iota, 3)
                step.link(dve.tensor_copy(C.iota_f[:, :], C.iota_i[:, :]))
                step.link(dve.tensor_copy(C.iota_b[:, :], C.iota_i[:, :]))
                step.link(dve.tensor_copy(C.part_f[:, :], C.part_i[:, :]))
                step.link(dve.tensor_scalar(C.ident[:, :], C.iota_f[:, :], C.part_f[:, 0:1], None, ALU.is_equal))
                step.link(dve.tensor_scalar(C.before[:, :], C.iota_f[:, :], C.part_f[:, 0:1], None, ALU.is_gt))
                step.link(dve.memset(C.ones[:, :], 1.0))
                step.link(dve.memset(C.zeros[:, :], 0.0))
                step.link(dve.memset(C.zeros_w[:, :], 0.0))


def stage_prepare(nc, C, A, S):
    with ExitStack() as ctx:
        m = Mem(nc, ctx)
        key = [m.sb(f"key{k}", [P, EC], I32) for k in range(2)]
        hi_i = m.sb("hi_i", [P, EC], I32)
        hi16 = [m.sb(f"hi16_{k}", [P, EC], I16) for k in range(2)]
        lo_i = m.sb("lo_i", [P, EC], I32)
        pos = m.sb("pos", [P, EC])
        pad_pos = m.sb("pad_pos", [P, EC])
        iota_c = m.sb("iota_c", [P, EC])
        slot_src = m.sb("slot_src", [P, EC], U32)
        slot_dst = m.sb("slot_dst", [P, EC], I32)
        lane, col = m.sb("lane", [P, EC]), m.sb("col", [P, EC])
        val = m.sb("val", [P, 2, EC])
        ends = m.sb("ends", [P, NT + 1])
        cnt = m.sb("cnt", [P, NT])
        grp_i = m.sb("grp_i", [P, NT], I32)
        grp = m.sb("grp", [P, NT])
        start = m.sb("start", [P, NT])
        off = m.sb("off", [P, NT])
        hit = m.sb("hit", [P, NT])
        gk_i = m.sb("gk_i", [P, 2], I32)
        gk = m.sb("gk", [P, 2])
        bkt_f = m.sb("bkt_f", [P, 2])
        bkt_i = m.sb("bkt_i", [P, 2], I32)
        recs = m.sb("recs", [P, EC, REC])
        fill = m.sb("fill", [P, 29, REC])
        stage = [m.sb(f"stage{b}", [P, BATCH, REC]) for b in range(2)]
        stage_pos = [m.sb(f"stage_pos{b}", [P, BATCH], U32) for b in range(2)]
        lane_hot = [m.sb(f"lane_hot{b}", [P, 2, P], F16) for b in range(HB)]
        col_hot = [m.sb(f"col_hot{b}", [P, NCOL], F16) for b in range(HB)]
        member = m.sb("member", [P, NT, EC], BF16)
        rank = m.sb("rank", [P, NT, EC])
        with ExitStack() as early:
            attr = Mem(nc, early).sb("attr", [P, EC * EDGE_DIM])
        xc = m.sb("xc", [P, CH, D])
        xnc = m.sb("xnc", [P, CH, D])
        xtc = m.sb("xtc", [P, KD, CH * P])
        w_pq = m.sb("w_pq", [P, 2, KD, HID])
        p_out = [m.sb(f"p_out{b}", [P, 2, HID]) for b in range(2)]
        q_out = [m.sb(f"q_out{b}", [P, HID]) for b in range(2)]
        stats = m.sb("stats", [P, CH, 6])
        small = m.sb("small", [P, 6, CH])

        acc = [m.ps(f"acc{k}", [P, HID]) for k in range(2)]
        tr = [m.ps(f"tr{k}", [P, HID]) for k in range(2)]
        pq = [[m.ps(f"pq{h}{b}", [P, HID]) for b in range(2)] for h in range(2)]

        s_key, s_attr, s_fill, s_filled = m.sem("s_key"), m.sem("s_attr"), m.sem("s_fill"), m.sem("s_filled")
        s_padkey = m.sem("s_padkey")
        s_iota = m.sem("s_iota_c")
        s_dve = m.sem("s_dve")
        s_cnt, s_sum = m.sem("s_cnt"), m.sem("s_sum")
        s_high, s_low = m.sem("s_high"), m.sem("s_low")
        s_order = m.sem("s_order")
        s_staged = m.sem("s_staged")
        s_scat = [m.sem(f"s_scat{b}") for b in range(2)]
        s_hot, s_hot_used, s_table = m.sem("s_hot"), m.sem("s_hot_used"), m.sem("s_table")
        s_bkt, s_bkt_out, s_bkt_in = m.sem("s_bkt"), m.sem("s_bkt_out"), m.sem("s_bkt_in")
        s_w, s_x, s_std_ready, s_std = m.sem("s_w"), m.sem("s_x"), m.sem("s_std_ready"), m.sem("s_std")
        s_ln = m.sem("s_ln")
        s_tr, s_xt = m.sem("s_tr"), m.sem("s_xt")
        s_pq, s_phi, s_plo, s_q = m.sem("s_pq"), m.sem("s_phi"), m.sem("s_plo"), m.sem("s_q")
        s_pst, s_qst = [m.sem(f"s_pst{b}") for b in range(2)], [m.sem(f"s_qst{b}") for b in range(2)]
        s_xnst, s_xtst = m.sem("s_xnst"), m.sem("s_xtst")
        s_stage = [m.sem(f"s_stage{b}") for b in range(2)]

        with nc.Block() as block:
            @block.sync
            def _(sp):
                for k, src in enumerate((A.src, A.dst)):
                    sp.dma_start(key[k][:, :], src.rearrange("(p c) -> p c", c=EC)).then_inc(s_key, 16)
                sp.dma_start(attr[:, :], A.edge_attr.rearrange("(p c) w -> p (c w)", c=EC)).then_inc(s_attr, 16)
                sp.wait_ge(s_fill, 3)
                recs_v = S.recs[0:NSLOT, :].rearrange("(n p r) w -> n p (r w)", p=P, r=29)
                for n in range(NSLOT // (29 * P)):
                    sp.dma_start(recs_v[n], fill[:, :, :].rearrange("p r w -> p (r w)")).then_inc(s_filled, 16)
                sp.wait_ge(s_low, 1)
                sp.wait_ge(s_order, 1)
                for h in range(2):
                    sp.dma_start(w_pq[:, h, :, :],
                                 A.mW1[h * D:(h + 1) * D, :].rearrange("(k p) n -> p k n", p=P)).then_inc(s_w, 16)
                sp.wait_ge(s_order, 2)
                def fill_stages(i):
                    for b in range(2):
                        at = (2 * i + b) * BATCH
                        wait_past(sp, s_scat[b], 16 * BATCH * i)
                        sp.dma_start(stage[b][:, :, :].rearrange("p c w -> p (c w)"),
                                     recs[:, bass.ds(at, BATCH), :].rearrange("p c w -> p (c w)")).then_inc(s_stage[b], 16)
                        sp.dma_start(stage_pos[b][:, :], slot_src[:, bass.ds(at, BATCH)]).then_inc(s_stage[b], 16)

                fill_stages(0)
                with sp.Fori(1, EC // (2 * BATCH)) as i:
                    fill_stages(i)

            @block.gpsimd
            def _(pool):
                pool.memset(fill[:, :, 0:1], -1.0).then_inc(s_fill, 1)
                pool.memset(fill[:, :, 1:2].bitcast(U32), 0).then_inc(s_fill, 1)
                pool.memset(fill[:, :, 2:REC], 0.0).then_inc(s_fill, 1)
                pool.iota(lo_i[:, :], [[1, EC]], base=NSLOT, channel_multiplier=0).then_inc(s_iota, 1)
                pool.iota(gk_i[:, :], [[1, 2]], base=0, channel_multiplier=2).then_inc(s_iota, 1)
                pool.wait_ge(s_attr, 16)
                pool.wait_ge(s_high, 1)
                pool.tensor_tensor(recs[:, :, 2 + EDGE_DIM:REC], attr[:, :].rearrange("p (c w) -> p c w", w=EDGE_DIM),
                                   recs[:, :, 2:2 + EDGE_DIM], ALU.subtract).then_inc(s_low, 1)
                pool.wait_ge(s_filled, 16 * (NSLOT // (29 * P)))
                with pool.Fori(0, EC // (2 * BATCH)) as i:
                    for b in range(2):
                        pool.wait_ge(s_stage[b], 32 * i + 32)
                        pool.nop(nofuse=True)
                        for j in range(BATCH):
                            pool.indirect_dma_start(
                                S.recs[:, :], bass.IndirectOffsetOnAxis(ap=stage_pos[b][:, j:j + 1], axis=0),
                                stage[b][:, j, :], None).then_inc(s_scat[b], 16)
                for b in range(2):
                    pool.wait_ge(s_scat[b], 16 * BATCH * (EC // (2 * BATCH)))

            @block.scalar
            def _(act):
                act.wait_ge(s_attr, 16)
                act.activation(recs[:, :, 2:2 + EDGE_DIM].bitcast(F32R),
                               attr[:, :].rearrange("p (c w) -> p c w", w=EDGE_DIM), ACT.Copy).then_inc(s_high, 1)
                act.wait_ge(s_bkt, 1)
                act.dma_start(S.bucket.rearrange("(p j) -> p j", j=2), bkt_i[0:NG // 2, :]).then_inc(s_bkt_out, 16)
                act.wait_ge(s_bkt_out, 16)
                act.dma_start(C.bucket[0:1, 0, :], S.bucket.rearrange("(a k) -> a k", a=1)).then_inc(s_bkt_in, 16)
                act.wait_ge(s_bkt, 2)
                act.dma_start(S.bucket2.rearrange("(p j) -> p j", j=2), bkt_i[0:NG // 2, :]).then_inc(s_bkt_out, 16)
                act.wait_ge(s_bkt_out, 32)
                act.dma_start(C.bucket[0:1, 1, :], S.bucket2.rearrange("(a k) -> a k", a=1)).then_inc(s_bkt_in, 16)
                x_v = A.x.rearrange("(t p) d -> p t d", p=P)
                act.wait_ge(s_low, 1)
                for c in chunks(act):
                    wait_past(act, s_ln, LN_STEPS * c)
                    act.dma_start(xc[:, :, :], x_v[:, bass.ds(c * CH, CH), :]).then_inc(s_x, 16)
                    square_root(act, small, s_std_ready, s_std, c)
                    act.wait_ge(s_ln, LN_STEPS * c + LN_STEPS)
                    act.dma_start(S.xn.rearrange("(t p) d -> p t d", p=P)[:, bass.ds(c * CH, CH), :],
                                  xnc[:, :, :]).then_inc(s_xnst, 16)
                    wait_past(act, s_xtst, 16 * c)
                    for k in range(KD):
                        for h in range(2):
                            w = 4 * P if h == 0 else P
                            act.wait_ge(s_tr, 4 * c + 2 * k + h + 1)
                            act.activation(xtc[:, k, 4 * P * h:4 * P * h + w], tr[h][:, 0:w],
                                           ACT.Copy).then_inc(s_xt, 1)
                    act.wait_ge(s_xt, 4 * c + 4)
                    act.dma_start(S.xnT.rearrange("(k p) n -> p k n", p=P)[:, :, bass.ds(c * CH * P, CH * P)],
                                  xtc[:, :, :]).then_inc(s_xtst, 16)
                    for t in range(CH):
                        b, uses = t % 2, (CH + 1 - t % 2) // 2
                        act.wait_ge(s_pq, 2 * CH * c + 2 * t + 1)
                        wait_past(act, s_pst[b], 16 * (uses * c + t // 2))
                        act.activation(p_out[b][:, 0, :].bitcast(F32R), pq[0][b][:, :], ACT.Copy).then_inc(s_phi, 1)
                        act.wait_ge(s_pq, 2 * CH * c + 2 * t + 2)
                        wait_past(act, s_qst[b], 16 * (uses * c + t // 2))
                        act.activation(q_out[b][:, :], pq[1][b][:, :], ACT.Copy).then_inc(s_q, 1)
                        act.wait_ge(s_q, CH * c + t + 1)
                        act.dma_start(S.q[bass.ds((c * CH + t) * P, P), :], q_out[b][:, :]).then_inc(s_qst[b], 16)
                        act.wait_ge(s_plo, CH * c + t + 1)
                        act.dma_start(S.p[bass.ds((c * CH + t) * P, P), :],
                                      p_out[b][:, :, :].rearrange("p h n -> p (h n)")).then_inc(s_pst[b], 16)
                for b in range(2):
                    act.wait_ge(s_pst[b], 16 * NCH * ((CH + 1 - b) // 2))
                    act.wait_ge(s_qst[b], 16 * NCH * ((CH + 1 - b) // 2))
                act.wait_ge(s_xnst, 16 * NCH)
                act.wait_ge(s_xtst, 16 * NCH)
                act.wait_ge(s_bkt_in, 32)

            @block.vector
            def _(dve):
                step = Chain(dve, s_dve)
                dve.wait_ge(s_iota, 2)
                step.link(dve.tensor_copy(iota_c[:, :], lo_i[:, :]))
                step.link(dve.tensor_copy(gk[:, :], gk_i[:, :]))
                for k in range(2):
                    dve.wait_ge(s_key, 32)
                    dve.tensor_scalar(hi_i[:, :], key[k][:, :], 7, None, ALU.logical_shift_right).then_inc(s_dve, 1)
                    dve.tensor_scalar(lo_i[:, :], key[k][:, :], P - 1, None, ALU.bitwise_and).then_inc(s_dve, 1)
                    step.n += 2
                    dve.wait_ge(s_dve, step.n)
                    dve.tensor_copy(hi16[k][:, :], hi_i[:, :]).then_inc(s_dve, 1)
                    if k == 0:
                        dve.tensor_copy(recs[:, :, 0], lo_i[:, :]).then_inc(s_dve, 1)
                        dve.tensor_scalar(val[:, 0, :], key[0][:, :], float(-NPAD // 2), None, ALU.add).then_inc(s_dve, 1)
                        dve.tensor_copy(recs[:, :, 1].bitcast(I32), key[1][:, :]).then_inc(s_dve, 1)
                        step.n += 4
                    else:
                        dve.tensor_scalar(val[:, 1, :], lo_i[:, :], 1.0, None, ALU.add).then_inc(s_dve, 1)
                        step.n += 2
                    dve.wait_ge(s_dve, step.n)
                    for b in range(NT):
                        dve.tensor_scalar(member[:, b, :], hi16[k][:, :], float(b), None, ALU.is_equal).then_inc(s_dve, 1)
                    step.n += NT
                    dve.wait_ge(s_dve, step.n)
                    flat = member[:, :, :].rearrange("p b c -> p (b c)")
                    step.link(dve.tensor_tensor_scan(rank[:, :, :].rearrange("p b c -> p (b c)"), flat, flat, 0.0,
                                                     ALU.add, ALU.bypass))
                    step.link(dve.memset(ends[:, 0:1], 0.0))
                    step.link(dve.tensor_copy(ends[:, 1:NT + 1], rank[:, :, EC - 1]))
                    step.link(dve.tensor_tensor(cnt[:, :], ends[:, 1:NT + 1], ends[:, 0:NT], ALU.subtract))
                    dve.sem_inc(s_cnt, 1)
                    dve.wait_ge(s_sum, k + 1)
                    step.link(dve.tensor_scalar(grp_i[:, :], acc[1][:, 0:NT], float(GROUP - 1), None, ALU.add))
                    step.link(dve.tensor_scalar(grp_i[:, :], grp_i[:, :], 8, None, ALU.logical_shift_right))
                    step.link(dve.tensor_copy(grp[:, :], grp_i[:, :]))
                    step.link(dve.tensor_tensor_scan(start[:, :], grp[:, :], grp[:, :], 0.0, ALU.add, ALU.bypass))
                    step.link(dve.tensor_tensor(start[:, :], start[:, :], grp[:, :], ALU.subtract))
                    step.link(dve.scalar_tensor_tensor(out=off[:, :], in0=start[:, :], scalar=float(GROUP),
                                                       in1=acc[0][:, 0:NT], op0=ALU.mult, op1=ALU.add))
                    step.link(dve.tensor_tensor(off[:, :], off[:, :], ends[:, 0:NT], ALU.subtract))
                    step.link(dve.tensor_scalar(off[:, :], off[:, :], -1.0, None, ALU.add))
                    for b in range(NT):
                        dve.scalar_tensor_tensor(out=rank[:, b, :], in0=rank[:, b, :], scalar=off[:, b:b + 1],
                                                 in1=member[:, b, :], op0=ALU.add, op1=ALU.mult).then_inc(s_dve, 1)
                    step.n += NT
                    dve.wait_ge(s_dve, step.n)
                    step.link(dve.tensor_reduce(pos[:, :], rank[:, :, :].rearrange("p b c -> p c b"), AX.X, ALU.add))
                    step.link(dve.scalar_tensor_tensor(out=pad_pos[:, :], in0=hi16[k][:, :], scalar=float(NT),
                                                       in1=iota_c[:, :], op0=ALU.is_equal, op1=ALU.mult))
                    slot = slot_src if k == 0 else slot_dst
                    step.link(dve.tensor_tensor(slot[:, :], pos[:, :], pad_pos[:, :], ALU.add))
                    if k == 0:
                        dve.sem_inc(s_order, 2)
                    if k == 1:
                        dve.wait_ge(s_bkt_in, 16)
                    for j in range(2):
                        step.link(dve.tensor_scalar(hit[:, :], start[:, :], gk[:, j:j + 1], None, ALU.is_le, ALU.add,
                                                    accum_out=bkt_f[:, j:j + 1]))
                    step.link(dve.tensor_scalar(bkt_i[:, :], bkt_f[:, :], -1.0, None, ALU.add))
                    dve.sem_inc(s_bkt, 1)
                step.link(dve.tensor_scalar(lo_i[:, :], slot_dst[:, :], 1, P - 1, ALU.logical_shift_right, ALU.bitwise_and))
                step.link(dve.tensor_copy(lane[:, :], lo_i[:, :]))
                step.link(dve.tensor_scalar(lo_i[:, :], slot_dst[:, :], 8, 1, ALU.logical_shift_right, ALU.logical_shift_left))
                step.link(dve.tensor_scalar(hi_i[:, :], slot_dst[:, :], 1, None, ALU.bitwise_and))
                step.link(dve.tensor_copy(col[:, :], lo_i[:, :]))
                step.link(dve.tensor_copy(pos[:, :], hi_i[:, :]))
                step.link(dve.tensor_tensor(col[:, :], col[:, :], pos[:, :], ALU.add))
                def hot(c, b):
                    dve.wait_ge(s_hot_used, c - b + HB)
                    for k in range(2):
                        dve.tensor_scalar(lane_hot[b][:, k, :], C.iota_b[:, :], lane[:, bass.ds(c, 1)],
                                          val[:, k, bass.ds(c, 1)], ALU.is_equal, ALU.mult).then_inc(s_hot, 1)
                    dve.tensor_scalar(col_hot[b][:, :], C.iota_h[:, :], col[:, bass.ds(c, 1)], None,
                                      ALU.is_equal).then_inc(s_hot, 1)

                dve.wait_ge(s_low, 1)
                for c in chunks(dve):
                    dve.wait_ge(s_x, 16 * c + 16)
                    wait_past(dve, s_xnst, 16 * c)
                    wait_past(dve, s_tr, 4 * c)
                    layer_norm_chunk(dve, s_ln, LN_STEPS * c, xc, xnc, stats, small, s_std_ready, s_std, c)
                    for t in range(CH):
                        with dve.Fori(0, TAB // HB) as g:
                            for b in range(HB):
                                hot((CH * c + t) * TAB + HB * g + b, b)
                        dve.wait_ge(s_phi, CH * c + t + 1)
                        dve.tensor_tensor(p_out[t % 2][:, 1, :], pq[0][t % 2][:, :], p_out[t % 2][:, 0, :],
                                          ALU.subtract).then_inc(s_plo, 1)
                with dve.Fori(NT * TAB // HB, EC // HB) as g:
                    for b in range(HB):
                        hot(HB * g + b, b)
                dve.wait_ge(s_table, 2)
                done = step
                done.link(dve.tensor_scalar(C.gidx[:, :], acc[0][:, 0:NCOL], float(NPAD // 2), None, ALU.add))
                done.link(dve.tensor_scalar(C.dloc[:, :], acc[1][:, 0:NCOL], -1.0, None, ALU.add))

            @block.tensor
            def _(pe):
                for k in range(2):
                    pe.wait_ge(s_cnt, k + 1)
                    pe.matmul(acc[0][:, 0:NT], C.before[:, :], cnt[:, :], start=True, stop=True)
                    pe.matmul(acc[1][:, 0:NT], C.ones[:, :], cnt[:, :], start=True, stop=True).then_inc(s_sum, 1)

                def place(c, b):
                    pe.wait_ge(s_hot, 3 * c + 3)
                    for k in range(2):
                        last = pe.matmul(acc[k][:, 0:NCOL], lane_hot[b][:, k, :], col_hot[b][:, :], start=False,
                                         stop=False)
                    last.then_inc(s_hot_used, 1)

                def edge_of_table(first):
                    for k in range(2):
                        last = pe.matmul(acc[k][:, 0:NCOL], C.zeros[:, :], C.zeros_w[:, :], start=first, stop=not first)
                    last.then_inc(s_table, 1)

                pe.wait_ge(s_bkt, 2)
                edge_of_table(True)
                pe.sem_inc(s_hot_used, HB)
                pe.wait_ge(s_w, 32)
                for c in chunks(pe):
                    for k in range(KD):
                        for h in range(2):
                            if k == 0 and h == 0:
                                pe.wait_ge(s_ln, LN_STEPS * c + LN_STEPS)
                            tiles = range(4) if h == 0 else range(4, CH)
                            wait_past(pe, s_xt, 4 * c + 2 * k + h - 1 if k else 4 * c)
                            for t in tiles:
                                last = pe.transpose(tr[h][:, (t % 4) * P:(t % 4 + 1) * P],
                                                    xnc[:, t, k * P:(k + 1) * P], C.ident[:, :])
                            last.then_inc(s_tr, 1)
                    pe.wait_ge(s_xt, 4 * c + 4)
                    for t in range(CH):
                        for h, freed in enumerate((s_plo, s_q)):
                            wait_past(pe, freed, CH * c + max(t - 1, 0))
                            for k in range(KD):
                                last = pe.matmul(pq[h][t % 2][:, :], xtc[:, k, t * P:(t + 1) * P], w_pq[:, h, k, :],
                                                 start=(k == 0), stop=(k == KD - 1))
                            last.then_inc(s_pq, 1)
                        with pe.Fori(0, TAB // HB) as g:
                            for b in range(HB):
                                place((CH * c + t) * TAB + HB * g + b, b)
                with pe.Fori(NT * TAB // HB, EC // HB) as g:
                    for b in range(HB):
                        place(HB * g + b, b)
                edge_of_table(False)


def stage_edge_network(nc, C, A, S):
    with ExitStack() as ctx:
        m = Mem(nc, ctx)
        GB, TB = 4, 8
        G, T = 2 * GB, 2 * TB
        NI = NG // G
        assert NI * G == NG
        p_hl = m.sb("p_hl", [P, NT, 2, HID], F32R)
        w_c = m.sb("w_c", [P, HID])
        w_ch = m.sb("w_ch", [P, HID])
        w_cat = m.sb("w_cat", [P, HID], F32R)
        rb = [m.sb(f"rb{b}", [P, GB, 2 * REC]) for b in range(2)]
        wide = [m.sb(f"wide{b}", [P, 2, P]) for b in range(4)]
        hot = [m.sb(f"hot{b}", [P, 2, P]) for b in range(4)]
        trs = [m.sb(f"trs{b}", [P, 4, P], F32R) for b in range(2)]
        qg = [m.sb(f"qg{b}", [P, HID]) for b in range(TB)]
        hb = [m.sb(f"hb{b}", [P, HID]) for b in range(4)]
        p_tr = [m.ps(f"p_tr{b}", [P, 4, P]) for b in range(2)]
        p_h = [m.ps(f"p_h{b}", [P, HID]) for b in range(2)]
        p_sum = [m.ps(f"p_sum{b}", [P, KH, P]) for b in range(2)]
        p_deg = [m.ps(f"p_deg{b}", [P, HID]) for b in range(2)]

        s_p, s_w, s_rec = m.sem("e_p"), m.sem("e_w"), [m.sem(f"e_rec{b}") for b in range(2)]
        s_gath = [m.sem(f"e_gath{b}") for b in range(TB)]
        s_init, s_prep = m.sem("e_init"), m.sem("e_prep")
        s_wide, s_hot, s_tr, s_trs = m.sem("e_wide"), m.sem("e_hot"), m.sem("e_tr"), m.sem("e_trs")
        s_h, s_add, s_relu, s_sum, s_acc = (m.sem(n) for n in ("e_h", "e_add", "e_relu", "e_sum", "e_acc"))
        recs_v = S.recs[0:NSLOT, :].rearrange("(g p j) w -> p g (j w)", p=P, j=2)

        def ahead(i, q, n):
            return (i, q + n) if q + n < G else (i + 1, q + n - G)

        def edges(i, step):
            step(0, True, False)
            with i.Fori(1, NI - 1) as it:
                step(it, False, False)
            step(NI - 1, False, True)

        with nc.Block() as block:
            @block.sync
            def _(sp):
                c0 = 2 * D
                sp.wait_ge(s_init, 3)
                for r in range(4):
                    sp.dma_start(w_c[16 * r:16 * r + 16, :], A.mW1[c0:c0 + EDGE_DIM, :]).then_inc(s_w, 16)
                for r in range(2):
                    sp.dma_start(w_c[64 + r:65 + r, :], A.mb1.rearrange("(a n) -> a n", a=1)).then_inc(s_w, 16)
                for n in range(2):
                    sp.dma_start(rb[n][:, :, :], recs_v[:, GB * n:GB * n + GB, :]).then_inc(s_rec[n], 16)
                for t in range(NT):
                    sp.dma_start(p_hl[:, t, :, :].rearrange("p h n -> p (h n)").bitcast(F32),
                                 S.p[t * P:(t + 1) * P, :]).then_inc(s_p, 16)
                with sp.Fori(1, NI) as i:
                    for b in range(2):
                        sp.wait_ge(s_add, T * i + TB * b - TB)
                        sp.dma_start(rb[b][:, :, :], recs_v[:, bass.ds(G * i + GB * b, GB), :]).then_inc(s_rec[b], 16)

            @block.gpsimd
            def _(pool):
                pool.memset(w_c[:, :], 0.0).then_inc(s_init, 1)
                pool.memset(C.aggT[:, :, :, :], 0.0).then_inc(s_init, 1)
                pool.memset(C.deg_src[:, :], 0.0).then_inc(s_init, 1)
                for b in range(4):
                    pool.memset(wide[b][:, :, 64:66], 1.0).then_inc(s_init, 1)
                    pool.memset(wide[b][:, :, 66:P], 0.0).then_inc(s_init, 1)

                def gathers(i, first, last):
                    for b in range(2):
                        pool.wait_ge(s_rec[b], 16 * i + 16)
                        pool.nop(nofuse=True)
                        for r in range(TB):
                            if not (first and b == 0):
                                pool.wait_ge(s_add, T * i + TB * b - TB + r + 1)
                                pool.nop(nofuse=True)
                            at = (r % 2) * REC + 1
                            pool.indirect_dma_start(
                                qg[r][:, :], None, S.q[:, :],
                                bass.IndirectOffsetOnAxis(ap=rb[b][:, r // 2, at:at + 1].bitcast(U32), axis=0)
                            ).then_inc(s_gath[r], 16)

                edges(pool, gathers)

            @block.scalar
            def _(act):
                act.wait_ge(s_w, 96)
                act.activation(w_cat[:, :], w_c[:, :], ACT.Copy).then_inc(s_prep, 1)
                act.wait_ge(s_prep, 1)
                act.activation(w_ch[:, :], w_cat[:, :].bitcast(F32), ACT.Copy).then_inc(s_prep, 1)
                act.wait_ge(s_init, 11)

                def widen(i, q):
                    b = q // GB
                    act.wait_ge(s_rec[b], 16 * i + 16)
                    src = rb[b][:, q % GB, :].rearrange("p (j w) -> p j w", w=REC)[:, :, 2:REC]
                    for h in range(2):
                        act.activation(wide[q % 4][:, :, 32 * h:32 * h + 32], src, ACT.Copy).then_inc(s_wide, 1)

                def take(i, q):
                    act.wait_ge(s_tr, G * i + q + 1)
                    act.activation(trs[q % 2][:, :, :], p_tr[q % 2][:, :, :], ACT.Copy).then_inc(s_trs, 1)

                def body(i, first, last):
                    if first:
                        widen(i, 0)
                        widen(i, 1)
                        take(i, 0)
                    for q in range(G):
                        if not (last and q >= G - 2):
                            widen(*ahead(i, q, 2))
                        if not (last and q == G - 1):
                            take(*ahead(i, q, 1))
                        for j in range(2):
                            t = 2 * q + j
                            act.wait_ge(s_add, T * i + t + 1)
                            act.activation(hb[t % 4][:, :], hb[t % 4][:, :], ACT.Relu).then_inc(s_relu, 1)

                edges(act, body)

            @block.vector
            def _(dve):
                dve.wait_ge(s_prep, 2)
                dve.tensor_tensor(w_cat[32:64, :], w_c[32:64, :], w_ch[32:64, :], ALU.subtract).then_inc(s_prep, 1)
                dve.tensor_tensor(w_cat[64:96, :], w_c[64:96, :], w_ch[64:96, :], ALU.subtract).then_inc(s_prep, 1)
                dve.wait_ge(s_prep, 4)
                dve.tensor_copy(w_cat[64:65, :], w_ch[64:65, :]).then_inc(s_prep, 1)

                def one_hot(i, q):
                    b = q // GB
                    dve.wait_ge(s_rec[b], 16 * i + 16)
                    for j in range(2):
                        dve.tensor_scalar(hot[q % 4][:, j, :], C.iota_f[:, :], rb[b][:, q % GB, j * REC:j * REC + 1],
                                          None, ALU.is_equal).then_inc(s_hot, 1)

                def accumulate(i, q, bucket):
                    dve.wait_ge(s_sum, G * i + q + 1)
                    wait_past(dve, s_acc, 2 * (G * i + q))
                    agg = C.aggT[:, bass.ds(bucket, 1), :, :].rearrange("p a k n -> p (a k n)")
                    dve.tensor_tensor(agg, p_sum[q % 2][:, :, :].rearrange("p k n -> p (k n)"), agg,
                                      ALU.add).then_inc(s_acc, 1)
                    deg = C.deg_src[:, bass.ds(bucket, 1)]
                    dve.tensor_tensor(deg, p_deg[q % 2][:, 0:1], deg, ALU.add).then_inc(s_acc, 1)

                def body(i, first, last):
                    if first:
                        dve.wait_ge(s_init, 11)
                        one_hot(i, 0)
                        one_hot(i, 1)
                        buckets = [None] + list(load_buckets(nc, dve, C.bucket[0:1, 0, 0:G]))
                    else:
                        buckets = load_buckets(nc, dve, C.bucket[0:1, 0, bass.ds(G * i - 1, G + 1)])
                    for q in range(G):
                        if not (last and q >= G - 2):
                            one_hot(*ahead(i, q, 2))
                        for j in range(2):
                            t = 2 * q + j
                            dve.wait_ge(s_h, T * i + t + 1)
                            dve.wait_ge(s_gath[t % TB], 16 * (2 * i + t // TB) + 16)
                            dve.tensor_tensor(hb[t % 4][:, :], p_h[t % 2][:, :], qg[t % TB][:, :],
                                              ALU.add).then_inc(s_add, 1)
                        if q > 0:
                            accumulate(i, q - 1, buckets[q])
                        elif not first:
                            accumulate(i - 1, G - 1, buckets[0])
                    if last:
                        accumulate(i, G - 1, buckets[G])

                edges(dve, body)

            @block.tensor
            def _(pe):
                def transposes(i, q):
                    pe.wait_ge(s_wide, 2 * (G * i + q) + 2)
                    pe.wait_ge(s_hot, 2 * (G * i + q) + 2)
                    for j in range(2):
                        pe.transpose(p_tr[q % 2][:, j, :], wide[q % 4][:, j, :], C.ident[:, :])
                    for j in range(2):
                        last = pe.transpose(p_tr[q % 2][:, 2 + j, :], hot[q % 4][:, j, :], C.ident[:, :])
                    last.then_inc(s_tr, 1)

                def hidden(i, q, bucket, first):
                    pe.wait_ge(s_trs, G * i + q + 1)
                    for j in range(2):
                        t = 2 * q + j
                        if not (first and t < 2):
                            pe.wait_ge(s_add, T * i + t - 1)
                        for h in range(2):
                            pe.matmul(p_h[j][:, :], trs[q % 2][:, 2 + j, :],
                                      p_hl[:, bass.ds(bucket, 1), h, :].rearrange("p a n -> p (a n)"),
                                      start=(h == 0), stop=False)
                        pe.matmul(p_h[j][:, :], trs[q % 2][:, j, :], w_cat[:, :], start=False,
                                  stop=True).then_inc(s_h, 1)

                def sums(i, q, first):
                    if not (first and q < 2):
                        pe.wait_ge(s_acc, 2 * (G * i + q) - 2)
                    for j in range(2):
                        t = 2 * q + j
                        pe.wait_ge(s_relu, T * i + t + 1)
                        for k in range(KH):
                            pe.matmul(p_sum[q % 2][:, k, :], hb[t % 4][:, k * P:(k + 1) * P], hot[q % 4][:, j, :],
                                      start=(j == 0 and k == 0), stop=(j == 1 and k == KH - 1), skip_group_check=True)
                        last = pe.matmul(p_deg[q % 2][:, 0:2], hot[q % 4][:, j, :], C.ones[:, 0:2],
                                         start=(j == 0), stop=(j == 1), skip_group_check=True)
                    last.then_inc(s_sum, 1)

                def body(i, first, last):
                    if first:
                        pe.wait_ge(s_p, 16 * NT)
                        pe.wait_ge(s_prep, 5)
                        transposes(i, 0)
                    buckets = load_buckets(nc, pe, C.bucket[0:1, 0, bass.ds(G * i, G)])
                    for q in range(G):
                        if not (last and q == G - 1):
                            transposes(*ahead(i, q, 1))
                        hidden(i, q, buckets[q], first)
                        if q > 0:
                            sums(i, q - 1, first)
                        elif not first:
                            sums(i - 1, G - 1, False)
                    if last:
                        sums(i, G - 1, False)

                edges(pe, body)


def load_buckets(nc, eng, ap):
    return nc.values_load_multi_w_load_instructions(ap, engines=[eng.engine], min_val=0, max_val=NT - 1)[1]


class Banks:

    def __init__(self, m, name, n, per):
        self.banks = [m.ps(f"{name}{b}", [P, HID]) for b in range(n)]
        self.full, self.empty, self.per = m.sem(f"{name}_full"), m.sem(f"{name}_empty"), per

    def to_fill(self, pe, c, g):
        n = len(self.banks)
        wait_past(pe, self.empty, self.per * c + (g - n + 1 if g >= n else 0))
        return self.banks[g % n]

    def to_take(self, eng, c, g):
        eng.wait_ge(self.full, self.per * c + g + 1)
        return self.banks[g % len(self.banks)]


HALVES = ((0, 3), (3, CH))


def transpose_chunk(pe, c, src, tr, ident, full, empty):
    for k in range(KD):
        for h, (a, b) in enumerate(HALVES):
            wait_past(pe, empty, 4 * c + (2 * k + h - 1 if k else 0))
            for t in range(a, b):
                last = pe.transpose(tr[h][:, (t - a) * P:(t - a + 1) * P], src[:, t, k * P:(k + 1) * P], ident)
            last.then_inc(full, 1)


def take_transposed(act, c, dst, tr, full, empty):
    for k in range(KD):
        for h, (a, b) in enumerate(HALVES):
            act.wait_ge(full, 4 * c + 2 * k + h + 1)
            act.activation(dst[:, k, a * P:b * P], tr[h][:, 0:(b - a) * P], ACT.Copy).then_inc(empty, 1)


def chunk(ap, c):
    return ap.rearrange("(t p) d -> p t d", p=P)[:, bass.ds(c * CH, CH), :]


def rows_on_partitions(w, p=P):
    return w.rearrange("(k p) n -> p k n", p=p)


def on_all(v):
    return v.rearrange("(a n) -> a n", a=1).to_broadcast([P, v.shape[0]])


def by_feature(v):
    return v.rearrange("(k p) -> p k", p=P)


def stage_update(nc, C, A, S):
    with ExitStack() as ctx:
        m = Mem(nc, ctx)
        w2 = m.sb("w2", [P, KH, D])
        b2 = m.sb("b2", [P, D])
        deg = m.sb("deg", [P, NPAD])
        u1 = m.sb("u1", [P, KH, HID])
        u1b = m.sb("u1b", [P, KH])
        u2 = m.sb("u2", [P, KH, D])
        u2b = m.sb("u2b", [P, 1, D])
        xT = m.sb("xT", [P, KD, CH * P])
        x, xn, r = m.sb("x", [P, CH, D]), m.sb("xn", [P, CH, D]), m.sb("r", [P, CH, D])
        msgT = m.sb("msgT", [P, KD, CH * P])
        uT = m.sb("uT", [P, KH, CH * P])
        x1, xn1 = m.sb("x1", [P, CH, D]), m.sb("xn1", [P, CH, D])
        stats, small = m.sb("stats2", [P, CH, 6]), m.sb("small2", [P, 6, CH])
        NA, NV = 2 * KD + 2 * KH, CH
        hidden, out = Banks(m, "u_h", 4, NA), Banks(m, "u_o", 4, NV)
        s_w, s_zero, s_deg, s_degrow = m.sem("u_w"), m.sem("u_zero"), m.sem("u_deg"), m.sem("u_degrow")
        s_xT, s_x, s_r, s_ln = m.sem("u_xT"), m.sem("u_x"), m.sem("u_r"), m.sem("u_ln")
        s_std_ready, s_std, s_st = m.sem("u_std_ready"), m.sem("u_std"), m.sem("u_st")

        with nc.Block() as block:
            @block.sync
            def _(sp):
                sp.dma_start(S.deg.rearrange("(t p) -> p t", p=P), C.deg_src[:, :],
                             allow_slow_non_contiguous=True).then_inc(s_deg, 16)
                sp.dma_start(w2[:, :, :], rows_on_partitions(A.mW2)).then_inc(s_w, 16)
                sp.dma_start(u1[:, :, :], rows_on_partitions(A.uW1)).then_inc(s_w, 16)
                sp.dma_start(u2[:, :, :], rows_on_partitions(A.uW2)).then_inc(s_w, 16)
                sp.dma_start(u1b[:, :], by_feature(A.ub1), allow_slow_non_contiguous=True).then_inc(s_w, 16)
                sp.dma_start(u2b[:, 0, :], on_all(A.ub2)).then_inc(s_w, 16)
                sp.wait_ge(s_zero, 2)
                sp.wait_ge(s_deg, 16)
                sp.dma_start(b2[0:1, :], A.mb2.rearrange("(a n) -> a n", a=1)).then_inc(s_w, 16)
                sp.dma_start(deg[0:1, :], S.deg.rearrange("(a n) -> a n", a=1)).then_inc(s_w, 16)
                for c in chunks(sp):
                    wait_past(sp, hidden.full, NA * c)
                    sp.dma_start(xT[:, :, :], S.xnT.rearrange("(k p) n -> p k n", p=P)[:, :, bass.ds(c * CH * P, CH * P)]
                                 ).then_inc(s_xT, 16)
                    wait_past(sp, s_r, 2 * c)
                    sp.dma_start(x[:, :, :], chunk(A.x, c)).then_inc(s_x, 16)
                    sp.dma_start(xn[:, :, :], chunk(S.xn, c)).then_inc(s_x, 16)
                    sp.wait_ge(s_ln, LN_STEPS * c + LN_STEPS)
                    sp.dma_start(chunk(S.x1, c), x1[:, :, :]).then_inc(s_st, 16)
                    sp.dma_start(chunk(S.xn1, c), xn1[:, :, :]).then_inc(s_st, 16)
                sp.wait_ge(s_st, 32 * NCH)

            @block.gpsimd
            def _(pool):
                pool.memset(b2[:, :], 0.0).then_inc(s_zero, 1)
                pool.memset(deg[:, :], 0.0).then_inc(s_zero, 1)
                pool.wait_ge(s_w, 112)
                for c in chunks(pool):
                    pool.wait_ge(s_x, 32 * c + 32)
                    wait_past(pool, out.empty, NV * c)
                    pool.tensor_tensor(r[:, :, :], x[:, :, :], xn[:, :, :], ALU.add).then_inc(s_r, 1)
                    pool.wait_ge(s_r, 2 * c + 1)
                    pool.tensor_tensor(r[:, :, :], r[:, :, :], u2b[:, :, :].to_broadcast([P, CH, D]),
                                       ALU.add).then_inc(s_r, 1)

            @block.scalar
            def _(act):
                act.wait_ge(s_w, 112)
                for c in chunks(act):
                    for k in range(KD):
                        for h, (a, b) in enumerate(HALVES):
                            g = 2 * k + h
                            src = hidden.to_take(act, c, g)
                            act.activation(msgT[:, k, a * P:b * P], src[:, 0:(b - a) * P], ACT.Copy).then_inc(hidden.empty, 1)
                    for k in range(KH):
                        for h, (a, b) in enumerate(HALVES):
                            g = 2 * KD + 2 * k + h
                            src = hidden.to_take(act, c, g)
                            act.activation(uT[:, k, a * P:b * P], src[:, 0:(b - a) * P], ACT.Relu,
                                           bias=u1b[:, k:k + 1]).then_inc(hidden.empty, 1)
                    square_root(act, small, s_std_ready, s_std, c)

            @block.vector
            def _(dve):
                for c in chunks(dve):
                    dve.wait_ge(s_r, 2 * c + 2)
                    wait_past(dve, s_st, 32 * c)
                    for t in range(CH):
                        src = out.to_take(dve, c, t)
                        dve.tensor_tensor(x1[:, t, :], src[:, 0:D], r[:, t, :], ALU.add).then_inc(out.empty, 1)
                    dve.wait_ge(out.empty, NV * c + NV)
                    layer_norm_chunk(dve, s_ln, LN_STEPS * c, x1, xn1, stats, small, s_std_ready, s_std, c)

            @block.tensor
            def _(pe):
                pe.wait_ge(s_w, 112)
                for c in chunks(pe):
                    for k in range(KD):
                        for h, (a, b) in enumerate(HALVES):
                            dst = hidden.to_fill(pe, c, 2 * k + h)[:, 0:(b - a) * P]
                            for j in range(KH):
                                pe.matmul(dst, w2[:, j, k * P:(k + 1) * P], C.aggT[:, bass.ds(c * CH + a, b - a), j, :],
                                          start=(j == 0), stop=False)
                            pe.matmul(dst, b2[:, k * P:(k + 1) * P], deg[:, bass.ds((c * CH + a) * P, (b - a) * P)],
                                      start=False, stop=True).then_inc(hidden.full, 1)
                    pe.wait_ge(s_xT, 16 * c + 16)
                    for k in range(KH):
                        for h, (a, b) in enumerate(HALVES):
                            dst = hidden.to_fill(pe, c, 2 * KD + 2 * k + h)[:, 0:(b - a) * P]
                            for j in range(KD):
                                pe.matmul(dst, u1[:, j, k * P:(k + 1) * P], xT[:, j, a * P:b * P], start=(j == 0), stop=False)
                            if k == 0:
                                pe.wait_ge(hidden.empty, NA * c + 2 * KD)
                            for j in range(KD):
                                last = pe.matmul(dst, u1[:, KD + j, k * P:(k + 1) * P], msgT[:, j, a * P:b * P],
                                                 start=False, stop=(j == KD - 1))
                            last.then_inc(hidden.full, 1)
                    pe.wait_ge(hidden.empty, NA * c + NA)
                    for t in range(CH):
                        dst = out.to_fill(pe, c, t)[:, 0:D]
                        for j in range(KH):
                            last = pe.matmul(dst, uT[:, j, t * P:(t + 1) * P], u2[:, j, :], start=(j == 0), stop=(j == KH - 1))
                        last.then_inc(out.full, 1)
        m.clear_sems()


def stage_experts(nc, C, A, S):
    NE, EH1, EH2 = A.eW1.shape[0], A.eW1.shape[2], A.eW2.shape[2]
    SH1, SH2 = A.sW1.shape[1], A.sW2.shape[1]
    KS = SH1 // P
    assert EH1 == P and SH2 == P and EH2 < P
    with ExitStack() as ctx:
        m = Mem(nc, ctx)
        w_s1, w_s2, w_s3 = m.sb("w_s1", [P, KD, SH1]), m.sb("w_s2", [P, KS, SH2]), m.sb("w_s3", [P, D])
        b_s1, b_s2, b_s3 = m.sb("b_s1", [P, KS]), m.sb("b_s2", [P, 1]), m.sb("b_s3", [P, 1, D])
        w_e1, w_e2 = m.sb("w_e1", [P, NE, KD, EH1]), m.sb("w_e2", [P, NE, EH2])
        w_e3 = m.sb("w_e3", [P, NE, D])
        b_e1, b_e2 = m.sb("b_e1", [P, NE]), m.sb("b_e2", [EH2, NE])
        w_g, b_g = m.sb("w_g", [P, KD, NE]), m.sb("b_g", [P, 1, NE])
        prio_i, prio = m.sb("prio_i", [P, 1, NE], I32), m.sb("prio", [P, 1, NE])
        x1, xn1, r, x2, xn2 = (m.sb(f"m_{n}", [P, CH, D]) for n in ("x1", "xn1", "r", "x2", "xn2"))
        xT = m.sb("m_xT", [P, KD, CH * P])
        h1, h2 = m.sb("h1", [P, KS, CH * P]), m.sb("h2", [P, CH * P])
        e1, e2 = m.sb("e1", [P, NE, CH * P]), m.sb("e2", [P, NE, CH * P])
        lg, ex, gt, key, first, second = (m.sb(f"g_{n}", [P, CH, NE]) for n in ("lg", "ex", "gt", "key", "first", "second"))
        c1, c2, c3, c4, c5, c6 = (m.sb(f"g_c{n}", [P, CH, 1]) for n in range(6))
        stats, small = m.sb("stats3", [P, CH, 6]), m.sb("small3", [P, 6, CH])
        NA, NV = 2 * (KS + 1 + 2 * NE), 1 + 3 * CH
        tr = [m.ps(f"m_tr{b}", [P, HID]) for b in range(2)]
        hidden, out = Banks(m, "m_h", 3, NA), Banks(m, "m_o", 3, NV)
        s_w, s_zero, s_x, s_trf, s_tre = (m.sem(f"m_{n}") for n in ("w", "zero", "x", "trf", "tre"))
        s_r, s_ln, s_std_ready, s_std, s_st = (m.sem(f"m_{n}") for n in ("r", "ln", "std_ready", "std", "st"))
        s_g, s_lg, s_ex, s_mix, s_prio = (m.sem(f"m_{n}") for n in ("g", "lg", "ex", "mix", "prio"))
        A_GROUPS = [("s1", k) for k in range(KS)] + [("e1", e) for e in range(NE)] + [("s2", 0)] + \
                   [("e2", e) for e in range(NE)]
        GSTEPS, MIX = 23, 5 * CH

        with nc.Block() as block:
            @block.sync
            def _(sp):
                sp.wait_ge(s_zero, 2)
                for dst, src in ((w_s1[:, :, :], rows_on_partitions(A.sW1)), (w_s2[:, :, :], rows_on_partitions(A.sW2)),
                                 (w_s3[:, :], A.sW3), (b_s1[:, :], by_feature(A.sb1)), (b_s2[:, :], by_feature(A.sb2)),
                                 (b_s3[:, 0, :], on_all(A.sb3)), (w_e2[:, :, :], A.eW2.rearrange("e p n -> p e n")),
                                 (w_e3[0:EH2, :, :], A.eW3.rearrange("e p n -> p e n")),
                                 (w_e3[EH2:EH2 + 1, :, :], A.eb3.rearrange("(a e) n -> a e n", a=1)),
                                 (b_e1[:, :], A.eb1.rearrange("e p -> p e")), (b_e2[:, :], A.eb2.rearrange("e p -> p e")),
                                 (w_g[:, :, :], rows_on_partitions(A.gW)), (b_g[:, 0, :], on_all(A.gb))):
                    sp.dma_start(dst, src, allow_slow_non_contiguous=True).then_inc(s_w, 16)
                for e in range(NE):
                    sp.dma_start(w_e1[:, e, :, :], rows_on_partitions(A.eW1[e])).then_inc(s_w, 16)
                for c in chunks(sp):
                    wait_past(sp, s_trf, 4 * c)
                    wait_past(sp, s_r, c)
                    sp.dma_start(xn1[:, :, :], chunk(S.xn1, c)).then_inc(s_x, 16)
                    sp.dma_start(x1[:, :, :], chunk(S.x1, c)).then_inc(s_x, 16)
                    sp.wait_ge(s_ln, LN_STEPS * c + LN_STEPS)
                    sp.dma_start(chunk(S.x2, c), x2[:, :, :]).then_inc(s_st, 16)
                    sp.dma_start(chunk(S.xn2, c), xn2[:, :, :]).then_inc(s_st, 16)
                sp.wait_ge(s_st, 32 * NCH)

            @block.gpsimd
            def _(pool):
                pool.memset(w_e3[64:P, :, :], 0.0).then_inc(s_zero, 1)
                pool.memset(e2[64:P, :, :], 0.0).then_inc(s_zero, 1)
                pool.wait_ge(s_zero, 2)
                pool.memset(e2[EH2:EH2 + 1, :, :], 1.0).then_inc(s_zero, 1)
                pool.wait_ge(s_zero, 3)
                pool.iota(prio_i[:, :, :], [[-1, NE]], base=NE, channel_multiplier=0).then_inc(s_prio, 1)
                pool.wait_ge(s_w, 16 * (13 + NE))
                for c in chunks(pool):
                    pool.wait_ge(s_x, 32 * c + 32)
                    wait_past(pool, out.empty, NV * c)
                    pool.tensor_tensor(r[:, :, :], x1[:, :, :], b_s3[:, :, :].to_broadcast([P, CH, D]),
                                       ALU.add).then_inc(s_r, 1)

            @block.scalar
            def _(act):
                act.wait_ge(s_w, 16 * (13 + NE))
                act.wait_ge(s_zero, 3)
                for c in chunks(act):
                    take_transposed(act, c, xT, tr, s_trf, s_tre)
                    act.wait_ge(s_lg, 2 * c + 1)
                    act.activation(ex[:, :, :], lg[:, :, :], ACT.Exp).then_inc(s_ex, 1)
                    act.wait_ge(s_lg, 2 * c + 2)
                    act.activation(c4[:, :, :], c3[:, :, :], ACT.Exp).then_inc(s_ex, 1)
                    for n, (kind, k) in enumerate(A_GROUPS):
                        dst, bias = {"s1": (h1[:, k % KS, :], b_s1[:, k % KS:k % KS + 1]), "s2": (h2[:, :], b_s2[:, 0:1]),
                                     "e1": (e1[:, k % NE, :], b_e1[:, k % NE:k % NE + 1]),
                                     "e2": (e2[0:EH2, k % NE, :], b_e2[:, k % NE:k % NE + 1])}[kind]
                        for h, (a, b) in enumerate(HALVES):
                            src = hidden.to_take(act, c, 2 * n + h)
                            act.activation(dst[:, a * P:b * P], src[0:dst.shape[0], 0:(b - a) * P], ACT.Relu,
                                           bias=bias).then_inc(hidden.empty, 1)
                    square_root(act, small, s_std_ready, s_std, c)

            @block.vector
            def _(dve):
                dve.wait_ge(s_prio, 1)
                dve.tensor_copy(prio[:, :, :], prio_i[:, :, :]).then_inc(s_prio, 1)
                dve.wait_ge(s_w, 16 * (13 + NE))
                wide = [P, CH, NE]

                def gates(c):
                    n = [0]

                    def step(ins):
                        ins.then_inc(s_g, 1)
                        n[0] += 1
                        dve.wait_ge(s_g, GSTEPS * c + n[0])

                    def pick(values, top, hit):
                        step(dve.tensor_reduce(top[:, :, 0], values[:, :, :], AX.X, ALU.max))
                        step(dve.tensor_tensor(key[:, :, :], values[:, :, :], top[:, :, :].to_broadcast(wide), ALU.is_equal))
                        step(dve.tensor_tensor(key[:, :, :], key[:, :, :], prio[:, :, :].to_broadcast(wide), ALU.mult))
                        step(dve.tensor_reduce(c6[:, :, 0], key[:, :, :], AX.X, ALU.max))
                        step(dve.tensor_tensor(hit[:, :, :], key[:, :, :], c6[:, :, :].to_broadcast(wide), ALU.is_equal))

                    logits = out.to_take(dve, c, 0)[:, 0:CH * NE].rearrange("p (t e) -> p t e", e=NE)
                    ins = dve.tensor_tensor(lg[:, :, :], logits, b_g[:, :, :].to_broadcast(wide), ALU.add)
                    step(ins)
                    dve.sem_inc(out.empty, 1)
                    step(dve.tensor_reduce(c1[:, :, 0], lg[:, :, :], AX.X, ALU.max))
                    dve.tensor_tensor(lg[:, :, :], lg[:, :, :], c1[:, :, :].to_broadcast(wide), ALU.subtract).then_inc(s_lg, 1)
                    dve.wait_ge(s_ex, 2 * c + 1)
                    step(dve.tensor_reduce(c1[:, :, 0], ex[:, :, :], AX.X, ALU.add))
                    step(dve.reciprocal(c2[:, :, :], c1[:, :, :]))
                    step(dve.tensor_tensor(gt[:, :, :], ex[:, :, :], c2[:, :, :].to_broadcast(wide), ALU.mult))
                    pick(gt, c1, first)
                    step(dve.scalar_tensor_tensor(out=gt[:, :, :], in0=first[:, :, :], scalar=-2.0, in1=gt[:, :, :],
                                                  op0=ALU.mult, op1=ALU.add))
                    pick(gt, c2, second)
                    dve.tensor_tensor(c3[:, :, :], c2[:, :, :], c1[:, :, :], ALU.subtract).then_inc(s_lg, 1)
                    dve.wait_ge(s_ex, 2 * c + 2)
                    step(dve.tensor_scalar(c1[:, :, :], c4[:, :, :], 1.0, None, ALU.add))
                    step(dve.reciprocal(c5[:, :, :], c1[:, :, :]))
                    step(dve.tensor_tensor(c4[:, :, :], c4[:, :, :], c5[:, :, :], ALU.mult))
                    step(dve.tensor_tensor(first[:, :, :], first[:, :, :], c5[:, :, :].to_broadcast(wide), ALU.mult))
                    step(dve.tensor_tensor(second[:, :, :], second[:, :, :], c4[:, :, :].to_broadcast(wide), ALU.mult))
                    step(dve.tensor_tensor(gt[:, :, :], first[:, :, :], second[:, :, :], ALU.add))
                    step(dve.tensor_copy(key[:, :, :], gt[:, :, :]))
                    assert n[0] == GSTEPS, n[0]

                for c in chunks(dve):
                    dve.wait_ge(s_prio, 2)
                    gates(c)
                    dve.wait_ge(s_r, c + 1)
                    wait_past(dve, s_st, 32 * c)
                    for t in range(CH):
                        for n in range(3):
                            src = out.to_take(dve, c, 1 + 3 * t + n)
                            for j in range(2 if n < 2 else 1):
                                term = 2 * n + j
                                if term == 0:
                                    ins = dve.tensor_tensor(x2[:, t, :], src[:, 0:D], r[:, t, :], ALU.add)
                                else:
                                    dve.wait_ge(s_mix, MIX * c + 5 * t + term)
                                    ins = dve.scalar_tensor_tensor(out=x2[:, t, :], in0=src[:, j * D:(j + 1) * D],
                                                                   scalar=gt[:, t, term - 1:term], in1=x2[:, t, :],
                                                                   op0=ALU.mult, op1=ALU.add)
                                ins.then_inc(s_mix, 1)
                            dve.wait_ge(s_mix, MIX * c + 5 * t + min(2 * n + 2, 5))
                            dve.sem_inc(out.empty, 1)
                    layer_norm_chunk(dve, s_ln, LN_STEPS * c, x2, xn2, stats, small, s_std_ready, s_std, c)

            @block.tensor
            def _(pe):
                pe.wait_ge(s_w, 16 * (13 + NE))
                for c in chunks(pe):
                    pe.wait_ge(s_x, 32 * c + 32)
                    transpose_chunk(pe, c, xn1, tr, C.ident[:, :], s_trf, s_tre)
                    pe.wait_ge(s_tre, 4 * c + 4)
                    dst = out.to_fill(pe, c, 0)
                    for t in range(CH):
                        for j in range(KD):
                            last = pe.matmul(dst[:, t * NE:(t + 1) * NE], xT[:, j, t * P:(t + 1) * P], w_g[:, j, :],
                                             start=(t == 0 and j == 0), stop=(j == KD - 1), skip_group_check=True)
                    last.then_inc(out.full, 1)
                    for n, (kind, k) in enumerate(A_GROUPS):
                        rows = EH2 if kind == "e2" else P
                        if kind == "s2":
                            pe.wait_ge(hidden.empty, NA * c + 2 * KS)
                        if kind == "e2":
                            pe.wait_ge(hidden.empty, NA * c + 2 * (KS + k + 1))
                        for h, (a, b) in enumerate(HALVES):
                            dst = hidden.to_fill(pe, c, 2 * n + h)[0:rows, 0:(b - a) * P]
                            if kind == "s1":
                                terms = [(w_s1[:, j, k * P:(k + 1) * P], xT[:, j, a * P:b * P]) for j in range(KD)]
                            elif kind == "e1":
                                terms = [(w_e1[:, k, j, :], xT[:, j, a * P:b * P]) for j in range(KD)]
                            elif kind == "s2":
                                terms = [(w_s2[:, j, :], h1[:, j, a * P:b * P]) for j in range(KS)]
                            else:
                                terms = [(w_e2[:, k, :], e1[:, k, a * P:b * P])]
                            for j, (w, v) in enumerate(terms):
                                last = pe.matmul(dst, w, v, start=(j == 0), stop=(j == len(terms) - 1))
                            last.then_inc(hidden.full, 1)
                    pe.wait_ge(hidden.empty, NA * c + NA)
                    for t in range(CH):
                        for n in range(3):
                            dst = out.to_fill(pe, c, 1 + 3 * t + n)
                            for j in range(2 if n < 2 else 1):
                                term = 2 * n + j
                                v, w = (h2[:, t * P:(t + 1) * P], w_s3[:, :]) if term == 0 else \
                                    (e2[:, term - 1, t * P:(t + 1) * P], w_e3[:, term - 1, :])
                                last = pe.matmul(dst[:, j * D:(j + 1) * D], v, w, start=(j == 0), stop=True,
                                                 skip_group_check=True)
                            last.then_inc(out.full, 1)

        m.clear_sems()


def stage_neighbours(nc, C, S, layer, rows):
    with ExitStack() as ctx:
        m = Mem(nc, ctx, f"layer{layer}_")
        TB, GB = 8, 4
        T, G = 2 * TB, 2 * GB
        NI = NG // G
        idx = [m.sb(f"idx{b}", [P, TB], U32) for b in range(2)]
        xg = [m.sb(f"xg{b}", [P, D]) for b in range(TB)]
        hot = [m.sb(f"n_hot{b}", [P, 2, P]) for b in range(4)]
        p_sum = [m.ps(f"n_sum{b}", [P, KD, P]) for b in range(2)]
        p_deg = [m.ps(f"n_deg{b}", [P, HID]) for b in range(2)]
        s_zero, s_idx, s_hot, s_sum, s_acc = (m.sem(f"n{layer}_{n}") for n in ("zero", "idx", "hot", "sum", "acc"))
        s_gath = [m.sem(f"n{layer}_gath{b}") for b in range(TB)]
        ACC = 2 if layer == 0 else 1

        def ahead(i, q, n):
            return (i, q + n) if q + n < G else (i + 1, q + n - G)

        def bodies(eng, step):
            step(0, True, False)
            with eng.Fori(1, NI - 1) as it:
                step(it, False, False)
            step(NI - 1, False, True)

        with nc.Block() as block:
            @block.gpsimd
            def _(pool):
                pool.memset(C.nbrT[:, :, :, :], 0.0).then_inc(s_zero, 1)
                if layer == 0:
                    pool.memset(C.deg_dst[:, :], 0.0).then_inc(s_zero, 1)

                def gathers(i, first, last):
                    for b in range(2):
                        pool.wait_ge(s_idx, 2 * i + b + 1)
                        pool.nop(nofuse=True)
                        for r in range(TB):
                            if not (first and b == 0) and r % 2 == 0:
                                pool.wait_ge(s_sum, G * i + GB * b - GB + r // 2 + 1)
                                pool.nop(nofuse=True)
                            pool.indirect_dma_start(xg[r][:, :], None, rows[:, :],
                                                    bass.IndirectOffsetOnAxis(ap=idx[b][:, r:r + 1], axis=0)
                                                    ).then_inc(s_gath[r], 16)

                bodies(pool, gathers)

            @block.scalar
            def _(act):
                def body(i, first, last):
                    for b in range(2):
                        if not first:
                            act.wait_ge(s_sum, G * i + GB * b - GB)
                        act.activation(idx[b][:, :].bitcast(F32), C.gidx[:, bass.ds(T * i + TB * b, TB)].bitcast(F32),
                                       ACT.Copy).then_inc(s_idx, 1)

                bodies(act, body)

            @block.vector
            def _(dve):
                def one_hot(i, q):
                    for j in range(2):
                        dve.tensor_scalar(hot[q % 4][:, j, :], C.iota_f[:, :],
                                          C.dloc[:, bass.ds(T * i + 2 * q + j, 1)], None, ALU.is_equal).then_inc(s_hot, 1)

                def accumulate(i, q, bucket):
                    dve.wait_ge(s_sum, G * i + q + 1)
                    wait_past(dve, s_acc, ACC * (G * i + q))
                    nbr = C.nbrT[:, bass.ds(bucket, 1), :, :].rearrange("p a k n -> p (a k n)")
                    dve.tensor_tensor(nbr, p_sum[q % 2][:, :, :].rearrange("p k n -> p (k n)"), nbr,
                                      ALU.add).then_inc(s_acc, 1)
                    if layer == 0:
                        deg = C.deg_dst[:, bass.ds(bucket, 1)]
                        dve.tensor_tensor(deg, p_deg[q % 2][:, 0:1], deg, ALU.add).then_inc(s_acc, 1)

                def body(i, first, last):
                    if first:
                        dve.wait_ge(s_zero, 2 if layer == 0 else 1)
                        one_hot(i, 0)
                        one_hot(i, 1)
                        buckets = [None] + list(load_buckets(nc, dve, C.bucket[0:1, 1, 0:G]))
                    else:
                        buckets = load_buckets(nc, dve, C.bucket[0:1, 1, bass.ds(G * i - 1, G + 1)])
                    for q in range(G):
                        if q > 0:
                            accumulate(i, q - 1, buckets[q])
                        elif not first:
                            accumulate(i - 1, G - 1, buckets[0])
                        if not (last and q >= G - 2):
                            one_hot(*ahead(i, q, 2))
                    if last:
                        accumulate(i, G - 1, buckets[G])

                bodies(dve, body)

            @block.tensor
            def _(pe):
                def body(i, first, last):
                    for q in range(G):
                        if not (first and q < 2):
                            pe.wait_ge(s_acc, ACC * (G * i + q - 1))
                        pe.wait_ge(s_hot, T * i + 2 * q + 2)
                        for j in range(2):
                            t = 2 * q + j
                            pe.wait_ge(s_gath[t % TB], 16 * (2 * i + t // TB) + 16)
                            for k in range(KD):
                                last_mm = pe.matmul(p_sum[q % 2][:, k, :], xg[t % TB][:, k * P:(k + 1) * P],
                                                    hot[q % 4][:, j, :], start=(j == 0 and k == 0),
                                                    stop=(j == 1 and k == KD - 1), skip_group_check=True)
                            if layer == 0:
                                last_mm = pe.matmul(p_deg[q % 2][:, 0:2], hot[q % 4][:, j, :], C.ones[:, 0:2],
                                                    start=(j == 0), stop=(j == 1), skip_group_check=True)
                        last_mm.then_inc(s_sum, 1)

                bodies(pe, body)


def stage_sage(nc, C, A, S, layer):
    W_l, W_r, bias = (A.W_l1, A.W_r1, A.b1) if layer == 0 else (A.W_l2, A.W_r2, A.b2)
    rows, res = (S.xn2, None) if layer == 0 else (S.hid, S.x2)
    with ExitStack() as ctx:
        m = Mem(nc, ctx, f"layer{layer}_")
        w_l, w_r, b_r = m.sb("w_l", [P, KD, D]), m.sb("w_r", [P, KD, D]), m.sb("b_r", [P, D])
        wr = m.sb("wr", [P, D])
        x, nb, o, y = (m.sb(f"s_{n}", [P, CH, D]) for n in ("x", "nb", "o", "y"))
        xr = m.sb("s_xr", [P, CH, D])
        junk = m.sb("s_junk", [P, D])
        xT = m.sb("s_xT", [P, KD, CH * P])
        stats, small = m.sb("stats4", [P, CH, 6]), m.sb("small4", [P, 6, CH])
        NV = CH
        tr = [m.ps(f"s_tr{b}", [P, HID]) for b in range(2)]
        out = Banks(m, f"s{layer}_o", 4, NV)
        s_w, s_x, s_xr, s_trf, s_tre, s_nb = (m.sem(f"s{layer}_{n}") for n in ("w", "x", "xr", "trf", "tre", "nb"))
        s_deg, s_o, s_ln, s_std_ready, s_std, s_st, s_w_out = (
            m.sem(f"s{layer}_{n}") for n in ("deg", "o", "ln", "std_ready", "std", "st", "w_out"))

        with nc.Block() as block:
            @block.sync
            def _(sp):
                sp.dma_start(w_l[:, :, :], rows_on_partitions(W_l)).then_inc(s_w, 16)
                sp.dma_start(w_r[:, :, :], rows_on_partitions(W_r)).then_inc(s_w, 16)
                sp.dma_start(b_r[:, :], on_all(bias)).then_inc(s_w, 16)
                sp.dma_start(wr[:, :], on_all(A.wr.rearrange("d a -> (d a)"))).then_inc(s_w, 16)
                for c in chunks(sp):
                    wait_past(sp, s_trf, 4 * c)
                    sp.dma_start(x[:, :, :], chunk(rows, c)).then_inc(s_x, 16)
                    if res is not None:
                        wait_past(sp, s_o, 2 * CH * c)
                        sp.dma_start(xr[:, :, :], chunk(res, c)).then_inc(s_xr, 16)
                        sp.wait_ge(s_ln, LN_STEPS * c + LN_STEPS)
                        sp.dma_start(chunk(S.x3, c), o[:, :, :]).then_inc(s_st, 16)
                        sp.dma_start(chunk(S.xn3, c), y[:, :, :]).then_inc(s_st, 16)
                    else:
                        sp.wait_ge(s_ln, CH * c + CH)
                        sp.dma_start(chunk(S.hid, c), y[:, :, :]).then_inc(s_st, 16)
                sp.wait_ge(s_st, (32 if res is not None else 16) * NCH)

            @block.scalar
            def _(act):
                for c in chunks(act):
                    wait_past(act, out.full, NV * c)
                    act.activation(nb[:, :, :].rearrange("p t n -> p (t n)"),
                                   C.nbrT[:, bass.ds(c * CH, CH), :, :].rearrange("p t k n -> p (t k n)"),
                                   ACT.Copy).then_inc(s_nb, 1)
                    take_transposed(act, c, xT, tr, s_trf, s_tre)
                    if res is None:
                        wait_past(act, s_st, 16 * c)
                        for t in range(CH):
                            act.wait_ge(s_o, 2 * CH * c + 2 * t + 2)
                            act.activation(y[:, t, :], o[:, t, :], ACT.Relu).then_inc(s_ln, 1)
                    else:
                        square_root(act, small, s_std_ready, s_std, c)

            @block.vector
            def _(dve):
                step = Chain(dve, s_deg)
                if layer == 0:
                    step.link(dve.tensor_scalar(C.deg_dst[:, :], C.deg_dst[:, :], 1.0, None, ALU.max))
                    step.link(dve.reciprocal(C.rdeg[:, :], C.deg_dst[:, :]))
                dve.wait_ge(s_w, 64)
                for c in chunks(dve):
                    if res is None:
                        wait_past(dve, s_ln, CH * c)
                    else:
                        wait_past(dve, s_st, 32 * c)
                        dve.wait_ge(s_xr, 16 * c + 16)
                    for t in range(CH):
                        src = out.to_take(dve, c, t)
                        dve.scalar_tensor_tensor(out=o[:, t, :], in0=src[:, 0:D], scalar=C.rdeg[:, bass.ds(c * CH + t, 1)],
                                                 in1=b_r[:, :], op0=ALU.mult, op1=ALU.add).then_inc(s_o, 1)
                        dve.wait_ge(s_o, 2 * CH * c + 2 * t + 1)
                        dve.tensor_tensor(o[:, t, :], src[:, D:2 * D], o[:, t, :], ALU.add).then_inc(s_o, 1)
                        dve.wait_ge(s_o, 2 * CH * c + 2 * t + 2)
                        dve.sem_inc(out.empty, 1)
                    if res is not None:
                        dve.tensor_tensor(o[:, :, :], o[:, :, :], xr[:, :, :], ALU.add).then_inc(s_w_out, 1)
                        dve.wait_ge(s_w_out, (1 + CH) * c + 1)
                        layer_norm_chunk(dve, s_ln, LN_STEPS * c, o, y, stats, small, s_std_ready, s_std, c)
                        dve.wait_ge(s_ln, LN_STEPS * c + LN_STEPS)
                        for t in range(CH):
                            if t > 0:
                                dve.wait_ge(s_w_out, (1 + CH) * c + 1 + t)
                            dve.scalar_tensor_tensor(out=junk[:, :], in0=y[:, t, :], scalar=1.0, in1=wr[:, :],
                                                     op0=ALU.mult, op1=ALU.mult,
                                                     accum_out=C.route[:, bass.ds(c * CH + t, 1)]).then_inc(s_w_out, 1)

            @block.tensor
            def _(pe):
                pe.wait_ge(s_w, 64)
                for c in chunks(pe):
                    pe.wait_ge(s_x, 16 * c + 16)
                    transpose_chunk(pe, c, x, tr, C.ident[:, :], s_trf, s_tre)
                    pe.wait_ge(s_tre, 4 * c + 4)
                    pe.wait_ge(s_nb, c + 1)
                    for t in range(CH):
                        dst = out.to_fill(pe, c, t)
                        for k in range(KD):
                            pe.matmul(dst[:, 0:D], nb[:, t, k * P:(k + 1) * P], w_l[:, k, :], start=(k == 0),
                                      stop=(k == KD - 1), skip_group_check=True)
                        for k in range(KD):
                            last = pe.matmul(dst[:, D:2 * D], xT[:, k, t * P:(t + 1) * P], w_r[:, k, :], start=(k == 0),
                                             stop=(k == KD - 1), skip_group_check=True)
                        last.then_inc(out.full, 1)

        m.clear_sems()


def stage_routed(nc, C, A, S, out_ap):
    NHID = A.w1.shape[1]
    KF = NHID // P
    KEEP = max(1, N_NODES // 2) - 1
    with ExitStack() as ctx:
        m = Mem(nc, ctx)
        w1, b1 = m.sb("w1", [P, KD, NHID]), m.sb("b1", [P, KF])
        w2, b2 = m.sb("w2f", [P, KF, D]), m.sb("b2f", [P, 1, D])
        br = m.sb("br", [P, 1])
        route = m.sb("route_b", [P, NT])
        row = m.sb("row", [P, N_NODES])
        junk, junk2 = m.sb("r_junk", [P, N_NODES], BF16), m.sb("r_junk2", [P, P])
        after = m.sb("after", [P, P])
        counts = m.sb("counts", [P, NT, 3])
        rank, gate = m.sb("rank_r", [P, NT]), m.sb("gate", [P, NT])
        xn, x3, r, o = (m.sb(f"r_{n}", [P, CH, D]) for n in ("xn", "x3", "r", "o"))
        xT = m.sb("r_xT", [P, KD, CH * P])
        hT = m.sb("r_hT", [P, KF, CH * P])
        y = m.sb("r_y", [P, NT, D])
        NA = 2 * KF
        tr = [m.ps(f"r_tr{b}", [P, HID]) for b in range(2)]
        hidden, out = Banks(m, "r_h", 4, NA), Banks(m, "r_o", 2, CH)
        s_w, s_br, s_x, s_trf, s_tre, s_add = (m.sem(f"r_{n}") for n in ("w", "br", "x", "trf", "tre", "add"))
        s_route, s_row, s_row_in, s_cnt, s_dve, s_y, s_o, s_st = (
            m.sem(f"r_{n}") for n in ("route", "row", "row_in", "cnt", "dve", "y", "o", "st"))

        with nc.Block() as block:
            @block.sync
            def _(sp):
                sp.dma_start(br[:, :], on_all(A.br)).then_inc(s_br, 16)
                sp.wait_ge(s_route, 1)
                sp.dma_start(S.route.rearrange("(t p) -> p t", p=P), route[:, :],
                             allow_slow_non_contiguous=True).then_inc(s_row, 16)
                sp.wait_ge(s_row, 16)
                sp.dma_start(row[:, :], on_all(S.route[0:N_NODES])).then_inc(s_row_in, 16)
                sp.dma_start(w1[:, :, :], rows_on_partitions(A.w1)).then_inc(s_w, 16)
                sp.dma_start(b1[:, :], by_feature(A.b1f), allow_slow_non_contiguous=True).then_inc(s_w, 16)
                sp.dma_start(w2[:, :, :], rows_on_partitions(A.w2)).then_inc(s_w, 16)
                sp.dma_start(b2[:, 0, :], on_all(A.b2f)).then_inc(s_w, 16)
                for c in chunks(sp):
                    wait_past(sp, s_trf, 4 * c)
                    wait_past(sp, s_add, c)
                    sp.dma_start(xn[:, :, :], chunk(S.xn3, c)).then_inc(s_x, 16)
                    sp.dma_start(x3[:, :, :], chunk(S.x3, c)).then_inc(s_x, 16)
                    sp.wait_ge(s_o, 2 * CH * c + 2 * CH)
                    sp.dma_start(chunk(out_ap, c), o[:, :, :]).then_inc(s_st, 16)
                sp.wait_ge(s_st, 16 * NCH)

            @block.gpsimd
            def _(pool):
                for c in chunks(pool):
                    pool.wait_ge(s_x, 32 * c + 32)
                    wait_past(pool, s_o, 2 * CH * c)
                    pool.tensor_tensor(r[:, :, :], xn[:, :, :], x3[:, :, :], ALU.add).then_inc(s_add, 1)

            @block.scalar
            def _(act):
                act.wait_ge(s_w, 64)
                for c in chunks(act):
                    take_transposed(act, c, xT, tr, s_trf, s_tre)
                    for k in range(KF):
                        for h, (a, b) in enumerate(HALVES):
                            src = hidden.to_take(act, c, 2 * k + h)
                            act.activation(hT[:, k, a * P:b * P], src[:, 0:(b - a) * P], ACT.Gelu_apprx_tanh,
                                           bias=b1[:, k:k + 1]).then_inc(hidden.empty, 1)
                    for t in range(CH):
                        src = out.to_take(act, c, t)
                        act.activation(y[:, bass.ds(c * CH + t, 1), :].rearrange("p a n -> p (a n)"), src[:, 0:D],
                                       ACT.Copy).then_inc(out.empty, 1)

            @block.vector
            def _(dve):
                step = Chain(dve, s_dve)
                dve.wait_ge(s_br, 16)
                dve.tensor_scalar(route[:, :], C.route[:, :], br[:, 0:1], None, ALU.add).then_inc(s_route, 1)
                step.link(dve.tensor_scalar(after[:, :], C.iota_f[:, :], C.part_f[:, 0:1], None, ALU.is_lt))
                step.link(dve.memset(counts[:, :, :], 0.0))
                dve.wait_ge(s_route, 1)
                dve.wait_ge(s_row_in, 16)
                for t in range(NT):
                    a, b = t * P, min((t + 1) * P, N_NODES)
                    own = route[:, t:t + 1]
                    if t > 0:
                        step.link(dve.tensor_scalar(junk[:, 0:a], row[:, 0:a], own, None, ALU.is_ge, ALU.add,
                                                    accum_out=counts[:, t, 0:1]))
                    step.link(dve.tensor_scalar(junk[:, a:N_NODES], row[:, a:N_NODES], own, None, ALU.is_gt, ALU.add,
                                                accum_out=counts[:, t, 1:2]))
                    step.link(dve.scalar_tensor_tensor(out=junk2[:, 0:b - a], in0=row[:, a:b], scalar=own,
                                                       in1=after[:, 0:b - a], op0=ALU.is_equal, op1=ALU.mult,
                                                       accum_out=counts[:, t, 2:3]))
                step.link(dve.tensor_reduce(rank[:, :], counts[:, :, :], AX.X, ALU.add))
                step.link(dve.scalar_tensor_tensor(out=gate[:, :], in0=rank[:, :], scalar=float(KEEP), in1=route[:, :],
                                                   op0=ALU.is_lt, op1=ALU.mult))
                dve.wait_ge(s_w, 64)
                for c in chunks(dve):
                    dve.wait_ge(s_add, c + 1)
                    wait_past(dve, s_st, 16 * c)
                    for t in range(CH):
                        dve.wait_ge(out.empty, CH * c + t + 1)
                        dve.tensor_tensor(o[:, t, :], y[:, bass.ds(c * CH + t, 1), :].rearrange("p a n -> p (a n)"),
                                          b2[:, 0, :], ALU.add).then_inc(s_o, 1)
                    for t in range(CH):
                        dve.wait_ge(s_o, 2 * CH * c + CH + t)
                        dve.scalar_tensor_tensor(out=o[:, t, :], in0=o[:, t, :], scalar=gate[:, bass.ds(c * CH + t, 1)],
                                                 in1=r[:, t, :], op0=ALU.mult, op1=ALU.add).then_inc(s_o, 1)

            @block.tensor
            def _(pe):
                pe.wait_ge(s_w, 64)
                for c in chunks(pe):
                    pe.wait_ge(s_x, 32 * c + 32)
                    transpose_chunk(pe, c, xn, tr, C.ident[:, :], s_trf, s_tre)
                    pe.wait_ge(s_tre, 4 * c + 4)
                    for k in range(KF):
                        for h, (a, b) in enumerate(HALVES):
                            dst = hidden.to_fill(pe, c, 2 * k + h)[:, 0:(b - a) * P]
                            for j in range(KD):
                                last = pe.matmul(dst, w1[:, j, k * P:(k + 1) * P], xT[:, j, a * P:b * P],
                                                 start=(j == 0), stop=(j == KD - 1))
                            last.then_inc(hidden.full, 1)
                    pe.wait_ge(hidden.empty, NA * c + NA)
                    for t in range(CH):
                        dst = out.to_fill(pe, c, t)[:, 0:D]
                        for j in range(KF):
                            last = pe.matmul(dst, hT[:, j, t * P:(t + 1) * P], w2[:, j, :], start=(j == 0), stop=(j == KF - 1))
                        last.then_inc(out.full, 1)


def build(nc, A, out):
    with ExitStack() as ctx:
        m = Mem(nc, ctx)
        C, S = Names(), Names()
        C.iota_i = m.sb("iota_i", [P, P], I32)
        C.iota_f = m.sb("iota_f", [P, P])
        C.iota_b = m.sb("iota_b", [P, P], F16)
        C.iota_h = m.sb("iota_h", [P, NCOL], I16)
        C.part_i = m.sb("part_i", [P, 1], I32)
        C.part_f = m.sb("part_f", [P, 1])
        C.ident = m.sb("ident", [P, P])
        C.before = m.sb("before", [P, P])
        C.ones = m.sb("ones", [P, P])
        C.zeros = m.sb("zeros", [P, P], F16)
        C.zeros_w = m.sb("zeros_w", [P, NCOL], F16)
        C.bucket = m.sb("bucket", [1, 2, NG], I32)
        C.gidx = m.sb("gidx", [P, NCOL], U32)
        C.dloc = m.sb("dloc", [P, NCOL])
        C.deg_dst, C.rdeg = m.sb("deg_dst", [P, NT]), m.sb("rdeg", [P, NT])
        C.route = m.sb("route", [P, NT])

        def dram(name, shape, dt=F32):
            return nc.dram_tensor(name, shape, dt).ap()

        S.recs = dram("recs_d", [NSLOT + EC, REC])
        S.bucket, S.bucket2 = dram("bucket_d", [NG], I32), dram("bucket2_d", [NG], I32)
        S.xn, S.xn1, S.xn2, S.xn3, S.x1, S.x2, S.x3, S.hid = (
            dram(f"{n}_d", [NPAD, D]) for n in ("xn", "xn1", "xn2", "xn3", "x1", "x2", "x3", "hid"))
        S.xnT = dram("xnT_d", [D, NPAD])
        S.p, S.q = dram("p_d", [NPAD, 2 * HID]), dram("q_d", [NPAD, HID])
        S.deg, S.route = dram("deg_d", [NPAD]), dram("route_d", [NPAD])

        stage_constants(nc, C)
        stage_prepare(nc, C, A, S)
        with ExitStack() as edge_ctx:
            e = Mem(nc, edge_ctx)
            C.aggT = e.sb("aggT", [P, NT, KH, P])
            C.deg_src = e.sb("deg_src", [P, NT])
            stage_edge_network(nc, C, A, S)
            stage_update(nc, C, A, S)
        stage_experts(nc, C, A, S)
        with ExitStack() as sage_ctx:
            e = Mem(nc, sage_ctx)
            C.nbrT = e.sb("nbrT", [P, NT, KD, P])
            for layer, rows in enumerate((S.xn2, S.hid)):
                stage_neighbours(nc, C, S, layer, rows)
                stage_sage(nc, C, A, S, layer)
        stage_routed(nc, C, A, S, out)


_INS = {"mW1": "L0_gnn_mW1", "mb1": "L0_gnn_mb1", "mW2": "L0_gnn_mW2", "mb2": "L0_gnn_mb2", "uW1": "L0_gnn_uW1",
        "ub1": "L0_gnn_ub1", "uW2": "L0_gnn_uW2", "ub2": "L0_gnn_ub2", "sW1": "L0_ffn_sW1", "sb1": "L0_ffn_sb1",
        "sW2": "L0_ffn_sW2", "sb2": "L0_ffn_sb2", "sW3": "L0_ffn_sW3", "sb3": "L0_ffn_sb3", "eW1": "L0_ffn_eW1",
        "eb1": "L0_ffn_eb1", "eW2": "L0_ffn_eW2", "eb2": "L0_ffn_eb2", "eW3": "L0_ffn_eW3", "eb3": "L0_ffn_eb3",
        "gW": "L0_ffn_gW", "gb": "L0_ffn_gb", "W_l1": "L1_gnn_W_l1", "b1": "L1_gnn_b1", "W_r1": "L1_gnn_W_r1",
        "W_l2": "L1_gnn_W_l2", "b2": "L1_gnn_b2", "W_r2": "L1_gnn_W_r2", "wr": "L1_ffn_wr", "br": "L1_ffn_br",
        "w1": "L1_ffn_w1", "b1f": "L1_ffn_b1", "w2": "L1_ffn_w2", "b2f": "L1_ffn_b2"}


def kernel(**inputs):
    import numpy as _np
    import concourse.bacc as _bacc
    from concourse import mybir as _mybir
    from concourse.bass_utils import run_bass_kernel_spmd as _run

    def padded(name, rows, fill):
        a = _np.asarray(inputs[name])
        whole = _np.full((rows,) + a.shape[1:], fill, a.dtype)
        whole[:a.shape[0]] = a
        return whole

    host = {"x": padded("x", NPAD, 0), "src": padded("src", EPAD, NPAD), "dst": padded("dst", EPAD, NPAD),
            "edge_attr": padded("edge_attr_16", EPAD, 0)}
    for short, name in _INS.items():
        host[short] = _np.ascontiguousarray(inputs[name])
    nc = _bacc.Bacc("TRN2", target_bir_lowering=False, num_devices=1)
    A, arrays = Names(), {}
    for short, a in host.items():
        arrays[f"in_{short}"] = a
        setattr(A, short, nc.dram_tensor(f"in_{short}", a.shape, _mybir.dt.from_np(a.dtype), kind="ExternalInput").ap())
    out = nc.dram_tensor("out_0", (NPAD, D), F32, kind="ExternalOutput").ap()
    build(nc, A, out)
    r = _run(nc, [arrays], core_ids=[0])
    return r.results[0]["out_0"][:N_NODES]
```

```python
from contextlib import ExitStack

import concourse.bass as bass
from concourse import mybir

ALU = mybir.AluOpType
ACT = mybir.ActivationFunctionType
AX = mybir.AxisListType
F32 = mybir.dt.float32
F32R = mybir.dt.float32r
F16 = mybir.dt.float16
BF16 = mybir.dt.bfloat16
I32 = mybir.dt.int32
U32 = mybir.dt.uint32
I16 = mybir.dt.int16

P = 128
N_NODES = 3125
D = 256
KD = D // P
HID = 512
KH = HID // P
N_EDGES = 53125
EDGE_DIM = 16
NT = -(-N_NODES // P)
NPAD = NT * P
EC = -(-N_EDGES // P)
EPAD = EC * P
GROUP = 2 * P
NG = (N_EDGES + NT * (GROUP - 1)) // GROUP
NSLOT = NG * GROUP
NCOL = 2 * NG
REC = 2 + 2 * EDGE_DIM
CH = 5
NCH = NT // CH
EPS = 1e-5
HB = 8
UNROLL = HB
TAB = EC // NT // UNROLL * UNROLL
BATCH = 8


class Names:
    pass


class Mem:

    def __init__(self, nc, ctx, prefix=""):
        self.nc, self.ctx, self.prefix, self.sems = nc, ctx, prefix, []

    def sb(self, name, shape, dt=F32):
        return self.ctx.enter_context(self.nc.sbuf_tensor(self.prefix + name, shape, dt))

    def ps(self, name, shape, dt=F32):
        return self.ctx.enter_context(self.nc.psum_tensor(self.prefix + name, shape, dt))

    def sem(self, name):
        self.sems.append(self.nc.alloc_semaphore(self.prefix + name))
        return self.sems[-1]

    def clear_sems(self):
        for sem in self.sems:
            self.nc.sync.sem_clear(sem)
            self.nc.release_semaphore(sem)


class Chain:

    def __init__(self, eng, sem):
        self.eng, self.sem, self.n = eng, sem, 0

    def link(self, ins):
        ins.then_inc(self.sem, 1)
        self.n += 1
        self.eng.wait_ge(self.sem, self.n)


def chunks(eng):
    yield 0
    with eng.Fori(1, NCH) as c:
        yield c


def load_ahead(eng, load, store):
    load(0)
    load(1)
    store(0)
    with eng.Fori(1, NCH - 1) as c:
        load(c + 1)
        store(c)
    store(NCH - 1)


def wait_past(eng, sem, count):
    if not (isinstance(count, int) and count == 0):
        eng.wait_ge(sem, count)


def layer_norm_chunk(dve, done, at, x, xn, stats, small):
    for t in range(CH):
        dve.bn_stats(stats[:, t, :], x[:, t, :]).then_inc(done, 1)
    dve.wait_ge(done, at + CH)
    mean, var, rstd, diff, diff2 = (small[:, n, :] for n in range(5))
    dve.tensor_tensor(mean, stats[:, :, 1], stats[:, :, 4], ALU.add).then_inc(done, 1)
    dve.tensor_tensor(diff, stats[:, :, 1], stats[:, :, 4], ALU.subtract).then_inc(done, 1)
    dve.tensor_tensor(var, stats[:, :, 2], stats[:, :, 5], ALU.add).then_inc(done, 1)
    dve.wait_ge(done, at + CH + 3)
    dve.tensor_scalar(mean, mean, 0.5, None, ALU.mult).then_inc(done, 1)
    dve.tensor_tensor(diff2, diff, diff, ALU.mult).then_inc(done, 1)
    dve.tensor_scalar(var, var, 1.0 / D, EPS, ALU.mult, ALU.add).then_inc(done, 1)
    dve.wait_ge(done, at + CH + 6)
    dve.scalar_tensor_tensor(out=var, in0=diff2, scalar=0.25, in1=var, op0=ALU.mult, op1=ALU.add).then_inc(done, 1)
    dve.wait_ge(done, at + CH + 7)
    bits = rstd.bitcast(I32)
    dve.tensor_scalar(bits, var.bitcast(I32), 1, None, ALU.logical_shift_right).then_inc(done, 1)
    dve.wait_ge(done, at + CH + 8)
    dve.tensor_scalar(bits, bits, -1.0, float(0x5F3759DF), ALU.mult, ALU.add).then_inc(done, 1)
    for n in range(NEWTON):
        first = at + CH + 9 + 4 * n
        dve.wait_ge(done, first)
        dve.tensor_tensor(diff, rstd, rstd, ALU.mult).then_inc(done, 1)
        dve.wait_ge(done, first + 1)
        dve.tensor_tensor(diff, diff, var, ALU.mult).then_inc(done, 1)
        dve.wait_ge(done, first + 2)
        dve.tensor_scalar(diff, diff, -0.5, 1.5, ALU.mult, ALU.add).then_inc(done, 1)
        dve.wait_ge(done, first + 3)
        dve.tensor_tensor(rstd, rstd, diff, ALU.mult).then_inc(done, 1)
    dve.wait_ge(done, at + CH + 9 + 4 * NEWTON)
    for t in range(CH):
        dve.tensor_scalar(xn[:, t, :], x[:, t, :], mean[:, t:t + 1], rstd[:, t:t + 1], ALU.subtract,
                          ALU.mult).then_inc(done, 1)


NEWTON = 4
LN_STEPS = 2 * CH + 9 + 4 * NEWTON


def stage_constants(nc, C):
    with ExitStack() as ctx:
        m = Mem(nc, ctx)
        s_iota, s_done = m.sem("s_iota"), m.sem("s_const")
        with nc.Block() as block:
            @block.gpsimd
            def _(pool):
                pool.iota(C.iota_i[:, :], [[1, P]], base=0, channel_multiplier=0).then_inc(s_iota, 1)
                pool.iota(C.iota_h[:, :], [[1, NCOL]], base=0, channel_multiplier=0,
                          allow_small_or_imprecise_dtypes=True).then_inc(s_iota, 1)
                pool.iota(C.part_i[:, :], [[0, 1]], base=0, channel_multiplier=1).then_inc(s_iota, 1)

            @block.vector
            def _(dve):
                step = Chain(dve, s_done)
                dve.wait_ge(s_iota, 3)
                step.link(dve.tensor_copy(C.iota_f[:, :], C.iota_i[:, :]))
                step.link(dve.tensor_copy(C.iota_b[:, :], C.iota_i[:, :]))
                step.link(dve.tensor_copy(C.part_f[:, :], C.part_i[:, :]))
                step.link(dve.tensor_scalar(C.ident[:, :], C.iota_f[:, :], C.part_f[:, 0:1], None, ALU.is_equal))
                step.link(dve.tensor_scalar(C.before[:, :], C.iota_f[:, :], C.part_f[:, 0:1], None, ALU.is_gt))
                step.link(dve.memset(C.ones[:, :], 1.0))
                step.link(dve.memset(C.zeros[:, :], 0.0))
                step.link(dve.memset(C.zeros_w[:, :], 0.0))


def stage_prepare(nc, C, A, S):
    with ExitStack() as ctx:
        m = Mem(nc, ctx)
        key = [m.sb(f"key{k}", [P, EC], I32) for k in range(2)]
        hi_i = m.sb("hi_i", [P, EC], I32)
        hi16 = [m.sb(f"hi16_{k}", [P, EC], I16) for k in range(2)]
        lo_i = m.sb("lo_i", [P, EC], I32)
        pos = m.sb("pos", [P, EC])
        pad_pos = m.sb("pad_pos", [P, EC])
        iota_c = m.sb("iota_c", [P, EC])
        slot_src = m.sb("slot_src", [P, EC], U32)
        slot_dst = m.sb("slot_dst", [P, EC], I32)
        lane, col = m.sb("lane", [P, EC]), m.sb("col", [P, EC])
        val = m.sb("val", [P, 2, EC])
        ends = m.sb("ends", [P, NT + 1])
        cnt = m.sb("cnt", [P, NT])
        grp_i = m.sb("grp_i", [P, NT], I32)
        grp = m.sb("grp", [P, NT])
        start = m.sb("start", [P, NT])
        off = m.sb("off", [P, NT])
        hit = m.sb("hit", [P, NT])
        gk_i = m.sb("gk_i", [P, 2], I32)
        gk = m.sb("gk", [P, 2])
        bkt_f = m.sb("bkt_f", [P, 2])
        bkt_i = m.sb("bkt_i", [P, 2], I32)
        recs = m.sb("recs", [P, EC, REC])
        fill = m.sb("fill", [P, 29, REC])
        stage = [m.sb(f"stage{b}", [P, BATCH, REC]) for b in range(2)]
        stage_pos = [m.sb(f"stage_pos{b}", [P, BATCH], U32) for b in range(2)]
        lane_one = [m.sb(f"lane_one{b}", [P, P], F16) for b in range(HB)]
        lane_hot = [m.sb(f"lane_hot{b}", [P, 2, P], F16) for b in range(HB)]
        col_hot = [m.sb(f"col_hot{b}", [P, NCOL], F16) for b in range(HB)]
        member = m.sb("member", [P, NT, EC], BF16)
        rank = m.sb("rank", [P, NT, EC])
        with ExitStack() as early:
            attr = Mem(nc, early).sb("attr", [P, EC * EDGE_DIM])
        xc = m.sb("xc", [P, CH, D])
        xnc = m.sb("xnc", [P, CH, D])
        xtc = m.sb("xtc", [P, KD, CH * P])
        w_pq = m.sb("w_pq", [P, 2, KD, HID])
        p_out = [m.sb(f"p_out{b}", [P, 2, HID]) for b in range(2)]
        q_out = [m.sb(f"q_out{b}", [P, HID]) for b in range(2)]
        stats = m.sb("stats", [P, CH, 6])
        small = m.sb("small", [P, 5, CH])

        acc = [m.ps(f"acc{k}", [P, HID]) for k in range(2)]
        tr = [m.ps(f"tr{k}", [P, HID]) for k in range(2)]
        pq = [[m.ps(f"pq{h}{b}", [P, HID]) for b in range(2)] for h in range(2)]

        s_key, s_attr, s_fill, s_filled = m.sem("s_key"), m.sem("s_attr"), m.sem("s_fill"), m.sem("s_filled")
        s_padkey = m.sem("s_padkey")
        s_iota = m.sem("s_iota_c")
        s_dve = m.sem("s_dve")
        s_cnt, s_sum = m.sem("s_cnt"), m.sem("s_sum")
        s_high, s_low = m.sem("s_high"), m.sem("s_low")
        s_order = m.sem("s_order")
        s_staged = m.sem("s_staged")
        s_scat = [m.sem(f"s_scat{b}") for b in range(2)]
        s_lane, s_col, s_scaled = m.sem("s_lane"), m.sem("s_col"), m.sem("s_scaled")
        s_hot_used, s_table = m.sem("s_hot_used"), m.sem("s_table")
        s_bkt, s_bkt_out, s_bkt_in = m.sem("s_bkt"), m.sem("s_bkt_out"), m.sem("s_bkt_in")
        s_w, s_x = m.sem("s_w"), m.sem("s_x")
        s_ln = m.sem("s_ln")
        s_tr, s_xt = m.sem("s_tr"), m.sem("s_xt")
        s_pq, s_phi, s_plo, s_q = m.sem("s_pq"), m.sem("s_phi"), m.sem("s_plo"), m.sem("s_q")
        s_pst, s_qst = [m.sem(f"s_pst{b}") for b in range(2)], [m.sem(f"s_qst{b}") for b in range(2)]
        s_xnst, s_xtst = m.sem("s_xnst"), m.sem("s_xtst")
        s_stage = [m.sem(f"s_stage{b}") for b in range(2)]

        with nc.Block() as block:
            @block.sync
            def _(sp):
                for k, src in enumerate((A.src, A.dst)):
                    sp.dma_start(key[k][:, :], src.rearrange("(p c) -> p c", c=EC)).then_inc(s_key, 16)
                sp.dma_start(attr[:, :], A.edge_attr.rearrange("(p c) w -> p (c w)", c=EC)).then_inc(s_attr, 16)
                sp.wait_ge(s_fill, 3)
                recs_v = S.recs[0:NSLOT, :].rearrange("(n p r) w -> n p (r w)", p=P, r=29)
                for n in range(NSLOT // (29 * P)):
                    sp.dma_start(recs_v[n], fill[:, :, :].rearrange("p r w -> p (r w)")).then_inc(s_filled, 16)
                sp.wait_ge(s_low, 1)
                sp.wait_ge(s_order, 1)
                for h in range(2):
                    sp.dma_start(w_pq[:, h, :, :],
                                 A.mW1[h * D:(h + 1) * D, :].rearrange("(k p) n -> p k n", p=P)).then_inc(s_w, 16)
                sp.wait_ge(s_order, 2)
                def fill_stages(i):
                    for b in range(2):
                        at = (2 * i + b) * BATCH
                        wait_past(sp, s_scat[b], 16 * BATCH * i)
                        sp.dma_start(stage[b][:, :, :].rearrange("p c w -> p (c w)"),
                                     recs[:, bass.ds(at, BATCH), :].rearrange("p c w -> p (c w)")).then_inc(s_stage[b], 16)
                        sp.dma_start(stage_pos[b][:, :], slot_src[:, bass.ds(at, BATCH)]).then_inc(s_stage[b], 16)

                fill_stages(0)
                with sp.Fori(1, EC // (2 * BATCH)) as i:
                    fill_stages(i)

            @block.gpsimd
            def _(pool):
                pool.memset(fill[:, :, 0:1], -1.0).then_inc(s_fill, 1)
                pool.memset(fill[:, :, 1:2].bitcast(U32), 0).then_inc(s_fill, 1)
                pool.memset(fill[:, :, 2:REC], 0.0).then_inc(s_fill, 1)
                pool.iota(lo_i[:, :], [[1, EC]], base=NSLOT, channel_multiplier=0).then_inc(s_iota, 1)
                pool.iota(gk_i[:, :], [[1, 2]], base=0, channel_multiplier=2).then_inc(s_iota, 1)
                pool.wait_ge(s_attr, 16)
                pool.wait_ge(s_high, 1)
                pool.tensor_tensor(recs[:, :, 2 + EDGE_DIM:REC], attr[:, :].rearrange("p (c w) -> p c w", w=EDGE_DIM),
                                   recs[:, :, 2:2 + EDGE_DIM], ALU.subtract).then_inc(s_low, 1)
                pool.wait_ge(s_filled, 16 * (NSLOT // (29 * P)))
                with pool.Fori(0, EC // (2 * BATCH)) as i:
                    for b in range(2):
                        pool.wait_ge(s_stage[b], 32 * i + 32)
                        pool.nop(nofuse=True)
                        for j in range(BATCH):
                            pool.indirect_dma_start(
                                S.recs[:, :], bass.IndirectOffsetOnAxis(ap=stage_pos[b][:, j:j + 1], axis=0),
                                stage[b][:, j, :], None).then_inc(s_scat[b], 16)
                for b in range(2):
                    pool.wait_ge(s_scat[b], 16 * BATCH * (EC // (2 * BATCH)))

            @block.scalar
            def _(act):
                act.wait_ge(s_attr, 16)
                act.activation(recs[:, :, 2:2 + EDGE_DIM].bitcast(F32R),
                               attr[:, :].rearrange("p (c w) -> p c w", w=EDGE_DIM), ACT.Copy).then_inc(s_high, 1)
                act.wait_ge(s_bkt, 1)
                act.dma_start(S.bucket.rearrange("(p j) -> p j", j=2), bkt_i[0:NG // 2, :]).then_inc(s_bkt_out, 16)
                act.wait_ge(s_bkt_out, 16)
                act.dma_start(C.bucket[0:1, 0, :], S.bucket.rearrange("(a k) -> a k", a=1)).then_inc(s_bkt_in, 16)
                act.wait_ge(s_bkt, 2)
                act.dma_start(S.bucket2.rearrange("(p j) -> p j", j=2), bkt_i[0:NG // 2, :]).then_inc(s_bkt_out, 16)
                act.wait_ge(s_bkt_out, 32)
                act.dma_start(C.bucket[0:1, 1, :], S.bucket2.rearrange("(a k) -> a k", a=1)).then_inc(s_bkt_in, 16)

                def scaled(c, b):
                    act.wait_ge(s_lane, c + 1)
                    for k in range(2):
                        act.activation(lane_hot[b][:, k, :], lane_one[b][:, :], ACT.Copy,
                                       scale=val[:, k, bass.ds(c, 1)]).then_inc(s_scaled, 1)

                x_v = A.x.rearrange("(t p) d -> p t d", p=P)
                act.wait_ge(s_low, 1)
                for c in chunks(act):
                    wait_past(act, s_ln, LN_STEPS * c)
                    act.dma_start(xc[:, :, :], x_v[:, bass.ds(c * CH, CH), :]).then_inc(s_x, 16)
                    act.wait_ge(s_ln, LN_STEPS * c + LN_STEPS)
                    act.dma_start(S.xn.rearrange("(t p) d -> p t d", p=P)[:, bass.ds(c * CH, CH), :],
                                  xnc[:, :, :]).then_inc(s_xnst, 16)
                    wait_past(act, s_xtst, 16 * c)
                    for k in range(KD):
                        for h in range(2):
                            w = 4 * P if h == 0 else P
                            act.wait_ge(s_tr, 4 * c + 2 * k + h + 1)
                            act.activation(xtc[:, k, 4 * P * h:4 * P * h + w], tr[h][:, 0:w],
                                           ACT.Copy).then_inc(s_xt, 1)
                    act.wait_ge(s_xt, 4 * c + 4)
                    act.dma_start(S.xnT.rearrange("(k p) n -> p k n", p=P)[:, :, bass.ds(c * CH * P, CH * P)],
                                  xtc[:, :, :]).then_inc(s_xtst, 16)
                    for t in range(CH):
                        b, uses = t % 2, (CH + 1 - t % 2) // 2
                        act.wait_ge(s_pq, 2 * CH * c + 2 * t + 1)
                        wait_past(act, s_pst[b], 16 * (uses * c + t // 2))
                        act.activation(p_out[b][:, 0, :].bitcast(F32R), pq[0][b][:, :], ACT.Copy).then_inc(s_phi, 1)
                        act.wait_ge(s_pq, 2 * CH * c + 2 * t + 2)
                        wait_past(act, s_qst[b], 16 * (uses * c + t // 2))
                        act.activation(q_out[b][:, :], pq[1][b][:, :], ACT.Copy).then_inc(s_q, 1)
                        act.wait_ge(s_q, CH * c + t + 1)
                        act.dma_start(S.q[bass.ds((c * CH + t) * P, P), :], q_out[b][:, :]).then_inc(s_qst[b], 16)
                        with act.Fori(0, TAB // UNROLL) as g:
                            for h in range(UNROLL):
                                scaled((CH * c + t) * TAB + UNROLL * g + h, h % HB)
                        act.wait_ge(s_plo, CH * c + t + 1)
                        act.dma_start(S.p[bass.ds((c * CH + t) * P, P), :],
                                      p_out[b][:, :, :].rearrange("p h n -> p (h n)")).then_inc(s_pst[b], 16)
                with act.Fori(NT * TAB // UNROLL, EC // UNROLL) as g:
                    for h in range(UNROLL):
                        scaled(UNROLL * g + h, h % HB)
                for b in range(2):
                    act.wait_ge(s_pst[b], 16 * NCH * ((CH + 1 - b) // 2))
                    act.wait_ge(s_qst[b], 16 * NCH * ((CH + 1 - b) // 2))
                act.wait_ge(s_xnst, 16 * NCH)
                act.wait_ge(s_xtst, 16 * NCH)
                act.wait_ge(s_bkt_in, 32)

            @block.vector
            def _(dve):
                step = Chain(dve, s_dve)
                dve.wait_ge(s_iota, 2)
                step.link(dve.tensor_copy(iota_c[:, :], lo_i[:, :]))
                step.link(dve.tensor_copy(gk[:, :], gk_i[:, :]))
                for k in range(2):
                    dve.wait_ge(s_key, 32)
                    dve.tensor_scalar(hi_i[:, :], key[k][:, :], 7, None, ALU.logical_shift_right).then_inc(s_dve, 1)
                    dve.tensor_scalar(lo_i[:, :], key[k][:, :], P - 1, None, ALU.bitwise_and).then_inc(s_dve, 1)
                    step.n += 2
                    dve.wait_ge(s_dve, step.n)
                    dve.tensor_copy(hi16[k][:, :], hi_i[:, :]).then_inc(s_dve, 1)
                    if k == 0:
                        dve.tensor_copy(recs[:, :, 0], lo_i[:, :]).then_inc(s_dve, 1)
                        dve.tensor_scalar(val[:, 0, :], key[0][:, :], float(-NPAD // 2), None, ALU.add).then_inc(s_dve, 1)
                        dve.tensor_copy(recs[:, :, 1].bitcast(I32), key[1][:, :]).then_inc(s_dve, 1)
                        step.n += 4
                    else:
                        dve.tensor_scalar(val[:, 1, :], lo_i[:, :], 1.0, None, ALU.add).then_inc(s_dve, 1)
                        step.n += 2
                    dve.wait_ge(s_dve, step.n)
                    for b in range(NT):
                        dve.tensor_scalar(member[:, b, :], hi16[k][:, :], float(b), None, ALU.is_equal).then_inc(s_dve, 1)
                    step.n += NT
                    dve.wait_ge(s_dve, step.n)
                    flat = member[:, :, :].rearrange("p b c -> p (b c)")
                    step.link(dve.tensor_tensor_scan(rank[:, :, :].rearrange("p b c -> p (b c)"), flat, flat, 0.0,
                                                     ALU.add, ALU.bypass))
                    step.link(dve.memset(ends[:, 0:1], 0.0))
                    step.link(dve.tensor_copy(ends[:, 1:NT + 1], rank[:, :, EC - 1]))
                    step.link(dve.tensor_tensor(cnt[:, :], ends[:, 1:NT + 1], ends[:, 0:NT], ALU.subtract))
                    dve.sem_inc(s_cnt, 1)
                    dve.wait_ge(s_sum, k + 1)
                    step.link(dve.tensor_scalar(grp_i[:, :], acc[1][:, 0:NT], float(GROUP - 1), None, ALU.add))
                    step.link(dve.tensor_scalar(grp_i[:, :], grp_i[:, :], 8, None, ALU.logical_shift_right))
                    step.link(dve.tensor_copy(grp[:, :], grp_i[:, :]))
                    step.link(dve.tensor_tensor_scan(start[:, :], grp[:, :], grp[:, :], 0.0, ALU.add, ALU.bypass))
                    step.link(dve.tensor_tensor(start[:, :], start[:, :], grp[:, :], ALU.subtract))
                    step.link(dve.scalar_tensor_tensor(out=off[:, :], in0=start[:, :], scalar=float(GROUP),
                                                       in1=acc[0][:, 0:NT], op0=ALU.mult, op1=ALU.add))
                    step.link(dve.tensor_tensor(off[:, :], off[:, :], ends[:, 0:NT], ALU.subtract))
                    step.link(dve.tensor_scalar(off[:, :], off[:, :], -1.0, None, ALU.add))
                    for b in range(NT):
                        dve.scalar_tensor_tensor(out=rank[:, b, :], in0=rank[:, b, :], scalar=off[:, b:b + 1],
                                                 in1=member[:, b, :], op0=ALU.add, op1=ALU.mult).then_inc(s_dve, 1)
                    step.n += NT
                    dve.wait_ge(s_dve, step.n)
                    step.link(dve.tensor_reduce(pos[:, :], rank[:, :, :].rearrange("p b c -> p c b"), AX.X, ALU.add))
                    step.link(dve.scalar_tensor_tensor(out=pad_pos[:, :], in0=hi16[k][:, :], scalar=float(NT),
                                                       in1=iota_c[:, :], op0=ALU.is_equal, op1=ALU.mult))
                    slot = slot_src if k == 0 else slot_dst
                    step.link(dve.tensor_tensor(slot[:, :], pos[:, :], pad_pos[:, :], ALU.add))
                    if k == 0:
                        dve.sem_inc(s_order, 2)
                    if k == 1:
                        dve.wait_ge(s_bkt_in, 16)
                    for j in range(2):
                        step.link(dve.tensor_scalar(hit[:, :], start[:, :], gk[:, j:j + 1], None, ALU.is_le, ALU.add,
                                                    accum_out=bkt_f[:, j:j + 1]))
                    step.link(dve.tensor_scalar(bkt_i[:, :], bkt_f[:, :], -1.0, None, ALU.add))
                    dve.sem_inc(s_bkt, 1)
                step.link(dve.tensor_scalar(lo_i[:, :], slot_dst[:, :], 1, P - 1, ALU.logical_shift_right, ALU.bitwise_and))
                step.link(dve.tensor_copy(lane[:, :], lo_i[:, :]))
                step.link(dve.tensor_scalar(lo_i[:, :], slot_dst[:, :], 8, 1, ALU.logical_shift_right, ALU.logical_shift_left))
                step.link(dve.tensor_scalar(hi_i[:, :], slot_dst[:, :], 1, None, ALU.bitwise_and))
                step.link(dve.tensor_copy(col[:, :], lo_i[:, :]))
                step.link(dve.tensor_copy(pos[:, :], hi_i[:, :]))
                step.link(dve.tensor_tensor(col[:, :], col[:, :], pos[:, :], ALU.add))
                def hot(c, b):
                    dve.wait_ge(s_hot_used, c + 1)
                    dve.tensor_scalar(lane_one[b][:, :], C.iota_b[:, :], lane[:, bass.ds(c, 1)], None,
                                      ALU.is_equal).then_inc(s_lane, 1)
                    dve.tensor_scalar(col_hot[b][:, :], C.iota_h[:, :], col[:, bass.ds(c, 1)], None,
                                      ALU.is_equal).then_inc(s_col, 1)

                dve.wait_ge(s_low, 1)
                for c in chunks(dve):
                    dve.wait_ge(s_x, 16 * c + 16)
                    wait_past(dve, s_xnst, 16 * c)
                    wait_past(dve, s_tr, 4 * c)
                    layer_norm_chunk(dve, s_ln, LN_STEPS * c, xc, xnc, stats, small)
                    for t in range(CH):
                        with dve.Fori(0, TAB // UNROLL) as g:
                            for b in range(UNROLL):
                                hot((CH * c + t) * TAB + UNROLL * g + b, b % HB)
                        dve.wait_ge(s_phi, CH * c + t + 1)
                        dve.tensor_tensor(p_out[t % 2][:, 1, :], pq[0][t % 2][:, :], p_out[t % 2][:, 0, :],
                                          ALU.subtract).then_inc(s_plo, 1)
                with dve.Fori(NT * TAB // UNROLL, EC // UNROLL) as g:
                    for b in range(UNROLL):
                        hot(UNROLL * g + b, b % HB)
                dve.wait_ge(s_table, 2)
                done = step
                done.link(dve.tensor_scalar(C.gidx[:, :], acc[0][:, 0:NCOL], float(NPAD // 2), None, ALU.add))
                done.link(dve.tensor_scalar(C.dloc[:, :], acc[1][:, 0:NCOL], -1.0, None, ALU.add))

            @block.tensor
            def _(pe):
                for k in range(2):
                    pe.wait_ge(s_cnt, k + 1)
                    pe.matmul(acc[0][:, 0:NT], C.before[:, :], cnt[:, :], start=True, stop=True)
                    pe.matmul(acc[1][:, 0:NT], C.ones[:, :], cnt[:, :], start=True, stop=True).then_inc(s_sum, 1)

                def place(c, b):
                    pe.wait_ge(s_col, c + 1)
                    pe.wait_ge(s_scaled, 2 * c + 2)
                    for k in range(2):
                        last = pe.matmul(acc[k][:, 0:NCOL], lane_hot[b][:, k, :], col_hot[b][:, :], start=False,
                                         stop=False)
                    last.then_inc(s_hot_used, 1)

                def edge_of_table(first):
                    for k in range(2):
                        last = pe.matmul(acc[k][:, 0:NCOL], C.zeros[:, :], C.zeros_w[:, :], start=first, stop=not first)
                    last.then_inc(s_table, 1)

                pe.wait_ge(s_bkt, 2)
                edge_of_table(True)
                pe.sem_inc(s_hot_used, HB)
                pe.wait_ge(s_w, 32)
                for c in chunks(pe):
                    for k in range(KD):
                        for h in range(2):
                            if k == 0 and h == 0:
                                pe.wait_ge(s_ln, LN_STEPS * c + LN_STEPS)
                            tiles = range(4) if h == 0 else range(4, CH)
                            wait_past(pe, s_xt, 4 * c + 2 * k + h - 1 if k else 4 * c)
                            for t in tiles:
                                last = pe.transpose(tr[h][:, (t % 4) * P:(t % 4 + 1) * P],
                                                    xnc[:, t, k * P:(k + 1) * P], C.ident[:, :])
                            last.then_inc(s_tr, 1)
                    pe.wait_ge(s_xt, 4 * c + 4)
                    for t in range(CH):
                        for h, freed in enumerate((s_plo, s_q)):
                            wait_past(pe, freed, CH * c + max(t - 1, 0))
                            for k in range(KD):
                                last = pe.matmul(pq[h][t % 2][:, :], xtc[:, k, t * P:(t + 1) * P], w_pq[:, h, k, :],
                                                 start=(k == 0), stop=(k == KD - 1))
                            last.then_inc(s_pq, 1)
                        with pe.Fori(0, TAB // UNROLL) as g:
                            for b in range(UNROLL):
                                place((CH * c + t) * TAB + UNROLL * g + b, b % HB)
                with pe.Fori(NT * TAB // UNROLL, EC // UNROLL) as g:
                    for b in range(UNROLL):
                        place(UNROLL * g + b, b % HB)
                edge_of_table(False)


def stage_edge_network(nc, C, A, S):
    with ExitStack() as ctx:
        m = Mem(nc, ctx)
        GB, TB = 4, 8
        G, T = 2 * GB, 2 * TB
        NI = NG // G
        assert NI * G == NG
        p_hl = m.sb("p_hl", [P, NT, 2, HID], F32R)
        with ExitStack() as early:
            w_c = Mem(nc, early).sb("w_c", [P, HID])
            w_ch = Mem(nc, early).sb("w_ch", [P, HID])
        h_hi, h_lo = ([m.sb(f"h_{n}{b}", [P, HID], F32R) for b in range(2)] for n in ("hi", "lo"))
        w_cat = m.sb("w_cat", [P, HID], F32R)
        rb = [m.sb(f"rb{b}", [P, GB, 2 * REC]) for b in range(2)]
        wide = [m.sb(f"wide{b}", [P, 2, P]) for b in range(2)]
        hot = [m.sb(f"hot{b}", [P, 2, P], F32R) for b in range(4)]
        trs = [m.sb(f"trs{b}", [P, 4, P], F32R) for b in range(2)]
        qg = [m.sb(f"qg{b}", [P, HID]) for b in range(TB)]
        hb = [m.sb(f"hb{b}", [P, HID]) for b in range(4)]
        p_tr = [m.ps(f"p_tr{b}", [P, 4, P]) for b in range(2)]
        p_h = [m.ps(f"p_h{b}", [P, HID]) for b in range(2)]
        p_sum = [m.ps(f"p_sum{b}", [P, HID]) for b in range(2)]
        deg_g = m.sb("deg_g", [P, G])

        s_p, s_w, s_rec = m.sem("e_p"), m.sem("e_w"), [m.sem(f"e_rec{b}") for b in range(2)]
        s_gath = [m.sem(f"e_gath{b}") for b in range(TB)]
        s_init, s_prep = m.sem("e_init"), m.sem("e_prep")
        s_wide, s_hot, s_tr, s_trs = m.sem("e_wide"), m.sem("e_hot"), m.sem("e_tr"), m.sem("e_trs")
        s_h, s_add, s_relu, s_low, s_sum, s_acc = (
            m.sem(n) for n in ("e_h", "e_add", "e_relu", "e_low", "e_sum", "e_acc"))
        recs_v = S.recs[0:NSLOT, :].rearrange("(g p j) w -> p g (j w)", p=P, j=2)

        def ahead(i, q, n):
            return (i, q + n) if q + n < G else (i + 1, q + n - G)

        def edges(i, step):
            step(0, True, False)
            with i.Fori(1, NI - 1) as it:
                step(it, False, False)
            step(NI - 1, False, True)

        with nc.Block() as block:
            @block.sync
            def _(sp):
                c0 = 2 * D
                sp.wait_ge(s_init, 3)
                for r in range(4):
                    sp.dma_start(w_c[16 * r:16 * r + 16, :], A.mW1[c0:c0 + EDGE_DIM, :]).then_inc(s_w, 16)
                for r in range(2):
                    sp.dma_start(w_c[64 + r:65 + r, :], A.mb1.rearrange("(a n) -> a n", a=1)).then_inc(s_w, 16)
                for n in range(2):
                    sp.dma_start(rb[n][:, :, :], recs_v[:, GB * n:GB * n + GB, :]).then_inc(s_rec[n], 16)
                for t in range(NT):
                    sp.dma_start(p_hl[:, t, :, :].rearrange("p h n -> p (h n)").bitcast(F32),
                                 S.p[t * P:(t + 1) * P, :]).then_inc(s_p, 16)
                with sp.Fori(1, NI) as i:
                    for b in range(2):
                        sp.wait_ge(s_add, T * i + TB * b - TB)
                        sp.dma_start(rb[b][:, :, :], recs_v[:, bass.ds(G * i + GB * b, GB), :]).then_inc(s_rec[b], 16)

            @block.gpsimd
            def _(pool):
                pool.memset(w_c[:, :], 0.0).then_inc(s_init, 1)
                pool.memset(C.agg[:, :, :], 0.0).then_inc(s_init, 1)
                pool.memset(C.deg_src[:, :], 0.0).then_inc(s_init, 1)
                for b in range(2):
                    pool.memset(wide[b][:, :, 64:66], 1.0).then_inc(s_init, 1)
                    pool.memset(wide[b][:, :, 66:P], 0.0).then_inc(s_init, 1)

                def gathers(i, first, last):
                    for b in range(2):
                        pool.wait_ge(s_rec[b], 16 * i + 16)
                        pool.nop(nofuse=True)
                        for r in range(TB):
                            if not (first and b == 0):
                                pool.wait_ge(s_add, T * i + TB * b - TB + r + 1)
                                pool.nop(nofuse=True)
                            at = (r % 2) * REC + 1
                            pool.indirect_dma_start(
                                qg[r][:, :], None, S.q[:, :],
                                bass.IndirectOffsetOnAxis(ap=rb[b][:, r // 2, at:at + 1].bitcast(U32), axis=0)
                            ).then_inc(s_gath[r], 16)

                edges(pool, gathers)

            @block.scalar
            def _(act):
                act.wait_ge(s_w, 96)
                act.activation(w_cat[:, :], w_c[:, :], ACT.Copy).then_inc(s_prep, 1)
                act.wait_ge(s_prep, 1)
                act.activation(w_ch[:, :], w_cat[:, :].bitcast(F32), ACT.Copy).then_inc(s_prep, 1)
                act.wait_ge(s_init, 7)

                def widen(i, q):
                    b = q // GB
                    act.wait_ge(s_rec[b], 16 * i + 16)
                    src = rb[b][:, q % GB, :].rearrange("p (j w) -> p j w", w=REC)[:, :, 2:REC]
                    for h in range(2):
                        act.activation(wide[q % 2][:, :, 32 * h:32 * h + 32], src, ACT.Copy).then_inc(s_wide, 1)

                def take(i, q):
                    act.wait_ge(s_tr, G * i + q + 1)
                    act.activation(trs[q % 2][:, 0:2, :], p_tr[q % 2][:, 0:2, :], ACT.Copy).then_inc(s_trs, 1)
                    act.activation(trs[q % 2][:, 2:4, :], p_tr[q % 2][:, 2:4, :], ACT.Copy,
                                   accum_out=deg_g[:, q:q + 1]).then_inc(s_trs, 1)

                def body(i, first, last):
                    if first:
                        widen(i, 0)
                        widen(i, 1)
                        take(i, 0)
                    for q in range(G):
                        if not (last and q >= G - 2):
                            widen(*ahead(i, q, 2))
                        if not (last and q == G - 1):
                            take(*ahead(i, q, 1))
                        for j in range(2):
                            t = 2 * q + j
                            act.wait_ge(s_add, T * i + t + 1)
                            dst = hb[t % 4] if j == 0 else h_hi[q % 2]
                            act.activation(dst[:, :], hb[t % 4][:, :], ACT.Relu).then_inc(s_relu, 1)

                edges(act, body)

            @block.vector
            def _(dve):
                dve.wait_ge(s_prep, 2)
                dve.tensor_tensor(w_cat[32:64, :], w_c[32:64, :], w_ch[32:64, :], ALU.subtract).then_inc(s_prep, 1)
                dve.tensor_tensor(w_cat[64:96, :], w_c[64:96, :], w_ch[64:96, :], ALU.subtract).then_inc(s_prep, 1)
                dve.wait_ge(s_prep, 4)
                dve.tensor_copy(w_cat[64:65, :], w_ch[64:65, :]).then_inc(s_prep, 1)

                def one_hot(i, q):
                    b = q // GB
                    dve.wait_ge(s_rec[b], 16 * i + 16)
                    for j in range(2):
                        dve.tensor_scalar(hot[q % 4][:, j, :], C.iota_f[:, :], rb[b][:, q % GB, j * REC:j * REC + 1],
                                          None, ALU.is_equal).then_inc(s_hot, 1)

                def accumulate(i, q, bucket):
                    dve.wait_ge(s_sum, G * i + q + 1)
                    wait_past(dve, s_acc, 2 * (G * i + q))
                    agg = C.agg[:, bass.ds(bucket, 1), :].rearrange("p a n -> p (a n)")
                    dve.tensor_tensor(agg, p_sum[q % 2][:, :], agg, ALU.add).then_inc(s_acc, 1)
                    deg = C.deg_src[:, bass.ds(bucket, 1)]
                    dve.tensor_tensor(deg, deg_g[:, q:q + 1], deg, ALU.add).then_inc(s_acc, 1)

                def low_part(i, q):
                    dve.wait_ge(s_relu, T * i + 2 * q + 2)
                    dve.scalar_tensor_tensor(out=h_lo[q % 2][:, :], in0=hb[(2 * q + 1) % 4][:, :], scalar=0.0,
                                             in1=h_hi[q % 2][:, :].bitcast(F32), op0=ALU.max,
                                             op1=ALU.subtract).then_inc(s_low, 1)

                def body(i, first, last):
                    if first:
                        dve.wait_ge(s_init, 7)
                        one_hot(i, 0)
                        one_hot(i, 1)
                        buckets = [None] + list(load_buckets(nc, dve, C.bucket[0:1, 0, 0:G]))
                    else:
                        buckets = load_buckets(nc, dve, C.bucket[0:1, 0, bass.ds(G * i - 1, G + 1)])
                    for q in range(G):
                        for j in range(2):
                            t = 2 * q + j
                            dve.wait_ge(s_h, T * i + t + 1)
                            dve.wait_ge(s_gath[t % TB], 16 * (2 * i + t // TB) + 16)
                            dve.tensor_tensor(hb[t % 4][:, :], p_h[t % 2][:, :], qg[t % TB][:, :],
                                              ALU.add).then_inc(s_add, 1)
                        if not (last and q >= G - 2):
                            one_hot(*ahead(i, q, 2))
                        low_part(i, q)
                        if q > 0:
                            accumulate(i, q - 1, buckets[q])
                        elif not first:
                            accumulate(i - 1, G - 1, buckets[0])
                    if last:
                        accumulate(i, G - 1, buckets[G])

                edges(dve, body)

            @block.tensor
            def _(pe):
                def transposes(i, q):
                    pe.wait_ge(s_wide, 2 * (G * i + q) + 2)
                    pe.wait_ge(s_hot, 2 * (G * i + q) + 2)
                    for j in range(2):
                        pe.transpose(p_tr[q % 2][:, j, :], wide[q % 2][:, j, :], C.ident[:, :])
                    for j in range(2):
                        last = pe.transpose(p_tr[q % 2][:, 2 + j, :], hot[q % 4][:, j, :].bitcast(F32), C.ident[:, :])
                    last.then_inc(s_tr, 1)

                def hidden(i, q, bucket, first):
                    pe.wait_ge(s_trs, 2 * (G * i + q) + 2)
                    for j in range(2):
                        t = 2 * q + j
                        if not (first and t < 2):
                            pe.wait_ge(s_add, T * i + t - 1)
                        for h in range(2):
                            pe.matmul(p_h[j][:, :], trs[q % 2][:, 2 + j, :],
                                      p_hl[:, bass.ds(bucket, 1), h, :].rearrange("p a n -> p (a n)"),
                                      start=(h == 0), stop=False)
                        pe.matmul(p_h[j][:, :], trs[q % 2][:, j, :], w_cat[:, :], start=False,
                                  stop=True).then_inc(s_h, 1)

                def sums(i, q, first):
                    if not (first and q < 2):
                        pe.wait_ge(s_acc, 2 * (G * i + q) - 2)
                    for j in range(2):
                        t = 2 * q + j
                        pe.wait_ge(s_relu, T * i + t + 1)
                        if j == 0:
                            pe.matmul(p_sum[q % 2][:, :], hot[q % 4][:, j, :].bitcast(F32), hb[t % 4][:, :],
                                      start=True, stop=False)
                        else:
                            pe.matmul(p_sum[q % 2][:, :], hot[q % 4][:, j, :], h_hi[q % 2][:, :],
                                      start=False, stop=False)
                            pe.wait_ge(s_low, G * i + q + 1)
                            pe.matmul(p_sum[q % 2][:, :], hot[q % 4][:, j, :], h_lo[q % 2][:, :],
                                      start=False, stop=True).then_inc(s_sum, 1)

                def body(i, first, last):
                    if first:
                        pe.wait_ge(s_p, 16 * NT)
                        pe.wait_ge(s_prep, 5)
                        transposes(i, 0)
                    buckets = load_buckets(nc, pe, C.bucket[0:1, 0, bass.ds(G * i, G)])
                    for q in range(G):
                        if not (last and q == G - 1):
                            transposes(*ahead(i, q, 1))
                        hidden(i, q, buckets[q], first)
                        if q > 0:
                            sums(i, q - 1, first)
                        elif not first:
                            sums(i - 1, G - 1, False)
                    if last:
                        sums(i, G - 1, False)

                edges(pe, body)


def load_buckets(nc, eng, ap):
    return nc.values_load_multi_w_load_instructions(ap, engines=[eng.engine], min_val=0, max_val=NT - 1)[1]


class Banks:

    def __init__(self, m, name, n, per):
        self.banks = [m.ps(f"{name}{b}", [P, HID]) for b in range(n)]
        self.full, self.empty, self.per = m.sem(f"{name}_full"), m.sem(f"{name}_empty"), per

    def to_fill(self, pe, c, g):
        n = len(self.banks)
        wait_past(pe, self.empty, self.per * c + (g - n + 1 if g >= n else 0))
        return self.banks[g % n]

    def to_take(self, eng, c, g):
        eng.wait_ge(self.full, self.per * c + g + 1)
        return self.banks[g % len(self.banks)]


HALVES = ((0, 3), (3, CH))


def transpose_chunk(pe, c, src, tr, ident, full, empty, blocks=KD):
    for k in range(blocks):
        for h, (a, b) in enumerate(HALVES):
            wait_past(pe, empty, 2 * blocks * c + (2 * k + h - 1 if k else 0))
            for t in range(a, b):
                last = pe.transpose(tr[h][:, (t - a) * P:(t - a + 1) * P], src[:, t, k * P:(k + 1) * P], ident)
            last.then_inc(full, 1)


def take_transposed(act, c, dst, tr, full, empty, blocks=KD):
    for k in range(blocks):
        for h, (a, b) in enumerate(HALVES):
            act.wait_ge(full, 2 * blocks * c + 2 * k + h + 1)
            act.activation(dst[:, k, a * P:b * P], tr[h][:, 0:(b - a) * P], ACT.Copy).then_inc(empty, 1)


def chunk(ap, c):
    return ap.rearrange("(t p) d -> p t d", p=P)[:, bass.ds(c * CH, CH), :]


def rows_on_partitions(w, p=P):
    return w.rearrange("(k p) n -> p k n", p=p)


def on_all(v):
    return v.rearrange("(a n) -> a n", a=1).to_broadcast([P, v.shape[0]])


def by_feature(v):
    return v.rearrange("(k p) -> p k", p=P)


def stage_update(nc, C, A, S):
    with ExitStack() as ctx:
        m = Mem(nc, ctx)
        w2 = m.sb("w2", [P, KH, D])
        b2 = m.sb("b2", [P, D])
        deg = m.sb("deg", [P, NPAD])
        u1 = m.sb("u1", [P, KH, HID])
        u1b = m.sb("u1b", [P, KH])
        u2 = m.sb("u2", [P, KH, D])
        u2b = m.sb("u2b", [P, 1, D])
        xT = m.sb("xT", [P, KD, CH * P])
        x, xn, r = m.sb("x", [P, CH, D]), m.sb("xn", [P, CH, D]), m.sb("r", [P, CH, D])
        msgT = m.sb("msgT", [P, KD, CH * P])
        uT = m.sb("uT", [P, KH, CH * P])
        x1, xn1 = m.sb("x1", [P, CH, D]), m.sb("xn1", [P, CH, D])
        stats, small = m.sb("stats2", [P, CH, 6]), m.sb("small2", [P, 5, CH])
        NA, NV = 2 * KD + 2 * KH, CH
        aggT = m.sb("aggT", [P, KH, CH * P])
        agg = m.sb("agg_c", [P, CH, HID])
        s_agg = m.sem("u_agg")
        tr = [m.ps(f"u_tr{b}", [P, HID]) for b in range(2)]
        hidden, out = Banks(m, "u_h", 4, NA), Banks(m, "u_o", 2, NV)
        s_trf, s_tre = m.sem("u_trf"), m.sem("u_tre")
        s_w, s_zero, s_deg, s_degrow = m.sem("u_w"), m.sem("u_zero"), m.sem("u_deg"), m.sem("u_degrow")
        s_xT, s_x, s_r, s_ln = m.sem("u_xT"), m.sem("u_x"), m.sem("u_r"), m.sem("u_ln")
        s_st = m.sem("u_st")

        with nc.Block() as block:
            @block.sync
            def _(sp):
                sp.dma_start(S.deg.rearrange("(t p) -> p t", p=P), C.deg_src[:, :],
                             allow_slow_non_contiguous=True).then_inc(s_deg, 16)
                sp.dma_start(w2[:, :, :], rows_on_partitions(A.mW2)).then_inc(s_w, 16)
                sp.dma_start(u1[:, :, :], rows_on_partitions(A.uW1)).then_inc(s_w, 16)
                sp.dma_start(u2[:, :, :], rows_on_partitions(A.uW2)).then_inc(s_w, 16)
                sp.dma_start(u1b[:, :], by_feature(A.ub1), allow_slow_non_contiguous=True).then_inc(s_w, 16)
                sp.dma_start(u2b[:, 0, :], on_all(A.ub2)).then_inc(s_w, 16)
                sp.wait_ge(s_zero, 2)
                sp.wait_ge(s_deg, 16)
                sp.dma_start(b2[0:1, :], A.mb2.rearrange("(a n) -> a n", a=1)).then_inc(s_w, 16)
                sp.dma_start(deg[0:1, :], S.deg.rearrange("(a n) -> a n", a=1)).then_inc(s_w, 16)

                def load(c):
                    wait_past(sp, s_trf, 2 * KH * c)
                    sp.dma_start(agg[:, :, :], C.agg[:, bass.ds(c * CH, CH), :]).then_inc(s_agg, 16)
                    wait_past(sp, s_r, 2 * c)
                    sp.dma_start(x[:, :, :], chunk(A.x, c)).then_inc(s_x, 16)
                    sp.dma_start(xn[:, :, :], chunk(S.xn, c)).then_inc(s_x, 16)
                    wait_past(sp, hidden.full, NA * c)
                    sp.dma_start(xT[:, :, :], S.xnT.rearrange("(k p) n -> p k n", p=P)[:, :, bass.ds(c * CH * P, CH * P)]
                                 ).then_inc(s_xT, 16)

                def store(c):
                    sp.wait_ge(s_ln, LN_STEPS * c + LN_STEPS)
                    sp.dma_start(chunk(S.x1, c), x1[:, :, :]).then_inc(s_st, 16)
                    sp.dma_start(chunk(S.xn1, c), xn1[:, :, :]).then_inc(s_st, 16)

                load_ahead(sp, load, store)
                sp.wait_ge(s_st, 32 * NCH)

            @block.gpsimd
            def _(pool):
                pool.memset(b2[:, :], 0.0).then_inc(s_zero, 1)
                pool.memset(deg[:, :], 0.0).then_inc(s_zero, 1)
                pool.wait_ge(s_w, 112)
                for c in chunks(pool):
                    pool.wait_ge(s_x, 32 * c + 32)
                    wait_past(pool, out.empty, NV * c)
                    pool.tensor_tensor(r[:, :, :], x[:, :, :], xn[:, :, :], ALU.add).then_inc(s_r, 1)
                    pool.wait_ge(s_r, 2 * c + 1)
                    pool.tensor_tensor(r[:, :, :], r[:, :, :], u2b[:, :, :].to_broadcast([P, CH, D]),
                                       ALU.add).then_inc(s_r, 1)

            @block.scalar
            def _(act):
                act.wait_ge(s_w, 112)
                for c in chunks(act):
                    take_transposed(act, c, aggT, tr, s_trf, s_tre, KH)
                    for k in range(KD):
                        for h, (a, b) in enumerate(HALVES):
                            g = 2 * k + h
                            src = hidden.to_take(act, c, g)
                            act.activation(msgT[:, k, a * P:b * P], src[:, 0:(b - a) * P], ACT.Copy).then_inc(hidden.empty, 1)
                    for k in range(KH):
                        for h, (a, b) in enumerate(HALVES):
                            g = 2 * KD + 2 * k + h
                            src = hidden.to_take(act, c, g)
                            act.activation(uT[:, k, a * P:b * P], src[:, 0:(b - a) * P], ACT.Relu,
                                           bias=u1b[:, k:k + 1]).then_inc(hidden.empty, 1)

            @block.vector
            def _(dve):
                for c in chunks(dve):
                    dve.wait_ge(s_r, 2 * c + 2)
                    wait_past(dve, s_st, 32 * c)
                    for t in range(CH):
                        src = out.to_take(dve, c, t)
                        dve.tensor_tensor(x1[:, t, :], src[:, 0:D], r[:, t, :], ALU.add).then_inc(out.empty, 1)
                    dve.wait_ge(out.empty, NV * c + NV)
                    layer_norm_chunk(dve, s_ln, LN_STEPS * c, x1, xn1, stats, small)

            @block.tensor
            def _(pe):
                pe.wait_ge(s_w, 112)
                for c in chunks(pe):
                    pe.wait_ge(s_agg, 16 * c + 16)
                    transpose_chunk(pe, c, agg, tr, C.ident[:, :], s_trf, s_tre, KH)
                    pe.wait_ge(s_tre, 2 * KH * (c + 1))
                    for k in range(KD):
                        for h, (a, b) in enumerate(HALVES):
                            dst = hidden.to_fill(pe, c, 2 * k + h)[:, 0:(b - a) * P]
                            for j in range(KH):
                                pe.matmul(dst, w2[:, j, k * P:(k + 1) * P], aggT[:, j, a * P:b * P],
                                          start=(j == 0), stop=False)
                            pe.matmul(dst, b2[:, k * P:(k + 1) * P], deg[:, bass.ds((c * CH + a) * P, (b - a) * P)],
                                      start=False, stop=True).then_inc(hidden.full, 1)
                    pe.wait_ge(s_xT, 16 * c + 16)
                    for k in range(KH):
                        for h, (a, b) in enumerate(HALVES):
                            dst = hidden.to_fill(pe, c, 2 * KD + 2 * k + h)[:, 0:(b - a) * P]
                            for j in range(KD):
                                pe.matmul(dst, u1[:, j, k * P:(k + 1) * P], xT[:, j, a * P:b * P], start=(j == 0), stop=False)
                            if k == 0:
                                pe.wait_ge(hidden.empty, NA * c + 2 * KD)
                            for j in range(KD):
                                last = pe.matmul(dst, u1[:, KD + j, k * P:(k + 1) * P], msgT[:, j, a * P:b * P],
                                                 start=False, stop=(j == KD - 1))
                            last.then_inc(hidden.full, 1)
                    pe.wait_ge(hidden.empty, NA * c + NA)
                    for t in range(CH):
                        dst = out.to_fill(pe, c, t)[:, 0:D]
                        for j in range(KH):
                            last = pe.matmul(dst, uT[:, j, t * P:(t + 1) * P], u2[:, j, :], start=(j == 0), stop=(j == KH - 1))
                        last.then_inc(out.full, 1)
        m.clear_sems()


def stage_experts(nc, C, A, S):
    NE, EH1, EH2 = A.eW1.shape[0], A.eW1.shape[2], A.eW2.shape[2]
    SH1, SH2 = A.sW1.shape[1], A.sW2.shape[1]
    KS = SH1 // P
    assert EH1 == P and SH2 == P and EH2 < P
    with ExitStack() as ctx:
        m = Mem(nc, ctx)
        w_s1, w_s2, w_s3 = m.sb("w_s1", [P, KD, SH1]), m.sb("w_s2", [P, KS, SH2]), m.sb("w_s3", [P, D])
        b_s1, b_s2, b_s3 = m.sb("b_s1", [P, KS]), m.sb("b_s2", [P, 1]), m.sb("b_s3", [P, 1, D])
        w_e1, w_e2 = m.sb("w_e1", [P, NE, KD, EH1]), m.sb("w_e2", [P, NE, EH2])
        w_e3 = m.sb("w_e3", [P, NE, D])
        b_e1, b_e2 = m.sb("b_e1", [P, NE]), m.sb("b_e2", [EH2, NE])
        w_g, b_g = m.sb("w_g", [P, KD, NE]), m.sb("b_g", [P, 1, NE])
        prio_i, prio = m.sb("prio_i", [P, 1, NE], I32), m.sb("prio", [P, 1, NE])
        x1, xn1, r, x2, xn2 = (m.sb(f"m_{n}", [P, CH, D]) for n in ("x1", "xn1", "r", "x2", "xn2"))
        xT = m.sb("m_xT", [P, KD, CH * P])
        h1, h2 = m.sb("h1", [P, KS, CH * P]), m.sb("h2", [P, CH * P])
        e1, e2 = m.sb("e1", [P, NE, CH * P]), m.sb("e2", [P, NE, CH * P])
        lg, ex, gt, key, first, second = (m.sb(f"g_{n}", [P, CH, NE]) for n in ("lg", "ex", "gt", "key", "first", "second"))
        c1, c2, c3, c4, c5, c6 = (m.sb(f"g_c{n}", [P, CH, 1]) for n in range(6))
        stats, small = m.sb("stats3", [P, CH, 6]), m.sb("small3", [P, 5, CH])
        NA, NV = 2 * (KS + 1 + 2 * NE), 1 + 3 * CH
        tr = [m.ps(f"m_tr{b}", [P, HID]) for b in range(2)]
        hidden, out = Banks(m, "m_h", 3, NA), Banks(m, "m_o", 3, NV)
        s_w, s_zero, s_x, s_trf, s_tre = (m.sem(f"m_{n}") for n in ("w", "zero", "x", "trf", "tre"))
        s_r, s_ln, s_st = (m.sem(f"m_{n}") for n in ("r", "ln", "st"))
        s_g, s_lg, s_ex, s_mix, s_prio = (m.sem(f"m_{n}") for n in ("g", "lg", "ex", "mix", "prio"))
        A_GROUPS = [("s1", k) for k in range(KS)] + [("e1", e) for e in range(NE)] + [("s2", 0)] + \
                   [("e2", e) for e in range(NE)]
        GSTEPS, MIX = 23, 5 * CH

        with nc.Block() as block:
            @block.sync
            def _(sp):
                sp.wait_ge(s_zero, 2)
                for dst, src in ((w_s1[:, :, :], rows_on_partitions(A.sW1)), (w_s2[:, :, :], rows_on_partitions(A.sW2)),
                                 (w_s3[:, :], A.sW3), (b_s1[:, :], by_feature(A.sb1)), (b_s2[:, :], by_feature(A.sb2)),
                                 (b_s3[:, 0, :], on_all(A.sb3)), (w_e2[:, :, :], A.eW2.rearrange("e p n -> p e n")),
                                 (w_e3[0:EH2, :, :], A.eW3.rearrange("e p n -> p e n")),
                                 (w_e3[EH2:EH2 + 1, :, :], A.eb3.rearrange("(a e) n -> a e n", a=1)),
                                 (b_e1[:, :], A.eb1.rearrange("e p -> p e")), (b_e2[:, :], A.eb2.rearrange("e p -> p e")),
                                 (w_g[:, :, :], rows_on_partitions(A.gW)), (b_g[:, 0, :], on_all(A.gb))):
                    sp.dma_start(dst, src, allow_slow_non_contiguous=True).then_inc(s_w, 16)
                for e in range(NE):
                    sp.dma_start(w_e1[:, e, :, :], rows_on_partitions(A.eW1[e])).then_inc(s_w, 16)

                def load(c):
                    wait_past(sp, s_trf, 4 * c)
                    wait_past(sp, s_r, c)
                    sp.dma_start(xn1[:, :, :], chunk(S.xn1, c)).then_inc(s_x, 16)
                    sp.dma_start(x1[:, :, :], chunk(S.x1, c)).then_inc(s_x, 16)

                def store(c):
                    sp.wait_ge(s_ln, LN_STEPS * c + LN_STEPS)
                    sp.dma_start(chunk(S.x2, c), x2[:, :, :]).then_inc(s_st, 16)
                    sp.dma_start(chunk(S.xn2, c), xn2[:, :, :]).then_inc(s_st, 16)

                load_ahead(sp, load, store)
                sp.wait_ge(s_st, 32 * NCH)

            @block.gpsimd
            def _(pool):
                pool.memset(w_e3[64:P, :, :], 0.0).then_inc(s_zero, 1)
                pool.memset(e2[64:P, :, :], 0.0).then_inc(s_zero, 1)
                pool.wait_ge(s_zero, 2)
                pool.memset(e2[EH2:EH2 + 1, :, :], 1.0).then_inc(s_zero, 1)
                pool.wait_ge(s_zero, 3)
                pool.iota(prio_i[:, :, :], [[-1, NE]], base=NE, channel_multiplier=0).then_inc(s_prio, 1)
                pool.wait_ge(s_w, 16 * (13 + NE))
                for c in chunks(pool):
                    pool.wait_ge(s_x, 32 * c + 32)
                    wait_past(pool, out.empty, NV * c)
                    pool.tensor_tensor(r[:, :, :], x1[:, :, :], b_s3[:, :, :].to_broadcast([P, CH, D]),
                                       ALU.add).then_inc(s_r, 1)

            @block.scalar
            def _(act):
                act.wait_ge(s_w, 16 * (13 + NE))
                act.wait_ge(s_zero, 3)
                for c in chunks(act):
                    take_transposed(act, c, xT, tr, s_trf, s_tre)
                    act.wait_ge(s_lg, 2 * c + 1)
                    act.activation(ex[:, :, :], lg[:, :, :], ACT.Exp).then_inc(s_ex, 1)
                    act.wait_ge(s_lg, 2 * c + 2)
                    act.activation(c4[:, :, :], c3[:, :, :], ACT.Exp).then_inc(s_ex, 1)
                    for n, (kind, k) in enumerate(A_GROUPS):
                        dst, bias = {"s1": (h1[:, k % KS, :], b_s1[:, k % KS:k % KS + 1]), "s2": (h2[:, :], b_s2[:, 0:1]),
                                     "e1": (e1[:, k % NE, :], b_e1[:, k % NE:k % NE + 1]),
                                     "e2": (e2[0:EH2, k % NE, :], b_e2[:, k % NE:k % NE + 1])}[kind]
                        for h, (a, b) in enumerate(HALVES):
                            src = hidden.to_take(act, c, 2 * n + h)
                            act.activation(dst[:, a * P:b * P], src[0:dst.shape[0], 0:(b - a) * P], ACT.Relu,
                                           bias=bias).then_inc(hidden.empty, 1)

            @block.vector
            def _(dve):
                dve.wait_ge(s_prio, 1)
                dve.tensor_copy(prio[:, :, :], prio_i[:, :, :]).then_inc(s_prio, 1)
                dve.wait_ge(s_w, 16 * (13 + NE))
                wide = [P, CH, NE]

                def gates(c):
                    n = [0]

                    def step(ins):
                        ins.then_inc(s_g, 1)
                        n[0] += 1
                        dve.wait_ge(s_g, GSTEPS * c + n[0])

                    def pick(values, top, hit):
                        step(dve.tensor_reduce(top[:, :, 0], values[:, :, :], AX.X, ALU.max))
                        step(dve.tensor_tensor(key[:, :, :], values[:, :, :], top[:, :, :].to_broadcast(wide), ALU.is_equal))
                        step(dve.tensor_tensor(key[:, :, :], key[:, :, :], prio[:, :, :].to_broadcast(wide), ALU.mult))
                        step(dve.tensor_reduce(c6[:, :, 0], key[:, :, :], AX.X, ALU.max))
                        step(dve.tensor_tensor(hit[:, :, :], key[:, :, :], c6[:, :, :].to_broadcast(wide), ALU.is_equal))

                    logits = out.to_take(dve, c, 0)[:, 0:CH * NE].rearrange("p (t e) -> p t e", e=NE)
                    ins = dve.tensor_tensor(lg[:, :, :], logits, b_g[:, :, :].to_broadcast(wide), ALU.add)
                    step(ins)
                    dve.sem_inc(out.empty, 1)
                    step(dve.tensor_reduce(c1[:, :, 0], lg[:, :, :], AX.X, ALU.max))
                    dve.tensor_tensor(lg[:, :, :], lg[:, :, :], c1[:, :, :].to_broadcast(wide), ALU.subtract).then_inc(s_lg, 1)
                    dve.wait_ge(s_ex, 2 * c + 1)
                    step(dve.tensor_reduce(c1[:, :, 0], ex[:, :, :], AX.X, ALU.add))
                    step(dve.reciprocal(c2[:, :, :], c1[:, :, :]))
                    step(dve.tensor_tensor(gt[:, :, :], ex[:, :, :], c2[:, :, :].to_broadcast(wide), ALU.mult))
                    pick(gt, c1, first)
                    step(dve.scalar_tensor_tensor(out=gt[:, :, :], in0=first[:, :, :], scalar=-2.0, in1=gt[:, :, :],
                                                  op0=ALU.mult, op1=ALU.add))
                    pick(gt, c2, second)
                    dve.tensor_tensor(c3[:, :, :], c2[:, :, :], c1[:, :, :], ALU.subtract).then_inc(s_lg, 1)
                    dve.wait_ge(s_ex, 2 * c + 2)
                    step(dve.tensor_scalar(c1[:, :, :], c4[:, :, :], 1.0, None, ALU.add))
                    step(dve.reciprocal(c5[:, :, :], c1[:, :, :]))
                    step(dve.tensor_tensor(c4[:, :, :], c4[:, :, :], c5[:, :, :], ALU.mult))
                    step(dve.tensor_tensor(first[:, :, :], first[:, :, :], c5[:, :, :].to_broadcast(wide), ALU.mult))
                    step(dve.tensor_tensor(second[:, :, :], second[:, :, :], c4[:, :, :].to_broadcast(wide), ALU.mult))
                    step(dve.tensor_tensor(gt[:, :, :], first[:, :, :], second[:, :, :], ALU.add))
                    step(dve.tensor_copy(key[:, :, :], gt[:, :, :]))
                    assert n[0] == GSTEPS, n[0]

                for c in chunks(dve):
                    dve.wait_ge(s_prio, 2)
                    gates(c)
                    dve.wait_ge(s_r, c + 1)
                    wait_past(dve, s_st, 32 * c)
                    for t in range(CH):
                        for n in range(3):
                            src = out.to_take(dve, c, 1 + 3 * t + n)
                            for j in range(2 if n < 2 else 1):
                                term = 2 * n + j
                                if term == 0:
                                    ins = dve.tensor_tensor(x2[:, t, :], src[:, 0:D], r[:, t, :], ALU.add)
                                else:
                                    dve.wait_ge(s_mix, MIX * c + 5 * t + term)
                                    ins = dve.scalar_tensor_tensor(out=x2[:, t, :], in0=src[:, j * D:(j + 1) * D],
                                                                   scalar=gt[:, t, term - 1:term], in1=x2[:, t, :],
                                                                   op0=ALU.mult, op1=ALU.add)
                                ins.then_inc(s_mix, 1)
                            dve.wait_ge(s_mix, MIX * c + 5 * t + min(2 * n + 2, 5))
                            dve.sem_inc(out.empty, 1)
                    layer_norm_chunk(dve, s_ln, LN_STEPS * c, x2, xn2, stats, small)

            @block.tensor
            def _(pe):
                pe.wait_ge(s_w, 16 * (13 + NE))
                for c in chunks(pe):
                    pe.wait_ge(s_x, 32 * c + 32)
                    transpose_chunk(pe, c, xn1, tr, C.ident[:, :], s_trf, s_tre)
                    pe.wait_ge(s_tre, 4 * c + 4)
                    dst = out.to_fill(pe, c, 0)
                    for t in range(CH):
                        for j in range(KD):
                            last = pe.matmul(dst[:, t * NE:(t + 1) * NE], xT[:, j, t * P:(t + 1) * P], w_g[:, j, :],
                                             start=(t == 0 and j == 0), stop=(j == KD - 1), skip_group_check=True)
                    last.then_inc(out.full, 1)
                    for n, (kind, k) in enumerate(A_GROUPS):
                        rows = EH2 if kind == "e2" else P
                        if kind == "s2":
                            pe.wait_ge(hidden.empty, NA * c + 2 * KS)
                        if kind == "e2":
                            pe.wait_ge(hidden.empty, NA * c + 2 * (KS + k + 1))
                        for h, (a, b) in enumerate(HALVES):
                            dst = hidden.to_fill(pe, c, 2 * n + h)[0:rows, 0:(b - a) * P]
                            if kind == "s1":
                                terms = [(w_s1[:, j, k * P:(k + 1) * P], xT[:, j, a * P:b * P]) for j in range(KD)]
                            elif kind == "e1":
                                terms = [(w_e1[:, k, j, :], xT[:, j, a * P:b * P]) for j in range(KD)]
                            elif kind == "s2":
                                terms = [(w_s2[:, j, :], h1[:, j, a * P:b * P]) for j in range(KS)]
                            else:
                                terms = [(w_e2[:, k, :], e1[:, k, a * P:b * P])]
                            for j, (w, v) in enumerate(terms):
                                last = pe.matmul(dst, w, v, start=(j == 0), stop=(j == len(terms) - 1))
                            last.then_inc(hidden.full, 1)
                    pe.wait_ge(hidden.empty, NA * c + NA)
                    for t in range(CH):
                        for n in range(3):
                            dst = out.to_fill(pe, c, 1 + 3 * t + n)
                            for j in range(2 if n < 2 else 1):
                                term = 2 * n + j
                                v, w = (h2[:, t * P:(t + 1) * P], w_s3[:, :]) if term == 0 else \
                                    (e2[:, term - 1, t * P:(t + 1) * P], w_e3[:, term - 1, :])
                                last = pe.matmul(dst[:, j * D:(j + 1) * D], v, w, start=(j == 0), stop=True,
                                                 skip_group_check=True)
                            last.then_inc(out.full, 1)

        m.clear_sems()


def stage_project(nc, C, A, S, layer):
    W_l = A.W_l1 if layer == 0 else A.W_l2
    with ExitStack() as ctx:
        m = Mem(nc, ctx, f"project{layer}_")
        w_l, b_r = m.sb("w_l", [P, KD, D]), m.sb("b_r", [P, 1, D])
        x, y = m.sb("x", [P, CH, D]), m.sb("y", [P, CH, D])
        h, rdeg = m.sb("h", [P, CH, D]), m.sb("rdeg", [P, CH, 1])
        xT = m.sb("xT", [P, KD, CH * P])
        tr = [m.ps(f"tr{b}", [P, HID]) for b in range(2)]
        out = Banks(m, "o", 4, CH)
        s_w, s_x, s_trf, s_tre, s_h, s_y_st, s_xT_st = (
            m.sem(n) for n in ("w", "x", "trf", "tre", "h", "y_st", "xT_st"))
        HSTEPS = 3 + CH
        X = 16 if layer == 0 else 1

        with nc.Block() as block:
            @block.sync
            def _(sp):
                sp.dma_start(w_l[:, :, :], rows_on_partitions(W_l)).then_inc(s_w, 16)
                sp.dma_start(b_r[:, 0, :], on_all(A.b1)).then_inc(s_w, 16)

                def load(c):
                    if layer == 0:
                        wait_past(sp, s_trf, 4 * c)
                        sp.dma_start(x[:, :, :], chunk(S.xn2, c)).then_inc(s_x, 16)

                def store(c):
                    sp.wait_ge(s_tre, 4 * c + 4)
                    sp.dma_start(S.xT.rearrange("(k p) n -> p k n", p=P)[:, :, bass.ds(c * CH * P, CH * P)],
                                 xT[:, :, :]).then_inc(s_xT_st, 16)
                    sp.wait_ge(out.empty, CH * c + CH)
                    sp.dma_start(chunk(S.y, c), y[:, :, :]).then_inc(s_y_st, 16)

                load_ahead(sp, load, store)
                sp.wait_ge(s_xT_st, 16 * NCH)
                sp.wait_ge(s_y_st, 16 * NCH)

            @block.scalar
            def _(act):
                for c in chunks(act):
                    if layer == 1:
                        act.wait_ge(s_h, HSTEPS * c + HSTEPS)
                        wait_past(act, s_trf, 4 * c)
                        act.activation(x[:, :, :], h[:, :, :], ACT.Relu).then_inc(s_x, 1)
                    wait_past(act, out.full, CH * c)
                    wait_past(act, s_xT_st, 16 * c)
                    take_transposed(act, c, xT, tr, s_trf, s_tre)

            @block.vector
            def _(dve):
                def second_rows(c):
                    at = HSTEPS * c
                    dve.tensor_scalar(rdeg[:, :, :], C.nbr[:, bass.ds(c * CH, CH), D:D + 1], 1.0, None,
                                      ALU.max).then_inc(s_h, 1)
                    dve.wait_ge(s_h, at + 1)
                    dve.reciprocal(rdeg[:, :, :], rdeg[:, :, :]).then_inc(s_h, 1)
                    dve.wait_ge(s_h, at + 2)
                    wait_past(dve, s_x, c)
                    for t in range(CH):
                        tile = bass.ds(c * CH + t, 1)
                        dve.scalar_tensor_tensor(out=h[:, t, :], in0=C.nbr[:, tile, 0:D].rearrange("p a n -> p (a n)"),
                                                 scalar=rdeg[:, t, :], in1=C.z[:, tile, :].rearrange("p a n -> p (a n)"),
                                                 op0=ALU.mult, op1=ALU.add).then_inc(s_h, 1)
                    dve.wait_ge(s_h, at + 2 + CH)
                    dve.tensor_tensor(h[:, :, :], h[:, :, :], b_r[:, :, :].to_broadcast([P, CH, D]), ALU.add).then_inc(s_h, 1)

                def products(c):
                    wait_past(dve, s_y_st, 16 * c)
                    for t in range(CH):
                        src = out.to_take(dve, c, t)
                        dve.tensor_copy(y[:, t, :], src[:, 0:D]).then_inc(out.empty, 1)

                dve.wait_ge(s_w, 32)
                if layer == 0:
                    for c in chunks(dve):
                        products(c)
                else:
                    second_rows(0)
                    second_rows(1)
                    products(0)
                    with dve.Fori(1, NCH - 1) as c:
                        second_rows(c + 1)
                        products(c)
                    products(NCH - 1)

            @block.tensor
            def _(pe):
                pe.wait_ge(s_w, 32)
                for c in chunks(pe):
                    pe.wait_ge(s_x, X * c + X)
                    transpose_chunk(pe, c, x, tr, C.ident[:, :], s_trf, s_tre)
                    pe.wait_ge(s_tre, 4 * c + 4)
                    for t in range(CH):
                        dst = out.to_fill(pe, c, t)
                        for k in range(KD):
                            last = pe.matmul(dst[:, 0:D], xT[:, k, t * P:(t + 1) * P], w_l[:, k, :], start=(k == 0),
                                             stop=(k == KD - 1))
                        last.then_inc(out.full, 1)
        m.clear_sems()


def stage_neighbours(nc, C, A, S, layer):
    W_r = A.W_r1 if layer == 0 else A.W_r2
    with ExitStack() as ctx:
        m = Mem(nc, ctx, f"nbr{layer}_")
        TB, GB = 8, 4
        T, G = 2 * TB, 2 * GB
        NI = NG // G
        assert NT + 1 < NI - 1
        W = D + 2
        idx = [m.sb(f"idx{b}", [P, TB], U32) for b in range(2)]
        yg = [m.sb(f"yg{b}", [P, W]) for b in range(TB)]
        hot = [m.sb(f"hot{b}", [P, 2, P]) for b in range(4)]
        w_r, xT = m.sb("w_r", [P, KD, D]), m.sb("xT", [P, KD, P])
        p_sum = [m.ps(f"sum{b}", [P, HID]) for b in range(2)]
        p_z = m.ps("z", [P, HID])
        s_zero, s_idx, s_hot, s_sum, s_acc = (m.sem(n) for n in ("zero", "idx", "hot", "sum", "acc"))
        s_w, s_xT, s_z, s_z_taken = (m.sem(n) for n in ("w", "xT", "z", "z_taken"))
        s_gath = [m.sem(f"gath{b}") for b in range(TB)]

        def ahead(i, q, n):
            return (i, q + n) if q + n < G else (i + 1, q + n - G)

        def bodies(eng, step):
            step(0, True, False, None)
            with eng.Fori(1, NT + 1) as it:
                step(it, False, False, it - 1)
            with eng.Fori(NT + 1, NI - 1) as it:
                step(it, False, False, None)
            step(NI - 1, False, True, None)

        with nc.Block() as block:
            @block.sync
            def _(sp):
                sp.dma_start(w_r[:, :, :], rows_on_partitions(W_r)).then_inc(s_w, 16)
                xT_v = S.xT.rearrange("(k p) n -> p k n", p=P)
                sp.dma_start(xT[:, :, :], xT_v[:, :, 0:P]).then_inc(s_xT, 16)
                with sp.Fori(1, NT) as t:
                    sp.wait_ge(s_z, t)
                    sp.dma_start(xT[:, :, :], xT_v[:, :, bass.ds(t * P, P)]).then_inc(s_xT, 16)

            @block.gpsimd
            def _(pool):
                for b in range(TB):
                    pool.memset(yg[b][:, D:W], 1.0).then_inc(s_zero, 1)
                pool.memset(C.nbr[:, :, :], 0.0).then_inc(s_zero, 1)

                def gathers(i, first, last, tile):
                    for b in range(2):
                        pool.wait_ge(s_idx, 2 * i + b + 1)
                        pool.nop(nofuse=True)
                        for r in range(TB):
                            if not (first and b == 0) and r % 2 == 0:
                                pool.wait_ge(s_sum, G * i + GB * b - GB + r // 2 + 1)
                                pool.nop(nofuse=True)
                            pool.indirect_dma_start(yg[r][:, 0:D], None, S.y[:, :],
                                                    bass.IndirectOffsetOnAxis(ap=idx[b][:, r:r + 1], axis=0)
                                                    ).then_inc(s_gath[r], 16)

                bodies(pool, gathers)

            @block.scalar
            def _(act):
                act.sem_inc(s_z_taken, 1)

                def body(i, first, last, tile):
                    for b in range(2):
                        if not first:
                            act.wait_ge(s_sum, G * i + GB * b - GB)
                        act.activation(idx[b][:, :].bitcast(F32), C.gidx[:, bass.ds(T * i + TB * b, TB)].bitcast(F32),
                                       ACT.Copy).then_inc(s_idx, 1)
                    if tile is not None:
                        act.wait_ge(s_z, i)
                        act.activation(C.z[:, bass.ds(tile, 1), :].rearrange("p a n -> p (a n)"), p_z[:, 0:D],
                                       ACT.Copy).then_inc(s_z_taken, 1)

                bodies(act, body)

            @block.vector
            def _(dve):
                def one_hot(i, q):
                    for j in range(2):
                        dve.tensor_scalar(hot[q % 4][:, j, :], C.iota_f[:, :],
                                          C.dloc[:, bass.ds(T * i + 2 * q + j, 1)], None, ALU.is_equal).then_inc(s_hot, 1)

                def accumulate(i, q, bucket):
                    dve.wait_ge(s_sum, G * i + q + 1)
                    wait_past(dve, s_acc, G * i + q)
                    nbr = C.nbr[:, bass.ds(bucket, 1), :].rearrange("p a n -> p (a n)")
                    dve.tensor_tensor(nbr, p_sum[q % 2][:, 0:W], nbr, ALU.add).then_inc(s_acc, 1)

                def body(i, first, last, tile):
                    if first:
                        dve.wait_ge(s_zero, TB + 1)
                        one_hot(i, 0)
                        one_hot(i, 1)
                        buckets = [None] + list(load_buckets(nc, dve, C.bucket[0:1, 1, 0:G]))
                    else:
                        buckets = load_buckets(nc, dve, C.bucket[0:1, 1, bass.ds(G * i - 1, G + 1)])
                    for q in range(G):
                        if q > 0:
                            accumulate(i, q - 1, buckets[q])
                        elif not first:
                            accumulate(i - 1, G - 1, buckets[0])
                        if not (last and q >= G - 2):
                            one_hot(*ahead(i, q, 2))
                    if last:
                        accumulate(i, G - 1, buckets[G])

                bodies(dve, body)

            @block.tensor
            def _(pe):
                pe.wait_ge(s_w, 16)
                pe.wait_ge(s_zero, TB + 1)

                def body(i, first, last, tile):
                    if tile is not None:
                        pe.wait_ge(s_xT, 16 * i)
                        pe.wait_ge(s_z_taken, i)
                        for k in range(KD):
                            mm = pe.matmul(p_z[:, 0:D], xT[:, k, :], w_r[:, k, :], start=(k == 0), stop=(k == KD - 1))
                        mm.then_inc(s_z, 1)
                    for q in range(G):
                        if not (first and q < 2):
                            pe.wait_ge(s_acc, G * i + q - 1)
                        pe.wait_ge(s_hot, T * i + 2 * q + 2)
                        for j in range(2):
                            t = 2 * q + j
                            pe.wait_ge(s_gath[t % TB], 16 * (2 * i + t // TB) + 16)
                            last_mm = pe.matmul(p_sum[q % 2][:, 0:W], hot[q % 4][:, j, :], yg[t % TB][:, :],
                                                start=(j == 0), stop=(j == 1))
                        last_mm.then_inc(s_sum, 1)

                bodies(pe, body)


def stage_finish(nc, C, A, S):
    with ExitStack() as ctx:
        m = Mem(nc, ctx, "finish_")
        b_r, wr = m.sb("b_r", [P, 1, D]), m.sb("wr", [P, D])
        xr, r, o, y = (m.sb(n, [P, CH, D]) for n in ("xr", "r", "o", "y"))
        junk, rdeg = m.sb("junk", [P, D]), m.sb("rdeg", [P, NT, 1])
        stats, small = m.sb("stats", [P, CH, 6]), m.sb("small", [P, 5, CH])
        s_w, s_xr, s_r, s_deg, s_o, s_ln, s_route, s_st = (
            m.sem(n) for n in ("w", "xr", "r", "deg", "o", "ln", "route", "st"))

        with nc.Block() as block:
            @block.sync
            def _(sp):
                sp.dma_start(b_r[:, 0, :], on_all(A.b2)).then_inc(s_w, 16)
                sp.dma_start(wr[:, :], on_all(A.wr.rearrange("d a -> (d a)"))).then_inc(s_w, 16)

                def load(c):
                    wait_past(sp, s_r, 2 * c)
                    sp.dma_start(xr[:, :, :], chunk(S.x2, c)).then_inc(s_xr, 16)

                def store(c):
                    sp.wait_ge(s_ln, LN_STEPS * c + LN_STEPS)
                    sp.dma_start(chunk(S.x3, c), o[:, :, :]).then_inc(s_st, 16)
                    sp.dma_start(chunk(S.xn3, c), y[:, :, :]).then_inc(s_st, 16)

                load_ahead(sp, load, store)
                sp.wait_ge(s_st, 32 * NCH)

            @block.gpsimd
            def _(pool):
                pool.wait_ge(s_w, 32)
                for c in chunks(pool):
                    pool.wait_ge(s_xr, 16 * c + 16)
                    wait_past(pool, s_o, (CH + 1) * c)
                    pool.tensor_tensor(r[:, :, :], xr[:, :, :], C.z[:, bass.ds(c * CH, CH), :], ALU.add).then_inc(s_r, 1)
                    pool.wait_ge(s_r, 2 * c + 1)
                    pool.tensor_tensor(r[:, :, :], r[:, :, :], b_r[:, :, :].to_broadcast([P, CH, D]),
                                       ALU.add).then_inc(s_r, 1)

            @block.vector
            def _(dve):
                step = Chain(dve, s_deg)
                step.link(dve.tensor_scalar(rdeg[:, :, :], C.nbr[:, :, D:D + 1], 1.0, None, ALU.max))
                step.link(dve.reciprocal(rdeg[:, :, :], rdeg[:, :, :]))
                dve.wait_ge(s_w, 32)
                for c in chunks(dve):
                    wait_past(dve, s_st, 32 * c)
                    dve.wait_ge(s_r, 2 * c + 2)
                    for t in range(CH):
                        tile = bass.ds(c * CH + t, 1)
                        dve.scalar_tensor_tensor(out=o[:, t, :], in0=C.nbr[:, tile, 0:D].rearrange("p a n -> p (a n)"),
                                                 scalar=rdeg[:, tile, :].rearrange("p a n -> p (a n)"), in1=r[:, t, :],
                                                 op0=ALU.mult, op1=ALU.add).then_inc(s_o, 1)
                    dve.wait_ge(s_o, (CH + 1) * c + CH)
                    dve.sem_inc(s_o, 1)
                    layer_norm_chunk(dve, s_ln, LN_STEPS * c, o, y, stats, small)
                    dve.wait_ge(s_ln, LN_STEPS * c + LN_STEPS)
                    for t in range(CH):
                        if t > 0:
                            dve.wait_ge(s_route, CH * c + t)
                        elif not isinstance(c, int):
                            dve.wait_ge(s_route, CH * c)
                        dve.scalar_tensor_tensor(out=junk[:, :], in0=y[:, t, :], scalar=1.0, in1=wr[:, :],
                                                 op0=ALU.mult, op1=ALU.mult,
                                                 accum_out=C.route[:, bass.ds(c * CH + t, 1)]).then_inc(s_route, 1)
        m.clear_sems()


def stage_routed(nc, C, A, S, out_ap):
    NHID = A.w1.shape[1]
    KF = NHID // P
    KEEP = max(1, N_NODES // 2) - 1
    with ExitStack() as ctx:
        m = Mem(nc, ctx)
        w1, b1 = m.sb("w1", [P, KD, NHID]), m.sb("b1", [P, KF])
        w2, b2 = m.sb("w2f", [P, KF, D]), m.sb("b2f", [P, 1, D])
        br = m.sb("br", [P, 1])
        route = m.sb("route_b", [P, NT])
        row = m.sb("row", [P, N_NODES])
        junk, junk2 = m.sb("r_junk", [P, N_NODES], BF16), m.sb("r_junk2", [P, P])
        after = m.sb("after", [P, P])
        counts = m.sb("counts", [P, NT, 3])
        rank, gate = m.sb("rank_r", [P, NT]), m.sb("gate", [P, NT])
        xn, x3, o = (m.sb(f"r_{n}", [P, CH, D]) for n in ("xn", "x3", "o"))
        r = m.sb("r_r", [P, NT, D])
        xT = m.sb("r_xT", [P, KD, CH * P])
        hT = m.sb("r_hT", [P, KF, CH * P])
        y = m.sb("r_y", [P, NT, D])
        NA = 2 * KF
        tr = [m.ps(f"r_tr{b}", [P, HID]) for b in range(2)]
        hidden, out = Banks(m, "r_h", 4, NA), Banks(m, "r_o", 2, CH)
        s_w, s_br, s_x, s_trf, s_tre, s_add = (m.sem(f"r_{n}") for n in ("w", "br", "x", "trf", "tre", "add"))
        s_route, s_row, s_row_in, s_cnt, s_dve, s_y, s_o, s_st = (
            m.sem(f"r_{n}") for n in ("route", "row", "row_in", "cnt", "dve", "y", "o", "st"))

        with nc.Block() as block:
            @block.sync
            def _(sp):
                sp.dma_start(br[:, :], on_all(A.br)).then_inc(s_br, 16)
                sp.dma_start(w1[:, :, :], rows_on_partitions(A.w1)).then_inc(s_w, 16)
                sp.dma_start(b1[:, :], by_feature(A.b1f), allow_slow_non_contiguous=True).then_inc(s_w, 16)
                sp.dma_start(w2[:, :, :], rows_on_partitions(A.w2)).then_inc(s_w, 16)
                sp.dma_start(b2[:, 0, :], on_all(A.b2f)).then_inc(s_w, 16)
                sp.wait_ge(s_route, 1)
                sp.dma_start(S.route.rearrange("(t p) -> p t", p=P), route[:, :],
                             allow_slow_non_contiguous=True).then_inc(s_row, 16)
                sp.wait_ge(s_row, 16)
                sp.dma_start(row[:, :], on_all(S.route[0:N_NODES])).then_inc(s_row_in, 16)
                for c in chunks(sp):
                    wait_past(sp, s_trf, 4 * c)
                    wait_past(sp, s_add, c)
                    sp.dma_start(xn[:, :, :], chunk(S.xn3, c)).then_inc(s_x, 16)
                    sp.dma_start(x3[:, :, :], chunk(S.x3, c)).then_inc(s_x, 16)
                for c in chunks(sp):
                    sp.wait_ge(s_o, 2 * CH * c + 2 * CH)
                    sp.dma_start(chunk(out_ap, c), o[:, :, :]).then_inc(s_st, 16)
                sp.wait_ge(s_st, 16 * NCH)

            @block.gpsimd
            def _(pool):
                for c in chunks(pool):
                    pool.wait_ge(s_x, 32 * c + 32)
                    pool.tensor_tensor(r[:, bass.ds(c * CH, CH), :], xn[:, :, :], x3[:, :, :], ALU.add).then_inc(s_add, 1)

            @block.scalar
            def _(act):
                act.wait_ge(s_w, 64)
                for c in chunks(act):
                    take_transposed(act, c, xT, tr, s_trf, s_tre)
                    for k in range(KF):
                        for h, (a, b) in enumerate(HALVES):
                            src = hidden.to_take(act, c, 2 * k + h)
                            act.activation(hT[:, k, a * P:b * P], src[:, 0:(b - a) * P], ACT.Gelu_apprx_tanh,
                                           bias=b1[:, k:k + 1]).then_inc(hidden.empty, 1)
                    for t in range(CH):
                        src = out.to_take(act, c, t)
                        act.activation(y[:, bass.ds(c * CH + t, 1), :].rearrange("p a n -> p (a n)"), src[:, 0:D],
                                       ACT.Copy).then_inc(out.empty, 1)

            @block.vector
            def _(dve):
                step = Chain(dve, s_dve)
                dve.wait_ge(s_br, 16)
                dve.tensor_scalar(route[:, :], C.route[:, :], br[:, 0:1], None, ALU.add).then_inc(s_route, 1)
                step.link(dve.tensor_scalar(after[:, :], C.iota_f[:, :], C.part_f[:, 0:1], None, ALU.is_lt))
                step.link(dve.memset(counts[:, :, :], 0.0))
                dve.wait_ge(s_route, 1)
                dve.wait_ge(s_row_in, 16)
                for t in range(NT):
                    a, b = t * P, min((t + 1) * P, N_NODES)
                    own = route[:, t:t + 1]
                    if t > 0:
                        step.link(dve.tensor_scalar(junk[:, 0:a], row[:, 0:a], own, None, ALU.is_ge, ALU.add,
                                                    accum_out=counts[:, t, 0:1]))
                    step.link(dve.tensor_scalar(junk[:, a:N_NODES], row[:, a:N_NODES], own, None, ALU.is_gt, ALU.add,
                                                accum_out=counts[:, t, 1:2]))
                    step.link(dve.scalar_tensor_tensor(out=junk2[:, 0:b - a], in0=row[:, a:b], scalar=own,
                                                       in1=after[:, 0:b - a], op0=ALU.is_equal, op1=ALU.mult,
                                                       accum_out=counts[:, t, 2:3]))
                step.link(dve.tensor_reduce(rank[:, :], counts[:, :, :], AX.X, ALU.add))
                step.link(dve.scalar_tensor_tensor(out=gate[:, :], in0=rank[:, :], scalar=float(KEEP), in1=route[:, :],
                                                   op0=ALU.is_lt, op1=ALU.mult))
                dve.wait_ge(s_w, 64)
                for c in chunks(dve):
                    dve.wait_ge(s_add, c + 1)
                    wait_past(dve, s_st, 16 * c)
                    for t in range(CH):
                        dve.wait_ge(out.empty, CH * c + t + 1)
                        dve.tensor_tensor(o[:, t, :], y[:, bass.ds(c * CH + t, 1), :].rearrange("p a n -> p (a n)"),
                                          b2[:, 0, :], ALU.add).then_inc(s_o, 1)
                    for t in range(CH):
                        dve.wait_ge(s_o, 2 * CH * c + CH + t)
                        dve.scalar_tensor_tensor(out=o[:, t, :], in0=o[:, t, :], scalar=gate[:, bass.ds(c * CH + t, 1)],
                                                 in1=r[:, bass.ds(c * CH + t, 1), :].rearrange("p a n -> p (a n)"),
                                                 op0=ALU.mult, op1=ALU.add).then_inc(s_o, 1)

            @block.tensor
            def _(pe):
                pe.wait_ge(s_w, 64)
                for c in chunks(pe):
                    pe.wait_ge(s_x, 32 * c + 32)
                    transpose_chunk(pe, c, xn, tr, C.ident[:, :], s_trf, s_tre)
                    pe.wait_ge(s_tre, 4 * c + 4)
                    for k in range(KF):
                        for h, (a, b) in enumerate(HALVES):
                            dst = hidden.to_fill(pe, c, 2 * k + h)[:, 0:(b - a) * P]
                            for j in range(KD):
                                last = pe.matmul(dst, w1[:, j, k * P:(k + 1) * P], xT[:, j, a * P:b * P],
                                                 start=(j == 0), stop=(j == KD - 1))
                            last.then_inc(hidden.full, 1)
                    pe.wait_ge(hidden.empty, NA * c + NA)
                    for t in range(CH):
                        dst = out.to_fill(pe, c, t)[:, 0:D]
                        for j in range(KF):
                            last = pe.matmul(dst, hT[:, j, t * P:(t + 1) * P], w2[:, j, :], start=(j == 0), stop=(j == KF - 1))
                        last.then_inc(out.full, 1)


def build(nc, A, out):
    with ExitStack() as ctx:
        m = Mem(nc, ctx)
        C, S = Names(), Names()
        C.iota_i = m.sb("iota_i", [P, P], I32)
        C.iota_f = m.sb("iota_f", [P, P])
        C.iota_b = m.sb("iota_b", [P, P], F16)
        C.iota_h = m.sb("iota_h", [P, NCOL], I16)
        C.part_i = m.sb("part_i", [P, 1], I32)
        C.part_f = m.sb("part_f", [P, 1])
        C.ident = m.sb("ident", [P, P])
        C.before = m.sb("before", [P, P])
        C.ones = m.sb("ones", [P, P])
        C.zeros = m.sb("zeros", [P, P], F16)
        C.zeros_w = m.sb("zeros_w", [P, NCOL], F16)
        C.bucket = m.sb("bucket", [1, 2, NG], I32)
        C.gidx = m.sb("gidx", [P, NCOL], U32)
        C.dloc = m.sb("dloc", [P, NCOL])
        C.route = m.sb("route", [P, NT])

        def dram(name, shape, dt=F32):
            return nc.dram_tensor(name, shape, dt).ap()

        S.recs = dram("recs_d", [NSLOT + EC, REC])
        S.bucket, S.bucket2 = dram("bucket_d", [NG], I32), dram("bucket2_d", [NG], I32)
        S.xn, S.xn1, S.xn2, S.xn3, S.x1, S.x2, S.x3, S.y = (
            dram(f"{n}_d", [NPAD, D]) for n in ("xn", "xn1", "xn2", "xn3", "x1", "x2", "x3", "y"))
        S.xnT, S.xT = dram("xnT_d", [D, NPAD]), dram("xT_d", [D, NPAD])
        S.p, S.q = dram("p_d", [NPAD, 2 * HID]), dram("q_d", [NPAD, HID])
        S.deg, S.route = dram("deg_d", [NPAD]), dram("route_d", [NPAD])

        stage_constants(nc, C)
        stage_prepare(nc, C, A, S)
        with ExitStack() as edge_ctx:
            e = Mem(nc, edge_ctx)
            C.agg = e.sb("agg", [P, NT, HID])
            C.deg_src = e.sb("deg_src", [P, NT])
            stage_edge_network(nc, C, A, S)
            stage_update(nc, C, A, S)
        stage_experts(nc, C, A, S)
        with ExitStack() as sage_ctx:
            e = Mem(nc, sage_ctx)
            C.nbr = e.sb("nbr", [P, NT, D + 2])
            C.z = e.sb("z", [P, NT, D])
            for layer in range(2):
                stage_project(nc, C, A, S, layer)
                stage_neighbours(nc, C, A, S, layer)
            stage_finish(nc, C, A, S)
        stage_routed(nc, C, A, S, out)


_INS = {"mW1": "L0_gnn_mW1", "mb1": "L0_gnn_mb1", "mW2": "L0_gnn_mW2", "mb2": "L0_gnn_mb2", "uW1": "L0_gnn_uW1",
        "ub1": "L0_gnn_ub1", "uW2": "L0_gnn_uW2", "ub2": "L0_gnn_ub2", "sW1": "L0_ffn_sW1", "sb1": "L0_ffn_sb1",
        "sW2": "L0_ffn_sW2", "sb2": "L0_ffn_sb2", "sW3": "L0_ffn_sW3", "sb3": "L0_ffn_sb3", "eW1": "L0_ffn_eW1",
        "eb1": "L0_ffn_eb1", "eW2": "L0_ffn_eW2", "eb2": "L0_ffn_eb2", "eW3": "L0_ffn_eW3", "eb3": "L0_ffn_eb3",
        "gW": "L0_ffn_gW", "gb": "L0_ffn_gb", "W_l1": "L1_gnn_W_l1", "b1": "L1_gnn_b1", "W_r1": "L1_gnn_W_r1",
        "W_l2": "L1_gnn_W_l2", "b2": "L1_gnn_b2", "W_r2": "L1_gnn_W_r2", "wr": "L1_ffn_wr", "br": "L1_ffn_br",
        "w1": "L1_ffn_w1", "b1f": "L1_ffn_b1", "w2": "L1_ffn_w2", "b2f": "L1_ffn_b2"}


def kernel(**inputs):
    import numpy as _np
    import concourse.bacc as _bacc
    from concourse import mybir as _mybir
    from concourse.bass_utils import run_bass_kernel_spmd as _run

    def padded(name, rows, fill):
        a = _np.asarray(inputs[name])
        whole = _np.full((rows,) + a.shape[1:], fill, a.dtype)
        whole[:a.shape[0]] = a
        return whole

    host = {"x": padded("x", NPAD, 0), "src": padded("src", EPAD, NPAD), "dst": padded("dst", EPAD, NPAD),
            "edge_attr": padded("edge_attr_16", EPAD, 0)}
    for short, name in _INS.items():
        host[short] = _np.ascontiguousarray(inputs[name])
    nc = _bacc.Bacc("TRN2", target_bir_lowering=False, num_devices=1)
    A, arrays = Names(), {}
    for short, a in host.items():
        arrays[f"in_{short}"] = a
        setattr(A, short, nc.dram_tensor(f"in_{short}", a.shape, _mybir.dt.from_np(a.dtype), kind="ExternalInput").ap())
    out = nc.dram_tensor("out_0", (NPAD, D), F32, kind="ExternalOutput").ap()
    build(nc, A, out)
    r = _run(nc, [arrays], core_ids=[0])
    return r.results[0]["out_0"][:N_NODES]
```

```python
from contextlib import ExitStack

import concourse.bass as bass
from concourse import mybir

ALU = mybir.AluOpType
ACT = mybir.ActivationFunctionType
AX = mybir.AxisListType
F32 = mybir.dt.float32
F32R = mybir.dt.float32r
F16 = mybir.dt.float16
BF16 = mybir.dt.bfloat16
I32 = mybir.dt.int32
U32 = mybir.dt.uint32
I16 = mybir.dt.int16

P = 128
N_NODES = 3125
D = 256
KD = D // P
HID = 512
KH = HID // P
N_EDGES = 53125
EDGE_DIM = 16
NT = -(-N_NODES // P)
NPAD = NT * P
EC = -(-N_EDGES // P)
EPAD = EC * P
GROUP = 2 * P
NG = (N_EDGES + NT * (GROUP - 1)) // GROUP
NSLOT = NG * GROUP
NCOL = 2 * NG
REC = 2 + 2 * EDGE_DIM
CH = 5
NCH = NT // CH
EPS = 1e-5
HB = 8
UNROLL = HB
TAB = EC // NT // UNROLL * UNROLL
BATCH = 8


class Names:
    pass


class Mem:

    def __init__(self, nc, ctx, prefix=""):
        self.nc, self.ctx, self.prefix, self.sems = nc, ctx, prefix, []

    def sb(self, name, shape, dt=F32):
        return self.ctx.enter_context(self.nc.sbuf_tensor(self.prefix + name, shape, dt))

    def ps(self, name, shape, dt=F32):
        return self.ctx.enter_context(self.nc.psum_tensor(self.prefix + name, shape, dt))

    def sem(self, name):
        self.sems.append(self.nc.alloc_semaphore(self.prefix + name))
        return self.sems[-1]

    def clear_sems(self):
        for sem in self.sems:
            self.nc.sync.sem_clear(sem)
            self.nc.release_semaphore(sem)


class Chain:

    def __init__(self, eng, sem):
        self.eng, self.sem, self.n = eng, sem, 0

    def link(self, ins):
        ins.then_inc(self.sem, 1)
        self.n += 1
        self.eng.wait_ge(self.sem, self.n)


def chunks(eng):
    yield 0
    with eng.Fori(1, NCH) as c:
        yield c


def load_ahead(eng, load, store, after_first=None):
    load(0)
    if after_first:
        after_first()
    load(1)
    store(0)
    with eng.Fori(1, NCH - 1) as c:
        load(c + 1)
        store(c)
    store(NCH - 1)


def wait_past(eng, sem, count):
    if not (isinstance(count, int) and count == 0):
        eng.wait_ge(sem, count)


def layer_norm_chunk(dve, done, at, x, xn, stats, small):
    for t in range(CH):
        dve.bn_stats(stats[:, t, :], x[:, t, :]).then_inc(done, 1)
    dve.wait_ge(done, at + CH)
    mean, var, rstd, diff, diff2 = (small[:, n, :] for n in range(5))
    dve.tensor_tensor(mean, stats[:, :, 1], stats[:, :, 4], ALU.add).then_inc(done, 1)
    dve.tensor_tensor(diff, stats[:, :, 1], stats[:, :, 4], ALU.subtract).then_inc(done, 1)
    dve.tensor_tensor(var, stats[:, :, 2], stats[:, :, 5], ALU.add).then_inc(done, 1)
    dve.wait_ge(done, at + CH + 3)
    dve.tensor_scalar(mean, mean, 0.5, None, ALU.mult).then_inc(done, 1)
    dve.tensor_tensor(diff2, diff, diff, ALU.mult).then_inc(done, 1)
    dve.tensor_scalar(var, var, 1.0 / D, EPS, ALU.mult, ALU.add).then_inc(done, 1)
    dve.wait_ge(done, at + CH + 6)
    dve.scalar_tensor_tensor(out=var, in0=diff2, scalar=0.25, in1=var, op0=ALU.mult, op1=ALU.add).then_inc(done, 1)
    dve.wait_ge(done, at + CH + 7)
    bits = rstd.bitcast(I32)
    dve.tensor_scalar(bits, var.bitcast(I32), 1, None, ALU.logical_shift_right).then_inc(done, 1)
    dve.wait_ge(done, at + CH + 8)
    dve.tensor_scalar(bits, bits, -1.0, float(0x5F3759DF), ALU.mult, ALU.add).then_inc(done, 1)
    for n in range(NEWTON):
        first = at + CH + 9 + 4 * n
        dve.wait_ge(done, first)
        dve.tensor_tensor(diff, rstd, rstd, ALU.mult).then_inc(done, 1)
        dve.wait_ge(done, first + 1)
        dve.tensor_tensor(diff, diff, var, ALU.mult).then_inc(done, 1)
        dve.wait_ge(done, first + 2)
        dve.tensor_scalar(diff, diff, -0.5, 1.5, ALU.mult, ALU.add).then_inc(done, 1)
        dve.wait_ge(done, first + 3)
        dve.tensor_tensor(rstd, rstd, diff, ALU.mult).then_inc(done, 1)
    dve.wait_ge(done, at + CH + 9 + 4 * NEWTON)
    for t in range(CH):
        dve.tensor_scalar(xn[:, t, :], x[:, t, :], mean[:, t:t + 1], rstd[:, t:t + 1], ALU.subtract,
                          ALU.mult).then_inc(done, 1)


NEWTON = 4
LN_STEPS = 2 * CH + 9 + 4 * NEWTON


def stage_constants(nc, C):
    with ExitStack() as ctx:
        m = Mem(nc, ctx)
        s_iota, s_done = m.sem("s_iota"), m.sem("s_const")
        with nc.Block() as block:
            @block.gpsimd
            def _(pool):
                pool.iota(C.iota_i[:, :], [[1, P]], base=0, channel_multiplier=0).then_inc(s_iota, 1)
                pool.iota(C.iota_h[:, :], [[1, NCOL]], base=0, channel_multiplier=0,
                          allow_small_or_imprecise_dtypes=True).then_inc(s_iota, 1)
                pool.iota(C.part_i[:, :], [[0, 1]], base=0, channel_multiplier=1).then_inc(s_iota, 1)

            @block.vector
            def _(dve):
                step = Chain(dve, s_done)
                dve.wait_ge(s_iota, 3)
                step.link(dve.tensor_copy(C.iota_f[:, :], C.iota_i[:, :]))
                step.link(dve.tensor_copy(C.iota_b[:, :], C.iota_i[:, :]))
                step.link(dve.tensor_copy(C.part_f[:, :], C.part_i[:, :]))
                step.link(dve.tensor_scalar(C.ident[:, :], C.iota_f[:, :], C.part_f[:, 0:1], None, ALU.is_equal))
                step.link(dve.tensor_scalar(C.before[:, :], C.iota_f[:, :], C.part_f[:, 0:1], None, ALU.is_gt))
                step.link(dve.memset(C.ones[:, :], 1.0))
                step.link(dve.memset(C.zeros[:, :], 0.0))
                step.link(dve.memset(C.zeros_w[:, :], 0.0))


def stage_prepare(nc, C, A, S):
    with ExitStack() as ctx:
        m = Mem(nc, ctx)
        key = [m.sb(f"key{k}", [P, EC], I32) for k in range(2)]
        hi_i = m.sb("hi_i", [P, EC], I32)
        hi16 = [m.sb(f"hi16_{k}", [P, EC], I16) for k in range(2)]
        lo_i = m.sb("lo_i", [P, EC], I32)
        pos = m.sb("pos", [P, EC])
        pad_pos = m.sb("pad_pos", [P, EC])
        iota_c = m.sb("iota_c", [P, EC])
        slot_src = m.sb("slot_src", [P, EC], U32)
        slot_dst = m.sb("slot_dst", [P, EC], I32)
        lane, col = m.sb("lane", [P, EC]), m.sb("col", [P, EC])
        val = m.sb("val", [P, 2, EC])
        ends = m.sb("ends", [P, NT + 1])
        cnt = m.sb("cnt", [P, NT])
        grp_i = m.sb("grp_i", [P, NT], I32)
        grp = m.sb("grp", [P, NT])
        start = m.sb("start", [P, NT])
        off = m.sb("off", [P, NT])
        hit = m.sb("hit", [P, NT])
        gk_i = m.sb("gk_i", [P, 2], I32)
        gk = m.sb("gk", [P, 2])
        bkt_f = m.sb("bkt_f", [P, 2])
        bkt_i = m.sb("bkt_i", [P, 2], I32)
        recs = m.sb("recs", [P, EC, REC])
        fill = m.sb("fill", [P, 29, REC])
        stage = [m.sb(f"stage{b}", [P, BATCH, REC]) for b in range(2)]
        stage_pos = [m.sb(f"stage_pos{b}", [P, BATCH], U32) for b in range(2)]
        lane_one = [m.sb(f"lane_one{b}", [P, P], F16) for b in range(HB)]
        lane_hot = [m.sb(f"lane_hot{b}", [P, 2, P], F16) for b in range(HB)]
        col_hot = [m.sb(f"col_hot{b}", [P, NCOL], F16) for b in range(HB)]
        member = m.sb("member", [P, NT, EC], BF16)
        rank = m.sb("rank", [P, NT, EC])
        with ExitStack() as early:
            attr = Mem(nc, early).sb("attr", [P, EC * EDGE_DIM])
        xc = m.sb("xc", [P, CH, D])
        xnc = m.sb("xnc", [P, CH, D])
        xtc = m.sb("xtc", [P, KD, CH * P])
        w_pq = m.sb("w_pq", [P, 2, KD, HID])
        p_out = [m.sb(f"p_out{b}", [P, HID]) for b in range(2)]
        q_out = [m.sb(f"q_out{b}", [P, HID]) for b in range(2)]
        stats = m.sb("stats", [P, CH, 6])
        small = m.sb("small", [P, 5, CH])

        acc = [m.ps(f"acc{k}", [P, HID]) for k in range(2)]
        tr = [m.ps(f"tr{k}", [P, HID]) for k in range(2)]
        pq = [[m.ps(f"pq{h}{b}", [P, HID]) for b in range(2)] for h in range(2)]

        s_key, s_attr, s_fill, s_filled = m.sem("s_key"), m.sem("s_attr"), m.sem("s_fill"), m.sem("s_filled")
        s_padkey = m.sem("s_padkey")
        s_iota = m.sem("s_iota_c")
        s_dve = m.sem("s_dve")
        s_cnt, s_sum = m.sem("s_cnt"), m.sem("s_sum")
        s_high, s_low = m.sem("s_high"), m.sem("s_low")
        s_order = m.sem("s_order")
        s_staged = m.sem("s_staged")
        s_scat = [m.sem(f"s_scat{b}") for b in range(2)]
        s_lane, s_col, s_scaled = m.sem("s_lane"), m.sem("s_col"), m.sem("s_scaled")
        s_hot_used, s_table = m.sem("s_hot_used"), m.sem("s_table")
        s_bkt, s_bkt_out, s_bkt_in = m.sem("s_bkt"), m.sem("s_bkt_out"), m.sem("s_bkt_in")
        s_w, s_x = m.sem("s_w"), m.sem("s_x")
        s_ln = m.sem("s_ln")
        s_tr, s_xt = m.sem("s_tr"), m.sem("s_xt")
        s_pq, s_p, s_q = m.sem("s_pq"), m.sem("s_p"), m.sem("s_q")
        s_pst, s_qst = [m.sem(f"s_pst{b}") for b in range(2)], [m.sem(f"s_qst{b}") for b in range(2)]
        s_xnst, s_xtst = m.sem("s_xnst"), m.sem("s_xtst")
        s_stage = [m.sem(f"s_stage{b}") for b in range(2)]

        with nc.Block() as block:
            @block.sync
            def _(sp):
                for k, src in enumerate((A.src, A.dst)):
                    sp.dma_start(key[k][:, :], src.rearrange("(p c) -> p c", c=EC)).then_inc(s_key, 16)
                sp.dma_start(attr[:, :], A.edge_attr.rearrange("(p c) w -> p (c w)", c=EC)).then_inc(s_attr, 16)
                sp.wait_ge(s_fill, 3)
                recs_v = S.recs[0:NSLOT, :].rearrange("(n p r) w -> n p (r w)", p=P, r=29)
                for n in range(NSLOT // (29 * P)):
                    sp.dma_start(recs_v[n], fill[:, :, :].rearrange("p r w -> p (r w)")).then_inc(s_filled, 16)
                sp.wait_ge(s_low, 1)
                sp.wait_ge(s_order, 1)
                for h in range(2):
                    sp.dma_start(w_pq[:, h, :, :],
                                 A.mW1[h * D:(h + 1) * D, :].rearrange("(k p) n -> p k n", p=P)).then_inc(s_w, 16)
                sp.wait_ge(s_order, 2)
                def fill_stages(i):
                    for b in range(2):
                        at = (2 * i + b) * BATCH
                        wait_past(sp, s_scat[b], 16 * BATCH * i)
                        sp.dma_start(stage[b][:, :, :].rearrange("p c w -> p (c w)"),
                                     recs[:, bass.ds(at, BATCH), :].rearrange("p c w -> p (c w)")).then_inc(s_stage[b], 16)
                        sp.dma_start(stage_pos[b][:, :], slot_src[:, bass.ds(at, BATCH)]).then_inc(s_stage[b], 16)

                fill_stages(0)
                with sp.Fori(1, EC // (2 * BATCH)) as i:
                    fill_stages(i)

            @block.gpsimd
            def _(pool):
                pool.memset(fill[:, :, 0:1], -1.0).then_inc(s_fill, 1)
                pool.memset(fill[:, :, 1:2].bitcast(U32), 0).then_inc(s_fill, 1)
                pool.memset(fill[:, :, 2:REC], 0.0).then_inc(s_fill, 1)
                pool.iota(lo_i[:, :], [[1, EC]], base=NSLOT, channel_multiplier=0).then_inc(s_iota, 1)
                pool.iota(gk_i[:, :], [[1, 2]], base=0, channel_multiplier=2).then_inc(s_iota, 1)
                pool.wait_ge(s_attr, 16)
                pool.wait_ge(s_high, 1)
                pool.tensor_tensor(recs[:, :, 2 + EDGE_DIM:REC], attr[:, :].rearrange("p (c w) -> p c w", w=EDGE_DIM),
                                   recs[:, :, 2:2 + EDGE_DIM], ALU.subtract).then_inc(s_low, 1)
                pool.wait_ge(s_filled, 16 * (NSLOT // (29 * P)))
                with pool.Fori(0, EC // (2 * BATCH)) as i:
                    for b in range(2):
                        pool.wait_ge(s_stage[b], 32 * i + 32)
                        pool.nop(nofuse=True)
                        for j in range(BATCH):
                            pool.indirect_dma_start(
                                S.recs[:, :], bass.IndirectOffsetOnAxis(ap=stage_pos[b][:, j:j + 1], axis=0),
                                stage[b][:, j, :], None).then_inc(s_scat[b], 16)
                for b in range(2):
                    pool.wait_ge(s_scat[b], 16 * BATCH * (EC // (2 * BATCH)))

            @block.scalar
            def _(act):
                act.wait_ge(s_attr, 16)
                act.activation(recs[:, :, 2:2 + EDGE_DIM].bitcast(F32R),
                               attr[:, :].rearrange("p (c w) -> p c w", w=EDGE_DIM), ACT.Copy).then_inc(s_high, 1)
                act.wait_ge(s_bkt, 1)
                act.dma_start(S.bucket.rearrange("(p j) -> p j", j=2), bkt_i[0:NG // 2, :]).then_inc(s_bkt_out, 16)
                act.wait_ge(s_bkt_out, 16)
                act.dma_start(C.bucket[0:1, 0, :], S.bucket.rearrange("(a k) -> a k", a=1)).then_inc(s_bkt_in, 16)
                act.wait_ge(s_bkt, 2)
                act.dma_start(S.bucket2.rearrange("(p j) -> p j", j=2), bkt_i[0:NG // 2, :]).then_inc(s_bkt_out, 16)
                act.wait_ge(s_bkt_out, 32)
                act.dma_start(C.bucket[0:1, 1, :], S.bucket2.rearrange("(a k) -> a k", a=1)).then_inc(s_bkt_in, 16)

                def scaled(c, b):
                    act.wait_ge(s_lane, c + 1)
                    for k in range(2):
                        act.activation(lane_hot[b][:, k, :], lane_one[b][:, :], ACT.Copy,
                                       scale=val[:, k, bass.ds(c, 1)]).then_inc(s_scaled, 1)

                x_v = A.x.rearrange("(t p) d -> p t d", p=P)
                act.wait_ge(s_low, 1)
                for c in chunks(act):
                    wait_past(act, s_ln, LN_STEPS * c)
                    act.dma_start(xc[:, :, :], x_v[:, bass.ds(c * CH, CH), :]).then_inc(s_x, 16)
                    act.wait_ge(s_ln, LN_STEPS * c + LN_STEPS)
                    act.dma_start(S.xn.rearrange("(t p) d -> p t d", p=P)[:, bass.ds(c * CH, CH), :],
                                  xnc[:, :, :]).then_inc(s_xnst, 16)
                    wait_past(act, s_xtst, 16 * c)
                    for k in range(KD):
                        for h in range(2):
                            w = 4 * P if h == 0 else P
                            act.wait_ge(s_tr, 4 * c + 2 * k + h + 1)
                            act.activation(xtc[:, k, 4 * P * h:4 * P * h + w], tr[h][:, 0:w],
                                           ACT.Copy).then_inc(s_xt, 1)
                    act.wait_ge(s_xt, 4 * c + 4)
                    act.dma_start(S.xnT.rearrange("(k p) n -> p k n", p=P)[:, :, bass.ds(c * CH * P, CH * P)],
                                  xtc[:, :, :]).then_inc(s_xtst, 16)

                    def take_projections(t):
                        b, uses = t % 2, (CH + 1 - t % 2) // 2
                        act.wait_ge(s_pq, 2 * CH * c + 2 * t + 1)
                        wait_past(act, s_pst[b], 16 * (uses * c + t // 2))
                        act.activation(p_out[b][:, :], pq[0][b][:, :], ACT.Copy).then_inc(s_p, 1)
                        act.wait_ge(s_pq, 2 * CH * c + 2 * t + 2)
                        wait_past(act, s_qst[b], 16 * (uses * c + t // 2))
                        act.activation(q_out[b][:, :], pq[1][b][:, :], ACT.Copy).then_inc(s_q, 1)
                        act.wait_ge(s_q, CH * c + t + 1)
                        act.dma_start(S.q[bass.ds((c * CH + t) * P, P), :], q_out[b][:, :]).then_inc(s_qst[b], 16)
                        act.wait_ge(s_p, CH * c + t + 1)
                        act.dma_start(S.p[bass.ds((c * CH + t) * P, P), :], p_out[b][:, :]).then_inc(s_pst[b], 16)

                    for t in range(CH):
                        with act.Fori(0, TAB // UNROLL) as g:
                            for h in range(UNROLL):
                                scaled((CH * c + t) * TAB + UNROLL * g + h, h % HB)
                        if t > 0:
                            take_projections(t - 1)
                    take_projections(CH - 1)
                with act.Fori(NT * TAB // UNROLL, EC // UNROLL) as g:
                    for h in range(UNROLL):
                        scaled(UNROLL * g + h, h % HB)
                for b in range(2):
                    act.wait_ge(s_pst[b], 16 * NCH * ((CH + 1 - b) // 2))
                    act.wait_ge(s_qst[b], 16 * NCH * ((CH + 1 - b) // 2))
                act.wait_ge(s_xnst, 16 * NCH)
                act.wait_ge(s_xtst, 16 * NCH)
                act.wait_ge(s_bkt_in, 32)

            @block.vector
            def _(dve):
                step = Chain(dve, s_dve)
                dve.wait_ge(s_iota, 2)
                step.link(dve.tensor_copy(iota_c[:, :], lo_i[:, :]))
                step.link(dve.tensor_copy(gk[:, :], gk_i[:, :]))
                for k in range(2):
                    dve.wait_ge(s_key, 32)
                    dve.tensor_scalar(hi_i[:, :], key[k][:, :], 7, None, ALU.logical_shift_right).then_inc(s_dve, 1)
                    dve.tensor_scalar(lo_i[:, :], key[k][:, :], P - 1, None, ALU.bitwise_and).then_inc(s_dve, 1)
                    step.n += 2
                    dve.wait_ge(s_dve, step.n)
                    dve.tensor_copy(hi16[k][:, :], hi_i[:, :]).then_inc(s_dve, 1)
                    if k == 0:
                        dve.tensor_copy(recs[:, :, 0], lo_i[:, :]).then_inc(s_dve, 1)
                        dve.tensor_scalar(val[:, 0, :], key[0][:, :], float(-NPAD // 2), None, ALU.add).then_inc(s_dve, 1)
                        dve.tensor_copy(recs[:, :, 1].bitcast(I32), key[1][:, :]).then_inc(s_dve, 1)
                        step.n += 4
                    else:
                        dve.tensor_scalar(val[:, 1, :], lo_i[:, :], 1.0, None, ALU.add).then_inc(s_dve, 1)
                        step.n += 2
                    dve.wait_ge(s_dve, step.n)
                    for b in range(NT):
                        dve.tensor_scalar(member[:, b, :], hi16[k][:, :], float(b), None, ALU.is_equal).then_inc(s_dve, 1)
                    step.n += NT
                    dve.wait_ge(s_dve, step.n)
                    flat = member[:, :, :].rearrange("p b c -> p (b c)")
                    step.link(dve.tensor_tensor_scan(rank[:, :, :].rearrange("p b c -> p (b c)"), flat, flat, 0.0,
                                                     ALU.add, ALU.bypass))
                    step.link(dve.memset(ends[:, 0:1], 0.0))
                    step.link(dve.tensor_copy(ends[:, 1:NT + 1], rank[:, :, EC - 1]))
                    step.link(dve.tensor_tensor(cnt[:, :], ends[:, 1:NT + 1], ends[:, 0:NT], ALU.subtract))
                    dve.sem_inc(s_cnt, 1)
                    dve.wait_ge(s_sum, k + 1)
                    step.link(dve.tensor_scalar(grp_i[:, :], acc[1][:, 0:NT], float(GROUP - 1), None, ALU.add))
                    step.link(dve.tensor_scalar(grp_i[:, :], grp_i[:, :], 8, None, ALU.logical_shift_right))
                    step.link(dve.tensor_copy(grp[:, :], grp_i[:, :]))
                    step.link(dve.tensor_tensor_scan(start[:, :], grp[:, :], grp[:, :], 0.0, ALU.add, ALU.bypass))
                    step.link(dve.tensor_tensor(start[:, :], start[:, :], grp[:, :], ALU.subtract))
                    step.link(dve.scalar_tensor_tensor(out=off[:, :], in0=start[:, :], scalar=float(GROUP),
                                                       in1=acc[0][:, 0:NT], op0=ALU.mult, op1=ALU.add))
                    step.link(dve.tensor_tensor(off[:, :], off[:, :], ends[:, 0:NT], ALU.subtract))
                    step.link(dve.tensor_scalar(off[:, :], off[:, :], -1.0, None, ALU.add))
                    for b in range(NT):
                        dve.scalar_tensor_tensor(out=rank[:, b, :], in0=rank[:, b, :], scalar=off[:, b:b + 1],
                                                 in1=member[:, b, :], op0=ALU.add, op1=ALU.mult).then_inc(s_dve, 1)
                    step.n += NT
                    dve.wait_ge(s_dve, step.n)
                    step.link(dve.tensor_reduce(pos[:, :], rank[:, :, :].rearrange("p b c -> p c b"), AX.X, ALU.add))
                    step.link(dve.scalar_tensor_tensor(out=pad_pos[:, :], in0=hi16[k][:, :], scalar=float(NT),
                                                       in1=iota_c[:, :], op0=ALU.is_equal, op1=ALU.mult))
                    slot = slot_src if k == 0 else slot_dst
                    step.link(dve.tensor_tensor(slot[:, :], pos[:, :], pad_pos[:, :], ALU.add))
                    if k == 0:
                        dve.sem_inc(s_order, 2)
                    if k == 1:
                        dve.wait_ge(s_bkt_in, 16)
                    for j in range(2):
                        step.link(dve.tensor_scalar(hit[:, :], start[:, :], gk[:, j:j + 1], None, ALU.is_le, ALU.add,
                                                    accum_out=bkt_f[:, j:j + 1]))
                    step.link(dve.tensor_scalar(bkt_i[:, :], bkt_f[:, :], -1.0, None, ALU.add))
                    dve.sem_inc(s_bkt, 1)
                step.link(dve.tensor_scalar(lo_i[:, :], slot_dst[:, :], 1, P - 1, ALU.logical_shift_right, ALU.bitwise_and))
                step.link(dve.tensor_copy(lane[:, :], lo_i[:, :]))
                step.link(dve.tensor_scalar(lo_i[:, :], slot_dst[:, :], 8, 1, ALU.logical_shift_right, ALU.logical_shift_left))
                step.link(dve.tensor_scalar(hi_i[:, :], slot_dst[:, :], 1, None, ALU.bitwise_and))
                step.link(dve.tensor_copy(col[:, :], lo_i[:, :]))
                step.link(dve.tensor_copy(pos[:, :], hi_i[:, :]))
                step.link(dve.tensor_tensor(col[:, :], col[:, :], pos[:, :], ALU.add))
                def hot(c, b):
                    dve.wait_ge(s_hot_used, c + 1)
                    dve.tensor_scalar(lane_one[b][:, :], C.iota_b[:, :], lane[:, bass.ds(c, 1)], None,
                                      ALU.is_equal).then_inc(s_lane, 1)
                    dve.tensor_scalar(col_hot[b][:, :], C.iota_h[:, :], col[:, bass.ds(c, 1)], None,
                                      ALU.is_equal).then_inc(s_col, 1)

                dve.wait_ge(s_low, 1)
                for c in chunks(dve):
                    dve.wait_ge(s_x, 16 * c + 16)
                    wait_past(dve, s_xnst, 16 * c)
                    wait_past(dve, s_tr, 4 * c)
                    layer_norm_chunk(dve, s_ln, LN_STEPS * c, xc, xnc, stats, small)
                    for t in range(CH):
                        with dve.Fori(0, TAB // UNROLL) as g:
                            for b in range(UNROLL):
                                hot((CH * c + t) * TAB + UNROLL * g + b, b % HB)
                with dve.Fori(NT * TAB // UNROLL, EC // UNROLL) as g:
                    for b in range(UNROLL):
                        hot(UNROLL * g + b, b % HB)
                dve.wait_ge(s_table, 2)
                done = step
                done.link(dve.tensor_scalar(C.gidx[:, :], acc[0][:, 0:NCOL], float(NPAD // 2), None, ALU.add))
                done.link(dve.tensor_scalar(C.dloc[:, :], acc[1][:, 0:NCOL], -1.0, None, ALU.add))

            @block.tensor
            def _(pe):
                for k in range(2):
                    pe.wait_ge(s_cnt, k + 1)
                    pe.matmul(acc[0][:, 0:NT], C.before[:, :], cnt[:, :], start=True, stop=True)
                    pe.matmul(acc[1][:, 0:NT], C.ones[:, :], cnt[:, :], start=True, stop=True).then_inc(s_sum, 1)

                def place(c, b):
                    pe.wait_ge(s_col, c + 1)
                    pe.wait_ge(s_scaled, 2 * c + 2)
                    for k in range(2):
                        last = pe.matmul(acc[k][:, 0:NCOL], lane_hot[b][:, k, :], col_hot[b][:, :], start=False,
                                         stop=False)
                    last.then_inc(s_hot_used, 1)

                def edge_of_table(first):
                    for k in range(2):
                        last = pe.matmul(acc[k][:, 0:NCOL], C.zeros[:, :], C.zeros_w[:, :], start=first, stop=not first)
                    last.then_inc(s_table, 1)

                pe.wait_ge(s_bkt, 2)
                edge_of_table(True)
                pe.sem_inc(s_hot_used, HB)
                pe.wait_ge(s_w, 32)
                for c in chunks(pe):
                    for k in range(KD):
                        for h in range(2):
                            if k == 0 and h == 0:
                                pe.wait_ge(s_ln, LN_STEPS * c + LN_STEPS)
                            tiles = range(4) if h == 0 else range(4, CH)
                            wait_past(pe, s_xt, 4 * c + 2 * k + h - 1 if k else 4 * c)
                            for t in tiles:
                                last = pe.transpose(tr[h][:, (t % 4) * P:(t % 4 + 1) * P],
                                                    xnc[:, t, k * P:(k + 1) * P], C.ident[:, :])
                            last.then_inc(s_tr, 1)
                    for t in range(CH):
                        with pe.Fori(0, TAB // UNROLL) as g:
                            for b in range(UNROLL):
                                place((CH * c + t) * TAB + UNROLL * g + b, b % HB)
                        if t == 0:
                            pe.wait_ge(s_xt, 4 * c + 4)
                        for h, freed in enumerate((s_p, s_q)):
                            wait_past(pe, freed, CH * c + max(t - 1, 0))
                            for k in range(KD):
                                last = pe.matmul(pq[h][t % 2][:, :], xtc[:, k, t * P:(t + 1) * P], w_pq[:, h, k, :],
                                                 start=(k == 0), stop=(k == KD - 1))
                            last.then_inc(s_pq, 1)
                with pe.Fori(NT * TAB // UNROLL, EC // UNROLL) as g:
                    for b in range(UNROLL):
                        place(UNROLL * g + b, b % HB)
                edge_of_table(False)


def stage_edge_network(nc, C, A, S):
    with ExitStack() as ctx:
        m = Mem(nc, ctx)
        GB, TB = 4, 8
        G, T = 2 * GB, 2 * TB
        NI = NG // G
        assert NI * G == NG
        p_hl = m.sb("p_hl", [P, NT, 2, HID], F32R)
        with ExitStack() as early:
            w_c = Mem(nc, early).sb("w_c", [P, HID])
            w_ch = Mem(nc, early).sb("w_ch", [P, HID])
        h_hi, h_lo = ([m.sb(f"h_{n}{b}", [P, HID], F32R) for b in range(2)] for n in ("hi", "lo"))
        w_cat = m.sb("w_cat", [P, HID], F32R)
        rb = [m.sb(f"rb{b}", [P, GB, 2 * REC]) for b in range(2)]
        wide = [m.sb(f"wide{b}", [P, 2, P]) for b in range(2)]
        hot = [m.sb(f"hot{b}", [P, 2, P], F32R) for b in range(4)]
        trs = [m.sb(f"trs{b}", [P, 4, P], F32R) for b in range(2)]
        qg = [m.sb(f"qg{b}", [P, HID]) for b in range(TB)]
        hb = [m.sb(f"hb{b}", [P, HID]) for b in range(4)]
        p_tr = [m.ps(f"p_tr{b}", [P, 4, P]) for b in range(2)]
        p_h = [m.ps(f"p_h{b}", [P, HID]) for b in range(4)]
        p_sum = [m.ps(f"p_sum{b}", [P, HID]) for b in range(2)]
        deg_g = m.sb("deg_g", [P, G])

        s_p, s_p_high, s_p_low = [m.sem(f"e_p{c}") for c in range(NCH)], m.sem("e_p_high"), m.sem("e_p_low")
        s_w, s_rec = m.sem("e_w"), [m.sem(f"e_rec{b}") for b in range(2)]
        s_gath = [m.sem(f"e_gath{b}") for b in range(TB)]
        s_init, s_agg_zero, s_prep = m.sem("e_init"), m.sem("e_agg_zero"), m.sem("e_prep")
        s_wide, s_hot, s_tr, s_trs = m.sem("e_wide"), m.sem("e_hot"), m.sem("e_tr"), m.sem("e_trs")
        s_h, s_add, s_relu, s_low, s_sum, s_acc = (
            m.sem(n) for n in ("e_h", "e_add", "e_relu", "e_low", "e_sum", "e_acc"))
        recs_v = S.recs[0:NSLOT, :].rearrange("(g p j) w -> p g (j w)", p=P, j=2)

        def ahead(i, q, n):
            return (i, q + n) if q + n < G else (i + 1, q + n - G)

        def behind(i, q, n):
            return (i, q - n) if q >= n else (i - 1, q - n + G)

        def edges(i, step):
            step(0, True, False)
            with i.Fori(1, NI - 1) as it:
                step(it, False, False)
            step(NI - 1, False, True)

        with nc.Block() as block:
            @block.sync
            def _(sp):
                c0 = 2 * D
                for n in range(2):
                    sp.dma_start(rb[n][:, :, :], recs_v[:, GB * n:GB * n + GB, :]).then_inc(s_rec[n], 16)
                sp.wait_ge(s_init, 1)
                for r in range(4):
                    sp.dma_start(w_c[16 * r:16 * r + 16, :], A.mW1[c0:c0 + EDGE_DIM, :]).then_inc(s_w, 16)
                for r in range(2):
                    sp.dma_start(w_c[64 + r:65 + r, :], A.mb1.rearrange("(a n) -> a n", a=1)).then_inc(s_w, 16)
                for c in range(NCH):
                    sp.dma_start(p_hl[:, c * CH:(c + 1) * CH, 1, :].bitcast(F32), chunk(S.p, c)).then_inc(s_p[c], 16)
                with sp.Fori(1, NI) as i:
                    for b in range(2):
                        sp.wait_ge(s_add, T * i + TB * b - TB)
                        sp.dma_start(rb[b][:, :, :], recs_v[:, bass.ds(G * i + GB * b, GB), :]).then_inc(s_rec[b], 16)

            @block.gpsimd
            def _(pool):
                pool.memset(w_c[:, :], 0.0).then_inc(s_init, 1)
                pool.memset(C.deg_src[:, :], 0.0).then_inc(s_init, 1)
                for b in range(2):
                    pool.memset(wide[b][:, :, 64:66], 1.0).then_inc(s_init, 1)
                    pool.memset(wide[b][:, :, 66:P], 0.0).then_inc(s_init, 1)

                def gathers(i, first, last):
                    for b in range(2):
                        pool.wait_ge(s_rec[b], 16 * i + 16)
                        pool.nop(nofuse=True)
                        for r in range(TB):
                            if not (first and b == 0):
                                pool.wait_ge(s_add, T * i + TB * b - TB + r + 1)
                                pool.nop(nofuse=True)
                            at = (r % 2) * REC + 1
                            pool.indirect_dma_start(
                                qg[r][:, :], None, S.q[:, :],
                                bass.IndirectOffsetOnAxis(ap=rb[b][:, r // 2, at:at + 1].bitcast(U32), axis=0)
                            ).then_inc(s_gath[r], 16)

                edges(pool, gathers)

            @block.scalar
            def _(act):
                act.wait_ge(s_w, 96)
                act.activation(w_cat[:, :], w_c[:, :], ACT.Copy).then_inc(s_prep, 1)
                act.wait_ge(s_prep, 1)
                act.activation(w_ch[:, :], w_cat[:, :].bitcast(F32), ACT.Copy).then_inc(s_prep, 1)
                for c in range(NCH):
                    act.wait_ge(s_p[c], 16)
                    act.activation(p_hl[:, c * CH:(c + 1) * CH, 0, :], p_hl[:, c * CH:(c + 1) * CH, 1, :].bitcast(F32),
                                   ACT.Copy).then_inc(s_p_high, 1)
                act.wait_ge(s_init, 6)

                def widen(i, q):
                    b = q // GB
                    act.wait_ge(s_rec[b], 16 * i + 16)
                    src = rb[b][:, q % GB, :].rearrange("p (j w) -> p j w", w=REC)[:, :, 2:REC]
                    for h in range(2):
                        act.activation(wide[q % 2][:, :, 32 * h:32 * h + 32], src, ACT.Copy).then_inc(s_wide, 1)

                def take(i, q):
                    act.wait_ge(s_tr, G * i + q + 1)
                    act.activation(trs[q % 2][:, 0:2, :], p_tr[q % 2][:, 0:2, :], ACT.Copy).then_inc(s_trs, 1)
                    act.activation(trs[q % 2][:, 2:4, :], p_tr[q % 2][:, 2:4, :], ACT.Copy,
                                   accum_out=deg_g[:, q:q + 1]).then_inc(s_trs, 1)

                def body(i, first, last):
                    if first:
                        widen(i, 0)
                        widen(i, 1)
                        take(i, 0)
                    for q in range(G):
                        if not (last and q >= G - 2):
                            widen(*ahead(i, q, 2))
                        if not (last and q == G - 1):
                            take(*ahead(i, q, 1))
                        for j in range(2):
                            t = 2 * q + j
                            act.wait_ge(s_add, T * i + t + 1)
                            dst = hb[t % 4] if j == 0 else h_hi[q % 2]
                            act.activation(dst[:, :], hb[t % 4][:, :], ACT.Relu).then_inc(s_relu, 1)

                edges(act, body)

            @block.vector
            def _(dve):
                dve.memset(C.agg[:, :, :], 0.0).then_inc(s_agg_zero, 1)
                dve.wait_ge(s_prep, 2)
                dve.tensor_tensor(w_cat[32:64, :], w_c[32:64, :], w_ch[32:64, :], ALU.subtract).then_inc(s_prep, 1)
                dve.tensor_tensor(w_cat[64:96, :], w_c[64:96, :], w_ch[64:96, :], ALU.subtract).then_inc(s_prep, 1)
                dve.wait_ge(s_prep, 4)
                dve.tensor_copy(w_cat[64:65, :], w_ch[64:65, :]).then_inc(s_prep, 1)
                for c in range(NCH):
                    high, low = (p_hl[:, c * CH:(c + 1) * CH, n, :] for n in range(2))
                    dve.wait_ge(s_p_high, c + 1)
                    dve.tensor_tensor(low, low.bitcast(F32), high.bitcast(F32), ALU.subtract).then_inc(s_p_low, 1)

                def one_hot(i, q):
                    b = q // GB
                    dve.wait_ge(s_rec[b], 16 * i + 16)
                    for j in range(2):
                        dve.tensor_scalar(hot[q % 4][:, j, :], C.iota_f[:, :], rb[b][:, q % GB, j * REC:j * REC + 1],
                                          None, ALU.is_equal).then_inc(s_hot, 1)

                def accumulate(i, q, bucket):
                    dve.wait_ge(s_sum, G * i + q + 1)
                    wait_past(dve, s_acc, 2 * (G * i + q))
                    agg = C.agg[:, bass.ds(bucket, 1), :].rearrange("p a n -> p (a n)")
                    dve.tensor_tensor(agg, p_sum[q % 2][:, :], agg, ALU.add).then_inc(s_acc, 1)
                    deg = C.deg_src[:, bass.ds(bucket, 1)]
                    dve.tensor_tensor(deg, deg_g[:, q:q + 1], deg, ALU.add).then_inc(s_acc, 1)

                def low_part(i, q):
                    dve.wait_ge(s_relu, T * i + 2 * q + 2)
                    dve.scalar_tensor_tensor(out=h_lo[q % 2][:, :], in0=hb[(2 * q + 1) % 4][:, :], scalar=0.0,
                                             in1=h_hi[q % 2][:, :].bitcast(F32), op0=ALU.max,
                                             op1=ALU.subtract).then_inc(s_low, 1)

                def body(i, first, last):
                    if first:
                        dve.wait_ge(s_init, 6)
                        dve.wait_ge(s_agg_zero, 1)
                        one_hot(i, 0)
                        one_hot(i, 1)
                    for q in range(G):
                        if q > 0 and not (first and q < 2):
                            accumulate(*behind(i, q, 2), buckets.pop(0))
                        if not (last and q >= G - 2):
                            if not (first and q < 2):
                                dve.wait_ge(s_sum, G * i + q - 1)
                            one_hot(*ahead(i, q, 2))
                        if not (first and q == 0):
                            low_part(*behind(i, q, 1))
                        for j in range(2):
                            t = 2 * q + j
                            dve.wait_ge(s_h, T * i + t + 1)
                            dve.wait_ge(s_gath[t % TB], 16 * (2 * i + t // TB) + 16)
                            dve.tensor_tensor(hb[t % 4][:, :], p_h[t % 4][:, :], qg[t % TB][:, :],
                                              ALU.add).then_inc(s_add, 1)
                        if q == 0:
                            since = 0 if first else G * i - 2
                            count = G - 2 if first else G + 2 if last else G
                            buckets = list(load_buckets(nc, dve, C.bucket[0:1, 0, bass.ds(since, count)]))
                            if not first:
                                accumulate(i - 1, G - 2, buckets.pop(0))
                    if last:
                        low_part(i, G - 1)
                        for q in (G - 2, G - 1):
                            accumulate(i, q, buckets.pop(0))

                edges(dve, body)

            @block.tensor
            def _(pe):
                def transposes(i, q):
                    pe.wait_ge(s_wide, 2 * (G * i + q) + 2)
                    pe.wait_ge(s_hot, 2 * (G * i + q) + 2)
                    for j in range(2):
                        pe.transpose(p_tr[q % 2][:, j, :], wide[q % 2][:, j, :], C.ident[:, :])
                    for j in range(2):
                        last = pe.transpose(p_tr[q % 2][:, 2 + j, :], hot[q % 4][:, j, :].bitcast(F32), C.ident[:, :])
                    last.then_inc(s_tr, 1)

                def hidden(i, q, bucket, first):
                    pe.wait_ge(s_trs, 2 * (G * i + q) + 2)
                    for j in range(2):
                        t = 2 * q + j
                        if not (first and t < 4):
                            pe.wait_ge(s_add, T * i + t - 3)
                        for h in range(2):
                            pe.matmul(p_h[t % 4][:, :], trs[q % 2][:, 2 + j, :],
                                      p_hl[:, bass.ds(bucket, 1), h, :].rearrange("p a n -> p (a n)"),
                                      start=(h == 0), stop=False)
                        pe.matmul(p_h[t % 4][:, :], trs[q % 2][:, j, :], w_cat[:, :], start=False,
                                  stop=True).then_inc(s_h, 1)

                def sums(i, q, first):
                    if not (first and q < 2):
                        pe.wait_ge(s_acc, 2 * (G * i + q) - 2)
                    for j in range(2):
                        t = 2 * q + j
                        pe.wait_ge(s_relu, T * i + t + 1)
                        if j == 0:
                            pe.matmul(p_sum[q % 2][:, :], hot[q % 4][:, j, :].bitcast(F32), hb[t % 4][:, :],
                                      start=True, stop=False)
                        else:
                            pe.matmul(p_sum[q % 2][:, :], hot[q % 4][:, j, :], h_hi[q % 2][:, :],
                                      start=False, stop=False)
                            pe.wait_ge(s_low, G * i + q + 1)
                            pe.matmul(p_sum[q % 2][:, :], hot[q % 4][:, j, :], h_lo[q % 2][:, :],
                                      start=False, stop=True).then_inc(s_sum, 1)

                def body(i, first, last):
                    if first:
                        pe.wait_ge(s_p_low, NCH)
                        pe.wait_ge(s_prep, 5)
                        transposes(i, 0)
                    for q in range(G):
                        if not (last and q == G - 1):
                            transposes(*ahead(i, q, 1))
                        if q == 0:
                            buckets = load_buckets(nc, pe, C.bucket[0:1, 0, bass.ds(G * i, G)])
                        hidden(i, q, buckets[q], first)
                        if q > 0:
                            sums(i, q - 1, first)
                        elif not first:
                            sums(i - 1, G - 1, False)
                    if last:
                        sums(i, G - 1, False)

                edges(pe, body)


def load_buckets(nc, eng, ap):
    return nc.values_load_multi_w_load_instructions(ap, engines=[eng.engine], min_val=0, max_val=NT - 1)[1]


class Banks:

    def __init__(self, m, name, n, per):
        self.banks = [m.ps(f"{name}{b}", [P, HID]) for b in range(n)]
        self.full, self.empty, self.per = m.sem(f"{name}_full"), m.sem(f"{name}_empty"), per

    def to_fill(self, pe, c, g):
        n = len(self.banks)
        wait_past(pe, self.empty, self.per * c + (g - n + 1 if g >= n else 0))
        return self.banks[g % n]

    def to_take(self, eng, c, g):
        eng.wait_ge(self.full, self.per * c + g + 1)
        return self.banks[g % len(self.banks)]


HALVES = ((0, 3), (3, CH))


def transpose_chunk(pe, c, src, tr, ident, full, empty, blocks=KD):
    for k in range(blocks):
        for h, (a, b) in enumerate(HALVES):
            wait_past(pe, empty, 2 * blocks * c + (2 * k + h - 1 if k else 0))
            for t in range(a, b):
                last = pe.transpose(tr[h][:, (t - a) * P:(t - a + 1) * P], src[:, t, k * P:(k + 1) * P], ident)
            last.then_inc(full, 1)


def take_transposed(act, c, dst, tr, full, empty, blocks=KD):
    for k in range(blocks):
        for h, (a, b) in enumerate(HALVES):
            act.wait_ge(full, 2 * blocks * c + 2 * k + h + 1)
            act.activation(dst[:, k, a * P:b * P], tr[h][:, 0:(b - a) * P], ACT.Copy).then_inc(empty, 1)


def chunk(ap, c):
    return ap.rearrange("(t p) d -> p t d", p=P)[:, bass.ds(c * CH, CH), :]


def rows_on_partitions(w, p=P):
    return w.rearrange("(k p) n -> p k n", p=p)


def on_all(v):
    return v.rearrange("(a n) -> a n", a=1).to_broadcast([P, v.shape[0]])


def by_feature(v):
    return v.rearrange("(k p) -> p k", p=P)


def stage_update(nc, C, A, S):
    with ExitStack() as ctx:
        m = Mem(nc, ctx)
        w2 = m.sb("w2", [P, KH, D])
        b2 = m.sb("b2", [P, D])
        deg = m.sb("deg", [P, NPAD])
        u1 = m.sb("u1", [P, KH, HID])
        u1b = m.sb("u1b", [P, KH])
        u2 = m.sb("u2", [P, KH, D])
        u2b = m.sb("u2b", [P, 1, D])
        xT = m.sb("xT", [P, KD, CH * P])
        x, xn, r = m.sb("x", [P, CH, D]), m.sb("xn", [P, CH, D]), m.sb("r", [P, CH, D])
        msgT = m.sb("msgT", [P, KD, CH * P])
        uT = m.sb("uT", [P, KH, CH * P])
        x1, xn1 = m.sb("x1", [P, CH, D]), m.sb("xn1", [P, CH, D])
        stats, small = m.sb("stats2", [P, CH, 6]), m.sb("small2", [P, 5, CH])
        NA, NV = 2 * KD + 2 * KH, CH
        aggT = m.sb("aggT", [P, KH, CH * P])
        agg = m.sb("agg_c", [P, CH, HID])
        s_agg = m.sem("u_agg")
        tr = [m.ps(f"u_tr{b}", [P, HID]) for b in range(2)]
        hidden, out = Banks(m, "u_h", 4, NA), Banks(m, "u_o", 2, NV)
        s_trf, s_tre = m.sem("u_trf"), m.sem("u_tre")
        s_w, s_zero, s_deg, s_degrow = m.sem("u_w"), m.sem("u_zero"), m.sem("u_deg"), m.sem("u_degrow")
        s_xT, s_x, s_r, s_ln = m.sem("u_xT"), m.sem("u_x"), m.sem("u_r"), m.sem("u_ln")
        s_st = m.sem("u_st")

        with nc.Block() as block:
            @block.sync
            def _(sp):
                sp.dma_start(S.deg.rearrange("(t p) -> p t", p=P), C.deg_src[:, :],
                             allow_slow_non_contiguous=True).then_inc(s_deg, 16)

                def biases():
                    sp.wait_ge(s_zero, 2)
                    sp.wait_ge(s_deg, 16)
                    sp.dma_start(b2[0:1, :], A.mb2.rearrange("(a n) -> a n", a=1)).then_inc(s_w, 16)
                    sp.dma_start(deg[0:1, :], S.deg.rearrange("(a n) -> a n", a=1)).then_inc(s_w, 16)

                def load(c):
                    wait_past(sp, s_trf, 2 * KH * c)
                    sp.dma_start(agg[:, :, :], C.agg[:, bass.ds(c * CH, CH), :]).then_inc(s_agg, 16)
                    wait_past(sp, s_r, 2 * c)
                    sp.dma_start(x[:, :, :], chunk(A.x, c)).then_inc(s_x, 16)
                    sp.dma_start(xn[:, :, :], chunk(S.xn, c)).then_inc(s_x, 16)
                    wait_past(sp, hidden.full, NA * c)
                    sp.dma_start(xT[:, :, :], S.xnT.rearrange("(k p) n -> p k n", p=P)[:, :, bass.ds(c * CH * P, CH * P)]
                                 ).then_inc(s_xT, 16)

                def store(c):
                    sp.wait_ge(s_ln, LN_STEPS * c + LN_STEPS)
                    sp.dma_start(chunk(S.x1, c), x1[:, :, :]).then_inc(s_st, 16)
                    sp.dma_start(chunk(S.xn1, c), xn1[:, :, :]).then_inc(s_st, 16)

                load_ahead(sp, load, store, biases)
                sp.wait_ge(s_st, 32 * NCH)

            @block.gpsimd
            def _(pool):
                pool.memset(b2[:, :], 0.0).then_inc(s_zero, 1)
                pool.memset(deg[:, :], 0.0).then_inc(s_zero, 1)
                pool.wait_ge(s_w, 112)
                for c in chunks(pool):
                    pool.wait_ge(s_x, 32 * c + 32)
                    wait_past(pool, out.empty, NV * c)
                    pool.tensor_tensor(r[:, :, :], x[:, :, :], xn[:, :, :], ALU.add).then_inc(s_r, 1)
                    pool.wait_ge(s_r, 2 * c + 1)
                    pool.tensor_tensor(r[:, :, :], r[:, :, :], u2b[:, :, :].to_broadcast([P, CH, D]),
                                       ALU.add).then_inc(s_r, 1)

            @block.scalar
            def _(act):
                act.dma_start(w2[:, :, :], rows_on_partitions(A.mW2)).then_inc(s_w, 16)
                act.dma_start(u1[:, :, :], rows_on_partitions(A.uW1)).then_inc(s_w, 16)
                act.dma_start(u2[:, :, :], rows_on_partitions(A.uW2)).then_inc(s_w, 16)
                act.dma_start(u1b[:, :], by_feature(A.ub1), allow_slow_non_contiguous=True).then_inc(s_w, 16)
                act.dma_start(u2b[:, 0, :], on_all(A.ub2)).then_inc(s_w, 16)
                for c in chunks(act):
                    take_transposed(act, c, aggT, tr, s_trf, s_tre, KH)
                    if isinstance(c, int):
                        act.wait_ge(s_w, 112)
                    for k in range(KD):
                        for h, (a, b) in enumerate(HALVES):
                            g = 2 * k + h
                            src = hidden.to_take(act, c, g)
                            act.activation(msgT[:, k, a * P:b * P], src[:, 0:(b - a) * P], ACT.Copy).then_inc(hidden.empty, 1)
                    for k in range(KH):
                        for h, (a, b) in enumerate(HALVES):
                            g = 2 * KD + 2 * k + h
                            src = hidden.to_take(act, c, g)
                            act.activation(uT[:, k, a * P:b * P], src[:, 0:(b - a) * P], ACT.Relu,
                                           bias=u1b[:, k:k + 1]).then_inc(hidden.empty, 1)

            @block.vector
            def _(dve):
                for c in chunks(dve):
                    dve.wait_ge(s_r, 2 * c + 2)
                    wait_past(dve, s_st, 32 * c)
                    for t in range(CH):
                        src = out.to_take(dve, c, t)
                        dve.tensor_tensor(x1[:, t, :], src[:, 0:D], r[:, t, :], ALU.add).then_inc(out.empty, 1)
                    dve.wait_ge(out.empty, NV * c + NV)
                    layer_norm_chunk(dve, s_ln, LN_STEPS * c, x1, xn1, stats, small)

            @block.tensor
            def _(pe):
                for c in chunks(pe):
                    pe.wait_ge(s_agg, 16 * c + 16)
                    transpose_chunk(pe, c, agg, tr, C.ident[:, :], s_trf, s_tre, KH)
                    pe.wait_ge(s_tre, 2 * KH * (c + 1))
                    if isinstance(c, int):
                        pe.wait_ge(s_w, 112)
                    for k in range(KD):
                        for h, (a, b) in enumerate(HALVES):
                            dst = hidden.to_fill(pe, c, 2 * k + h)[:, 0:(b - a) * P]
                            for j in range(KH):
                                pe.matmul(dst, w2[:, j, k * P:(k + 1) * P], aggT[:, j, a * P:b * P],
                                          start=(j == 0), stop=False)
                            pe.matmul(dst, b2[:, k * P:(k + 1) * P], deg[:, bass.ds((c * CH + a) * P, (b - a) * P)],
                                      start=False, stop=True).then_inc(hidden.full, 1)
                    pe.wait_ge(s_xT, 16 * c + 16)
                    for k in range(KH):
                        for h, (a, b) in enumerate(HALVES):
                            dst = hidden.to_fill(pe, c, 2 * KD + 2 * k + h)[:, 0:(b - a) * P]
                            for j in range(KD):
                                pe.matmul(dst, u1[:, j, k * P:(k + 1) * P], xT[:, j, a * P:b * P], start=(j == 0), stop=False)
                            if k == 0:
                                pe.wait_ge(hidden.empty, NA * c + 2 * KD)
                            for j in range(KD):
                                last = pe.matmul(dst, u1[:, KD + j, k * P:(k + 1) * P], msgT[:, j, a * P:b * P],
                                                 start=False, stop=(j == KD - 1))
                            last.then_inc(hidden.full, 1)
                    pe.wait_ge(hidden.empty, NA * c + NA)
                    for t in range(CH):
                        dst = out.to_fill(pe, c, t)[:, 0:D]
                        for j in range(KH):
                            last = pe.matmul(dst, uT[:, j, t * P:(t + 1) * P], u2[:, j, :], start=(j == 0), stop=(j == KH - 1))
                        last.then_inc(out.full, 1)
        m.clear_sems()


def stage_experts(nc, C, A, S):
    NE, EH1, EH2 = A.eW1.shape[0], A.eW1.shape[2], A.eW2.shape[2]
    SH1, SH2 = A.sW1.shape[1], A.sW2.shape[1]
    KS = SH1 // P
    assert EH1 == P and SH2 == P and EH2 < P
    with ExitStack() as ctx:
        m = Mem(nc, ctx)
        w_s1, w_s2, w_s3 = m.sb("w_s1", [P, KD, SH1]), m.sb("w_s2", [P, KS, SH2]), m.sb("w_s3", [P, D])
        b_s1, b_s2, b_s3 = m.sb("b_s1", [P, KS]), m.sb("b_s2", [P, 1]), m.sb("b_s3", [P, 1, D])
        w_e1, w_e2 = m.sb("w_e1", [P, NE, KD, EH1]), m.sb("w_e2", [P, NE, EH2])
        w_e3 = m.sb("w_e3", [P, NE, D])
        b_e1, b_e2 = m.sb("b_e1", [P, NE]), m.sb("b_e2", [EH2, NE])
        w_g, b_g = m.sb("w_g", [P, KD, NE]), m.sb("b_g", [P, 1, NE])
        prio_i, prio = m.sb("prio_i", [P, 1, NE], I32), m.sb("prio", [P, 1, NE])
        x1, xn1, r, x2, xn2 = (m.sb(f"m_{n}", [P, CH, D]) for n in ("x1", "xn1", "r", "x2", "xn2"))
        xT = m.sb("m_xT", [P, KD, CH * P])
        h1, h2 = m.sb("h1", [P, KS, CH * P]), m.sb("h2", [P, CH * P])
        e1, e2 = m.sb("e1", [P, NE, CH * P]), m.sb("e2", [P, NE, CH * P])
        lg, ex, gt, key, first, second = (m.sb(f"g_{n}", [P, CH, NE]) for n in ("lg", "ex", "gt", "key", "first", "second"))
        c1, c2, c3, c4, c5, c6 = (m.sb(f"g_c{n}", [P, CH, 1]) for n in range(6))
        stats, small = m.sb("stats3", [P, CH, 6]), m.sb("small3", [P, 5, CH])
        NA, NV = 2 * (KS + 1 + 2 * NE), 1 + 3 * CH
        tr = [m.ps(f"m_tr{b}", [P, HID]) for b in range(2)]
        hidden, out = Banks(m, "m_h", 3, NA), Banks(m, "m_o", 3, NV)
        s_w, s_zero, s_x, s_trf, s_tre = (m.sem(f"m_{n}") for n in ("w", "zero", "x", "trf", "tre"))
        s_r, s_ln, s_st = (m.sem(f"m_{n}") for n in ("r", "ln", "st"))
        s_g, s_lg, s_ex, s_mix, s_prio = (m.sem(f"m_{n}") for n in ("g", "lg", "ex", "mix", "prio"))
        A_GROUPS = [("s1", k) for k in range(KS)] + [("e1", e) for e in range(NE)] + [("s2", 0)] + \
                   [("e2", e) for e in range(NE)]
        GSTEPS, MIX = 23, 5 * CH

        with nc.Block() as block:
            @block.sync
            def _(sp):
                def weights():
                    for e in range(NE):
                        sp.dma_start(w_e1[:, e, :, :], rows_on_partitions(A.eW1[e])).then_inc(s_w, 16)
                    for dst, src in ((w_s2[:, :, :], rows_on_partitions(A.sW2)), (w_s3[:, :], A.sW3),
                                     (w_e2[:, :, :], A.eW2.rearrange("e p n -> p e n"))):
                        sp.dma_start(dst, src).then_inc(s_w, 16)
                    sp.wait_ge(s_zero, 2)
                    for dst, src in ((w_e3[0:EH2, :, :], A.eW3.rearrange("e p n -> p e n")),
                                     (w_e3[EH2:EH2 + 1, :, :], A.eb3.rearrange("(a e) n -> a e n", a=1))):
                        sp.dma_start(dst, src).then_inc(s_w, 16)

                def load(c):
                    wait_past(sp, s_trf, 4 * c)
                    wait_past(sp, s_r, c)
                    sp.dma_start(xn1[:, :, :], chunk(S.xn1, c)).then_inc(s_x, 16)
                    sp.dma_start(x1[:, :, :], chunk(S.x1, c)).then_inc(s_x, 16)

                def store(c):
                    sp.wait_ge(s_ln, LN_STEPS * c + LN_STEPS)
                    sp.dma_start(chunk(S.x2, c), x2[:, :, :]).then_inc(s_st, 16)
                    sp.dma_start(chunk(S.xn2, c), xn2[:, :, :]).then_inc(s_st, 16)

                load_ahead(sp, load, store, weights)
                sp.wait_ge(s_st, 32 * NCH)

            @block.gpsimd
            def _(pool):
                pool.memset(w_e3[64:P, :, :], 0.0).then_inc(s_zero, 1)
                pool.memset(e2[64:P, :, :], 0.0).then_inc(s_zero, 1)
                pool.wait_ge(s_zero, 2)
                pool.memset(e2[EH2:EH2 + 1, :, :], 1.0).then_inc(s_zero, 1)
                pool.wait_ge(s_zero, 3)
                pool.iota(prio_i[:, :, :], [[-1, NE]], base=NE, channel_multiplier=0).then_inc(s_prio, 1)
                pool.wait_ge(s_w, 16 * (13 + NE))
                for c in chunks(pool):
                    pool.wait_ge(s_x, 32 * c + 32)
                    wait_past(pool, out.empty, NV * c)
                    pool.tensor_tensor(r[:, :, :], x1[:, :, :], b_s3[:, :, :].to_broadcast([P, CH, D]),
                                       ALU.add).then_inc(s_r, 1)

            @block.scalar
            def _(act):
                for dst, src in ((w_s1[:, :, :], rows_on_partitions(A.sW1)), (w_g[:, :, :], rows_on_partitions(A.gW)),
                                 (b_g[:, 0, :], on_all(A.gb)), (b_s1[:, :], by_feature(A.sb1)),
                                 (b_e1[:, :], A.eb1.rearrange("e p -> p e")), (b_s2[:, :], by_feature(A.sb2)),
                                 (b_e2[:, :], A.eb2.rearrange("e p -> p e")), (b_s3[:, 0, :], on_all(A.sb3))):
                    act.dma_start(dst, src, allow_slow_non_contiguous=True).then_inc(s_w, 16)
                for c in chunks(act):
                    take_transposed(act, c, xT, tr, s_trf, s_tre)
                    if isinstance(c, int):
                        act.wait_ge(s_w, 16 * (13 + NE))
                        act.wait_ge(s_zero, 3)
                    for n, (kind, k) in enumerate(A_GROUPS):
                        if n == KS:
                            act.wait_ge(s_lg, 2 * c + 1)
                            act.activation(ex[:, :, :], lg[:, :, :], ACT.Exp).then_inc(s_ex, 1)
                        if n == KS + NE:
                            act.wait_ge(s_lg, 2 * c + 2)
                            act.activation(c4[:, :, :], c3[:, :, :], ACT.Exp).then_inc(s_ex, 1)
                        dst, bias = {"s1": (h1[:, k % KS, :], b_s1[:, k % KS:k % KS + 1]), "s2": (h2[:, :], b_s2[:, 0:1]),
                                     "e1": (e1[:, k % NE, :], b_e1[:, k % NE:k % NE + 1]),
                                     "e2": (e2[0:EH2, k % NE, :], b_e2[:, k % NE:k % NE + 1])}[kind]
                        for h, (a, b) in enumerate(HALVES):
                            src = hidden.to_take(act, c, 2 * n + h)
                            act.activation(dst[:, a * P:b * P], src[0:dst.shape[0], 0:(b - a) * P], ACT.Relu,
                                           bias=bias).then_inc(hidden.empty, 1)

            @block.vector
            def _(dve):
                dve.wait_ge(s_prio, 1)
                dve.tensor_copy(prio[:, :, :], prio_i[:, :, :]).then_inc(s_prio, 1)
                dve.wait_ge(s_w, 16 * (13 + NE))
                wide = [P, CH, NE]

                def gates(c):
                    n = [0]

                    def step(ins):
                        ins.then_inc(s_g, 1)
                        n[0] += 1
                        dve.wait_ge(s_g, GSTEPS * c + n[0])

                    def pick(values, top, hit):
                        step(dve.tensor_reduce(top[:, :, 0], values[:, :, :], AX.X, ALU.max))
                        step(dve.tensor_tensor(key[:, :, :], values[:, :, :], top[:, :, :].to_broadcast(wide), ALU.is_equal))
                        step(dve.tensor_tensor(key[:, :, :], key[:, :, :], prio[:, :, :].to_broadcast(wide), ALU.mult))
                        step(dve.tensor_reduce(c6[:, :, 0], key[:, :, :], AX.X, ALU.max))
                        step(dve.tensor_tensor(hit[:, :, :], key[:, :, :], c6[:, :, :].to_broadcast(wide), ALU.is_equal))

                    logits = out.to_take(dve, c, 0)[:, 0:CH * NE].rearrange("p (t e) -> p t e", e=NE)
                    ins = dve.tensor_tensor(lg[:, :, :], logits, b_g[:, :, :].to_broadcast(wide), ALU.add)
                    step(ins)
                    dve.sem_inc(out.empty, 1)
                    step(dve.tensor_reduce(c1[:, :, 0], lg[:, :, :], AX.X, ALU.max))
                    dve.tensor_tensor(lg[:, :, :], lg[:, :, :], c1[:, :, :].to_broadcast(wide), ALU.subtract).then_inc(s_lg, 1)
                    dve.wait_ge(s_ex, 2 * c + 1)
                    step(dve.tensor_reduce(c1[:, :, 0], ex[:, :, :], AX.X, ALU.add))
                    step(dve.reciprocal(c2[:, :, :], c1[:, :, :]))
                    step(dve.tensor_tensor(gt[:, :, :], ex[:, :, :], c2[:, :, :].to_broadcast(wide), ALU.mult))
                    pick(gt, c1, first)
                    step(dve.scalar_tensor_tensor(out=gt[:, :, :], in0=first[:, :, :], scalar=-2.0, in1=gt[:, :, :],
                                                  op0=ALU.mult, op1=ALU.add))
                    pick(gt, c2, second)
                    dve.tensor_tensor(c3[:, :, :], c2[:, :, :], c1[:, :, :], ALU.subtract).then_inc(s_lg, 1)
                    dve.wait_ge(s_ex, 2 * c + 2)
                    step(dve.tensor_scalar(c1[:, :, :], c4[:, :, :], 1.0, None, ALU.add))
                    step(dve.reciprocal(c5[:, :, :], c1[:, :, :]))
                    step(dve.tensor_tensor(c4[:, :, :], c4[:, :, :], c5[:, :, :], ALU.mult))
                    step(dve.tensor_tensor(first[:, :, :], first[:, :, :], c5[:, :, :].to_broadcast(wide), ALU.mult))
                    step(dve.tensor_tensor(second[:, :, :], second[:, :, :], c4[:, :, :].to_broadcast(wide), ALU.mult))
                    step(dve.tensor_tensor(gt[:, :, :], first[:, :, :], second[:, :, :], ALU.add))
                    step(dve.tensor_copy(key[:, :, :], gt[:, :, :]))
                    assert n[0] == GSTEPS, n[0]

                for c in chunks(dve):
                    dve.wait_ge(s_prio, 2)
                    gates(c)
                    dve.wait_ge(s_r, c + 1)
                    wait_past(dve, s_st, 32 * c)
                    for t in range(CH):
                        for n in range(3):
                            src = out.to_take(dve, c, 1 + 3 * t + n)
                            for j in range(2 if n < 2 else 1):
                                term = 2 * n + j
                                if term == 0:
                                    ins = dve.tensor_tensor(x2[:, t, :], src[:, 0:D], r[:, t, :], ALU.add)
                                else:
                                    dve.wait_ge(s_mix, MIX * c + 5 * t + term)
                                    ins = dve.scalar_tensor_tensor(out=x2[:, t, :], in0=src[:, j * D:(j + 1) * D],
                                                                   scalar=gt[:, t, term - 1:term], in1=x2[:, t, :],
                                                                   op0=ALU.mult, op1=ALU.add)
                                ins.then_inc(s_mix, 1)
                            dve.wait_ge(s_mix, MIX * c + 5 * t + min(2 * n + 2, 5))
                            dve.sem_inc(out.empty, 1)
                    layer_norm_chunk(dve, s_ln, LN_STEPS * c, x2, xn2, stats, small)

            @block.tensor
            def _(pe):
                for c in chunks(pe):
                    pe.wait_ge(s_x, 32 * c + 32)
                    transpose_chunk(pe, c, xn1, tr, C.ident[:, :], s_trf, s_tre)
                    if isinstance(c, int):
                        pe.wait_ge(s_w, 16 * (13 + NE))
                    pe.wait_ge(s_tre, 4 * c + 4)
                    dst = out.to_fill(pe, c, 0)
                    for t in range(CH):
                        for j in range(KD):
                            last = pe.matmul(dst[:, t * NE:(t + 1) * NE], xT[:, j, t * P:(t + 1) * P], w_g[:, j, :],
                                             start=(t == 0 and j == 0), stop=(j == KD - 1), skip_group_check=True)
                    last.then_inc(out.full, 1)
                    for n, (kind, k) in enumerate(A_GROUPS):
                        rows = EH2 if kind == "e2" else P
                        if kind == "s2":
                            pe.wait_ge(hidden.empty, NA * c + 2 * KS)
                        if kind == "e2":
                            pe.wait_ge(hidden.empty, NA * c + 2 * (KS + k + 1))
                        for h, (a, b) in enumerate(HALVES):
                            dst = hidden.to_fill(pe, c, 2 * n + h)[0:rows, 0:(b - a) * P]
                            if kind == "s1":
                                terms = [(w_s1[:, j, k * P:(k + 1) * P], xT[:, j, a * P:b * P]) for j in range(KD)]
                            elif kind == "e1":
                                terms = [(w_e1[:, k, j, :], xT[:, j, a * P:b * P]) for j in range(KD)]
                            elif kind == "s2":
                                terms = [(w_s2[:, j, :], h1[:, j, a * P:b * P]) for j in range(KS)]
                            else:
                                terms = [(w_e2[:, k, :], e1[:, k, a * P:b * P])]
                            for j, (w, v) in enumerate(terms):
                                last = pe.matmul(dst, w, v, start=(j == 0), stop=(j == len(terms) - 1))
                            last.then_inc(hidden.full, 1)
                    pe.wait_ge(hidden.empty, NA * c + NA)
                    for t in range(CH):
                        for n in range(3):
                            dst = out.to_fill(pe, c, 1 + 3 * t + n)
                            for j in range(2 if n < 2 else 1):
                                term = 2 * n + j
                                v, w = (h2[:, t * P:(t + 1) * P], w_s3[:, :]) if term == 0 else \
                                    (e2[:, term - 1, t * P:(t + 1) * P], w_e3[:, term - 1, :])
                                last = pe.matmul(dst[:, j * D:(j + 1) * D], v, w, start=(j == 0), stop=True,
                                                 skip_group_check=True)
                            last.then_inc(out.full, 1)

        m.clear_sems()


def stage_project(nc, C, A, S, layer):
    W_l = A.W_l1 if layer == 0 else A.W_l2
    with ExitStack() as ctx:
        m = Mem(nc, ctx, f"project{layer}_")
        w_l, b_r = m.sb("w_l", [P, KD, D]), m.sb("b_r", [P, 1, D])
        x, y = m.sb("x", [P, CH, D]), m.sb("y", [P, CH, D])
        h, rdeg = m.sb("h", [P, CH, D]), m.sb("rdeg", [P, CH, 1])
        xT = m.sb("xT", [P, KD, CH * P])
        tr = [m.ps(f"tr{b}", [P, HID]) for b in range(2)]
        out = Banks(m, "o", 4, CH)
        s_w, s_x, s_trf, s_tre, s_h, s_y_st, s_xT_st = (
            m.sem(n) for n in ("w", "x", "trf", "tre", "h", "y_st", "xT_st"))
        HSTEPS = 3 + CH
        X = 16 if layer == 0 else 1

        with nc.Block() as block:
            @block.sync
            def _(sp):
                sp.dma_start(w_l[:, :, :], rows_on_partitions(W_l)).then_inc(s_w, 16)
                sp.dma_start(b_r[:, 0, :], on_all(A.b1)).then_inc(s_w, 16)

                def load(c):
                    if layer == 0:
                        wait_past(sp, s_trf, 4 * c)
                        sp.dma_start(x[:, :, :], chunk(S.xn2, c)).then_inc(s_x, 16)

                def store(c):
                    sp.wait_ge(s_tre, 4 * c + 4)
                    sp.dma_start(S.xT.rearrange("(k p) n -> p k n", p=P)[:, :, bass.ds(c * CH * P, CH * P)],
                                 xT[:, :, :]).then_inc(s_xT_st, 16)
                    sp.wait_ge(out.empty, CH * c + CH)
                    sp.dma_start(chunk(S.y, c), y[:, :, :]).then_inc(s_y_st, 16)

                load_ahead(sp, load, store)
                sp.wait_ge(s_xT_st, 16 * NCH)
                sp.wait_ge(s_y_st, 16 * NCH)

            @block.scalar
            def _(act):
                for c in chunks(act):
                    if layer == 1:
                        act.wait_ge(s_h, HSTEPS * c + HSTEPS)
                        wait_past(act, s_trf, 4 * c)
                        act.activation(x[:, :, :], h[:, :, :], ACT.Relu).then_inc(s_x, 1)
                    wait_past(act, out.full, CH * c)
                    wait_past(act, s_xT_st, 16 * c)
                    take_transposed(act, c, xT, tr, s_trf, s_tre)

            @block.vector
            def _(dve):
                def second_rows(c):
                    at = HSTEPS * c
                    dve.tensor_scalar(rdeg[:, :, :], C.nbr[:, bass.ds(c * CH, CH), D:D + 1], 1.0, None,
                                      ALU.max).then_inc(s_h, 1)
                    dve.wait_ge(s_h, at + 1)
                    dve.reciprocal(rdeg[:, :, :], rdeg[:, :, :]).then_inc(s_h, 1)
                    dve.wait_ge(s_h, at + 2)
                    wait_past(dve, s_x, c)
                    for t in range(CH):
                        tile = bass.ds(c * CH + t, 1)
                        dve.scalar_tensor_tensor(out=h[:, t, :], in0=C.nbr[:, tile, 0:D].rearrange("p a n -> p (a n)"),
                                                 scalar=rdeg[:, t, :], in1=C.z[:, tile, :].rearrange("p a n -> p (a n)"),
                                                 op0=ALU.mult, op1=ALU.add).then_inc(s_h, 1)
                    dve.wait_ge(s_h, at + 2 + CH)
                    dve.tensor_tensor(h[:, :, :], h[:, :, :], b_r[:, :, :].to_broadcast([P, CH, D]), ALU.add).then_inc(s_h, 1)

                def products(c):
                    wait_past(dve, s_y_st, 16 * c)
                    for t in range(CH):
                        src = out.to_take(dve, c, t)
                        dve.tensor_copy(y[:, t, :], src[:, 0:D]).then_inc(out.empty, 1)

                dve.wait_ge(s_w, 32)
                if layer == 0:
                    for c in chunks(dve):
                        products(c)
                else:
                    second_rows(0)
                    second_rows(1)
                    products(0)
                    with dve.Fori(1, NCH - 1) as c:
                        second_rows(c + 1)
                        products(c)
                    products(NCH - 1)

            @block.tensor
            def _(pe):
                pe.wait_ge(s_w, 32)
                for c in chunks(pe):
                    pe.wait_ge(s_x, X * c + X)
                    transpose_chunk(pe, c, x, tr, C.ident[:, :], s_trf, s_tre)
                    pe.wait_ge(s_tre, 4 * c + 4)
                    for t in range(CH):
                        dst = out.to_fill(pe, c, t)
                        for k in range(KD):
                            last = pe.matmul(dst[:, 0:D], xT[:, k, t * P:(t + 1) * P], w_l[:, k, :], start=(k == 0),
                                             stop=(k == KD - 1))
                        last.then_inc(out.full, 1)
        m.clear_sems()


def stage_neighbours(nc, C, A, S, layer):
    W_r = A.W_r1 if layer == 0 else A.W_r2
    with ExitStack() as ctx:
        m = Mem(nc, ctx, f"nbr{layer}_")
        TB, GB = 8, 4
        T, G = 2 * TB, 2 * GB
        NI = NG // G
        assert NT + 1 < NI - 1
        W = D + 2
        idx = [m.sb(f"idx{b}", [P, TB], U32) for b in range(2)]
        yg = [m.sb(f"yg{b}", [P, W]) for b in range(TB)]
        hot = [m.sb(f"hot{b}", [P, 2, P]) for b in range(4)]
        w_r, xT = m.sb("w_r", [P, KD, D]), m.sb("xT", [P, KD, P])
        p_sum = [m.ps(f"sum{b}", [P, HID]) for b in range(2)]
        p_z = m.ps("z", [P, HID])
        s_zero, s_idx, s_hot, s_sum, s_acc = (m.sem(n) for n in ("zero", "idx", "hot", "sum", "acc"))
        s_w, s_xT, s_z, s_z_taken, s_nbr_zero = (m.sem(n) for n in ("w", "xT", "z", "z_taken", "nbr_zero"))
        s_gath = [m.sem(f"gath{b}") for b in range(TB)]

        def ahead(i, q, n):
            return (i, q + n) if q + n < G else (i + 1, q + n - G)

        def bodies(eng, step):
            step(0, True, False, None)
            with eng.Fori(1, NT + 1) as it:
                step(it, False, False, it - 1)
            with eng.Fori(NT + 1, NI - 1) as it:
                step(it, False, False, None)
            step(NI - 1, False, True, None)

        with nc.Block() as block:
            @block.sync
            def _(sp):
                sp.dma_start(w_r[:, :, :], rows_on_partitions(W_r)).then_inc(s_w, 16)
                xT_v = S.xT.rearrange("(k p) n -> p k n", p=P)
                sp.dma_start(xT[:, :, :], xT_v[:, :, 0:P]).then_inc(s_xT, 16)
                with sp.Fori(1, NT) as t:
                    sp.wait_ge(s_z, t)
                    sp.dma_start(xT[:, :, :], xT_v[:, :, bass.ds(t * P, P)]).then_inc(s_xT, 16)

            @block.gpsimd
            def _(pool):
                for b in range(TB):
                    pool.memset(yg[b][:, D:W], 1.0).then_inc(s_zero, 1)

                def gathers(i, first, last, tile):
                    for b in range(2):
                        pool.wait_ge(s_idx, 2 * i + b + 1)
                        pool.nop(nofuse=True)
                        for r in range(TB):
                            if not (first and b == 0) and r % 2 == 0:
                                pool.wait_ge(s_sum, G * i + GB * b - GB + r // 2 + 1)
                                pool.nop(nofuse=True)
                            pool.indirect_dma_start(yg[r][:, 0:D], None, S.y[:, :],
                                                    bass.IndirectOffsetOnAxis(ap=idx[b][:, r:r + 1], axis=0)
                                                    ).then_inc(s_gath[r], 16)

                bodies(pool, gathers)

            @block.scalar
            def _(act):
                act.sem_inc(s_z_taken, 1)

                def body(i, first, last, tile):
                    for b in range(2):
                        if not first:
                            act.wait_ge(s_sum, G * i + GB * b - GB)
                        act.activation(idx[b][:, :].bitcast(F32), C.gidx[:, bass.ds(T * i + TB * b, TB)].bitcast(F32),
                                       ACT.Copy).then_inc(s_idx, 1)
                    if tile is not None:
                        act.wait_ge(s_z, i)
                        act.activation(C.z[:, bass.ds(tile, 1), :].rearrange("p a n -> p (a n)"), p_z[:, 0:D],
                                       ACT.Copy).then_inc(s_z_taken, 1)

                bodies(act, body)

            @block.vector
            def _(dve):
                def one_hot(i, q):
                    for j in range(2):
                        dve.tensor_scalar(hot[q % 4][:, j, :], C.iota_f[:, :],
                                          C.dloc[:, bass.ds(T * i + 2 * q + j, 1)], None, ALU.is_equal).then_inc(s_hot, 1)

                def accumulate(i, q, bucket):
                    dve.wait_ge(s_sum, G * i + q + 1)
                    wait_past(dve, s_acc, G * i + q)
                    nbr = C.nbr[:, bass.ds(bucket, 1), :].rearrange("p a n -> p (a n)")
                    dve.tensor_tensor(nbr, p_sum[q % 2][:, 0:W], nbr, ALU.add).then_inc(s_acc, 1)

                def body(i, first, last, tile):
                    if first:
                        dve.memset(C.nbr[:, :, :], 0.0).then_inc(s_nbr_zero, 1)
                        dve.wait_ge(s_nbr_zero, 1)
                        one_hot(i, 0)
                        one_hot(i, 1)
                        buckets = [None] + list(load_buckets(nc, dve, C.bucket[0:1, 1, 0:G]))
                    else:
                        buckets = load_buckets(nc, dve, C.bucket[0:1, 1, bass.ds(G * i - 1, G + 1)])
                    for q in range(G):
                        if q > 0:
                            accumulate(i, q - 1, buckets[q])
                        elif not first:
                            accumulate(i - 1, G - 1, buckets[0])
                        if not (last and q >= G - 2):
                            one_hot(*ahead(i, q, 2))
                    if last:
                        accumulate(i, G - 1, buckets[G])

                bodies(dve, body)

            @block.tensor
            def _(pe):
                pe.wait_ge(s_w, 16)
                pe.wait_ge(s_zero, TB)

                def body(i, first, last, tile):
                    if tile is not None:
                        pe.wait_ge(s_xT, 16 * i)
                        pe.wait_ge(s_z_taken, i)
                        for k in range(KD):
                            mm = pe.matmul(p_z[:, 0:D], xT[:, k, :], w_r[:, k, :], start=(k == 0), stop=(k == KD - 1))
                        mm.then_inc(s_z, 1)
                    for q in range(G):
                        if not (first and q < 2):
                            pe.wait_ge(s_acc, G * i + q - 1)
                        pe.wait_ge(s_hot, T * i + 2 * q + 2)
                        for j in range(2):
                            t = 2 * q + j
                            pe.wait_ge(s_gath[t % TB], 16 * (2 * i + t // TB) + 16)
                            last_mm = pe.matmul(p_sum[q % 2][:, 0:W], hot[q % 4][:, j, :], yg[t % TB][:, :],
                                                start=(j == 0), stop=(j == 1))
                        last_mm.then_inc(s_sum, 1)

                bodies(pe, body)


def stage_last(nc, C, A, S, out_ap):
    NHID = A.w1.shape[1]
    KF = NHID // P
    KEEP = max(1, N_NODES // 2) - 1
    with ExitStack() as ctx:
        m = Mem(nc, ctx, "last_")
        w1, b1 = m.sb("w1", [P, KD, NHID]), m.sb("b1", [P, KF])
        w2, b2 = m.sb("w2", [P, KF, D]), m.sb("b2", [P, 1, D])
        b_r, wr, br = m.sb("b_r", [P, 1, D]), m.sb("wr", [P, D]), m.sb("br", [P, 1])
        rdeg = m.sb("rdeg", [P, NT, 1])
        xr, r, x3, y, xn = (m.sb(n, [P, CH, D]) for n in ("xr", "r", "x3", "y", "xn"))
        stats, small = m.sb("stats", [P, CH, 6]), m.sb("small", [P, 5, CH])
        row_junk = m.sb("row_junk", [P, D])
        route = m.sb("route", [P, NT])
        raw_route = m.sb("raw_route", [P, NT])
        row = m.sb("row", [P, N_NODES])
        junk, junk2 = m.sb("junk", [P, N_NODES], BF16), m.sb("junk2", [P, P])
        after = m.sb("after", [P, P])
        counts = m.sb("counts", [P, NT, 3])
        rank, gate = m.sb("rank", [P, NT]), m.sb("gate", [P, NT])
        xT = m.sb("xT", [P, KD, CH * P])
        hT = m.sb("hT", [P, KF, CH * P])
        NA = 2 * KF
        tr = [m.ps(f"tr{b}", [P, HID]) for b in range(2)]
        hidden, out = Banks(m, "h", 4, NA), Banks(m, "o", 2, CH)
        s_w, s_w_sage, s_br, s_xr, s_r, s_deg, s_x3, s_ln, s_weigh = (
            m.sem(n) for n in ("w", "w_sage", "br", "xr", "r", "deg", "x3", "ln", "weigh"))
        s_xn_st, s_xn, s_trf, s_tre, s_sum, s_b2 = (m.sem(n) for n in ("xn_st", "xn", "trf", "tre", "sum", "b2"))
        s_route, s_row, s_row_in, s_dve, s_out, s_st = (
            m.sem(n) for n in ("route", "row", "row_in", "dve", "out", "st"))

        with nc.Block() as block:
            @block.sync
            def _(sp):
                sp.dma_start(b_r[:, 0, :], on_all(A.b2)).then_inc(s_w_sage, 16)
                sp.dma_start(wr[:, :], on_all(A.wr.rearrange("d a -> (d a)"))).then_inc(s_w_sage, 16)
                sp.dma_start(xr[:, :, :], chunk(S.x2, 0)).then_inc(s_xr, 16)
                sp.dma_start(w1[:, :, :], rows_on_partitions(A.w1)).then_inc(s_w, 16)
                sp.dma_start(b1[:, :], by_feature(A.b1f), allow_slow_non_contiguous=True).then_inc(s_w, 16)
                sp.dma_start(w2[:, :, :], rows_on_partitions(A.w2)).then_inc(s_w, 16)
                sp.dma_start(b2[:, 0, :], on_all(A.b2f)).then_inc(s_w, 16)
                sp.dma_start(br[:, :], on_all(A.br)).then_inc(s_br, 16)

                def load(c):
                    if not (isinstance(c, int) and c == 0):
                        sp.wait_ge(s_r, 2 * c)
                        sp.dma_start(xr[:, :, :], chunk(S.x2, c)).then_inc(s_xr, 16)

                def store(c):
                    sp.wait_ge(s_ln, LN_STEPS * c + LN_STEPS)
                    sp.dma_start(chunk(S.xn3, c), y[:, :, :]).then_inc(s_xn_st, 16)

                load_ahead(sp, load, store)
                sp.wait_ge(s_route, 1)
                sp.dma_start(S.route.rearrange("(t p) -> p t", p=P), route[:, :],
                             allow_slow_non_contiguous=True).then_inc(s_row, 16)
                sp.wait_ge(s_row, 16)
                sp.dma_start(row[:, :], on_all(S.route[0:N_NODES])).then_inc(s_row_in, 16)
                for c in chunks(sp):
                    sp.wait_ge(s_out, CH * c + CH)
                    sp.dma_start(chunk(out_ap, c), C.nbr[:, bass.ds(c * CH, CH), 0:D]).then_inc(s_st, 16)
                sp.wait_ge(s_st, 16 * NCH)

            @block.gpsimd
            def _(pool):
                pool.wait_ge(s_w_sage, 32)

                def addends(c):
                    pool.wait_ge(s_xr, 16 * c + 16)
                    wait_past(pool, s_x3, (CH + 1) * c)
                    pool.tensor_tensor(r[:, :, :], xr[:, :, :], C.z[:, bass.ds(c * CH, CH), :], ALU.add).then_inc(s_r, 1)
                    pool.wait_ge(s_r, 2 * c + 1)
                    pool.tensor_tensor(r[:, :, :], r[:, :, :], b_r[:, :, :].to_broadcast([P, CH, D]),
                                       ALU.add).then_inc(s_r, 1)

                def residual(c):
                    pool.wait_ge(s_ln, LN_STEPS * c + LN_STEPS)
                    pool.tensor_tensor(C.z[:, bass.ds(c * CH, CH), :], x3[:, :, :], y[:, :, :], ALU.add).then_inc(s_sum, 1)

                load_ahead(pool, addends, residual)
                pool.wait_ge(s_w, 64)
                for c in chunks(pool):
                    pool.wait_ge(out.empty, CH * c + CH)
                    pool.tensor_tensor(C.nbr[:, bass.ds(c * CH, CH), 0:D], C.nbr[:, bass.ds(c * CH, CH), 0:D],
                                       b2[:, :, :].to_broadcast([P, CH, D]), ALU.add).then_inc(s_b2, 1)

            @block.scalar
            def _(act):
                def load_xn(c):
                    act.wait_ge(s_xn_st, 16 * c + 16)
                    act.dma_start(xn[:, :, :], chunk(S.xn3, c)).then_inc(s_xn, 16)

                def body(c, last):
                    take_transposed(act, c, xT, tr, s_trf, s_tre)
                    if not last:
                        load_xn(c + 1)
                    for k in range(KF):
                        for h, (a, b) in enumerate(HALVES):
                            src = hidden.to_take(act, c, 2 * k + h)
                            act.activation(hT[:, k, a * P:b * P], src[:, 0:(b - a) * P], ACT.Gelu_apprx_tanh,
                                           bias=b1[:, k:k + 1]).then_inc(hidden.empty, 1)
                    for t in range(CH):
                        src = out.to_take(act, c, t)
                        act.activation(C.nbr[:, bass.ds(c * CH + t, 1), 0:D].rearrange("p a n -> p (a n)"), src[:, 0:D],
                                       ACT.Copy).then_inc(out.empty, 1)

                act.wait_ge(s_w, 64)
                load_xn(0)
                body(0, False)
                with act.Fori(1, NCH - 1) as c:
                    body(c, False)
                body(NCH - 1, True)

            @block.vector
            def _(dve):
                step = Chain(dve, s_deg)
                step.link(dve.tensor_scalar(rdeg[:, :, :], C.nbr[:, :, D:D + 1], 1.0, None, ALU.max))
                step.link(dve.reciprocal(rdeg[:, :, :], rdeg[:, :, :]))
                dve.wait_ge(s_w_sage, 32)
                for c in chunks(dve):
                    wait_past(dve, s_xn_st, 16 * c)
                    wait_past(dve, s_sum, c)
                    dve.wait_ge(s_r, 2 * c + 2)
                    for t in range(CH):
                        tile = bass.ds(c * CH + t, 1)
                        dve.scalar_tensor_tensor(out=x3[:, t, :], in0=C.nbr[:, tile, 0:D].rearrange("p a n -> p (a n)"),
                                                 scalar=rdeg[:, tile, :].rearrange("p a n -> p (a n)"), in1=r[:, t, :],
                                                 op0=ALU.mult, op1=ALU.add).then_inc(s_x3, 1)
                    dve.wait_ge(s_x3, (CH + 1) * c + CH)
                    dve.sem_inc(s_x3, 1)
                    layer_norm_chunk(dve, s_ln, LN_STEPS * c, x3, y, stats, small)
                    dve.wait_ge(s_ln, LN_STEPS * c + LN_STEPS)
                    for t in range(CH):
                        wait_past(dve, s_weigh, CH * c + t)
                        dve.scalar_tensor_tensor(out=row_junk[:, :], in0=y[:, t, :], scalar=1.0, in1=wr[:, :],
                                                 op0=ALU.mult, op1=ALU.mult,
                                                 accum_out=raw_route[:, bass.ds(c * CH + t, 1)]).then_inc(s_weigh, 1)
                step = Chain(dve, s_dve)
                dve.wait_ge(s_br, 16)
                dve.wait_ge(s_weigh, NT)
                dve.tensor_scalar(route[:, :], raw_route[:, :], br[:, 0:1], None, ALU.add).then_inc(s_route, 1)
                step.link(dve.tensor_scalar(after[:, :], C.iota_f[:, :], C.part_f[:, 0:1], None, ALU.is_lt))
                step.link(dve.memset(counts[:, :, :], 0.0))
                dve.wait_ge(s_route, 1)
                dve.wait_ge(s_row_in, 16)
                for t in range(NT):
                    a, b = t * P, min((t + 1) * P, N_NODES)
                    own = route[:, t:t + 1]
                    if t > 0:
                        step.link(dve.tensor_scalar(junk[:, 0:a], row[:, 0:a], own, None, ALU.is_ge, ALU.add,
                                                    accum_out=counts[:, t, 0:1]))
                    step.link(dve.tensor_scalar(junk[:, a:N_NODES], row[:, a:N_NODES], own, None, ALU.is_gt, ALU.add,
                                                accum_out=counts[:, t, 1:2]))
                    step.link(dve.scalar_tensor_tensor(out=junk2[:, 0:b - a], in0=row[:, a:b], scalar=own,
                                                       in1=after[:, 0:b - a], op0=ALU.is_equal, op1=ALU.mult,
                                                       accum_out=counts[:, t, 2:3]))
                step.link(dve.tensor_reduce(rank[:, :], counts[:, :, :], AX.X, ALU.add))
                step.link(dve.scalar_tensor_tensor(out=gate[:, :], in0=rank[:, :], scalar=float(KEEP), in1=route[:, :],
                                                   op0=ALU.is_lt, op1=ALU.mult))
                for c in chunks(dve):
                    dve.wait_ge(s_b2, c + 1)
                    for t in range(CH):
                        tile = bass.ds(c * CH + t, 1)
                        rows = C.nbr[:, tile, 0:D].rearrange("p a n -> p (a n)")
                        dve.scalar_tensor_tensor(out=rows, in0=rows, scalar=gate[:, tile],
                                                 in1=C.z[:, tile, :].rearrange("p a n -> p (a n)"),
                                                 op0=ALU.mult, op1=ALU.add).then_inc(s_out, 1)

            @block.tensor
            def _(pe):
                pe.wait_ge(s_w, 64)
                for c in chunks(pe):
                    pe.wait_ge(s_xn, 16 * c + 16)
                    transpose_chunk(pe, c, xn, tr, C.ident[:, :], s_trf, s_tre)
                    pe.wait_ge(s_tre, 4 * c + 4)
                    for k in range(KF):
                        for h, (a, b) in enumerate(HALVES):
                            dst = hidden.to_fill(pe, c, 2 * k + h)[:, 0:(b - a) * P]
                            for j in range(KD):
                                last = pe.matmul(dst, w1[:, j, k * P:(k + 1) * P], xT[:, j, a * P:b * P],
                                                 start=(j == 0), stop=(j == KD - 1))
                            last.then_inc(hidden.full, 1)
                    pe.wait_ge(hidden.empty, NA * c + NA)
                    for t in range(CH):
                        dst = out.to_fill(pe, c, t)[:, 0:D]
                        for j in range(KF):
                            last = pe.matmul(dst, hT[:, j, t * P:(t + 1) * P], w2[:, j, :], start=(j == 0), stop=(j == KF - 1))
                        last.then_inc(out.full, 1)


def build(nc, A, out):
    with ExitStack() as ctx:
        m = Mem(nc, ctx)
        C, S = Names(), Names()
        C.iota_i = m.sb("iota_i", [P, P], I32)
        C.iota_f = m.sb("iota_f", [P, P])
        C.iota_b = m.sb("iota_b", [P, P], F16)
        C.iota_h = m.sb("iota_h", [P, NCOL], I16)
        C.part_i = m.sb("part_i", [P, 1], I32)
        C.part_f = m.sb("part_f", [P, 1])
        C.ident = m.sb("ident", [P, P])
        C.before = m.sb("before", [P, P])
        C.ones = m.sb("ones", [P, P])
        C.zeros = m.sb("zeros", [P, P], F16)
        C.zeros_w = m.sb("zeros_w", [P, NCOL], F16)
        C.bucket = m.sb("bucket", [1, 2, NG], I32)
        C.gidx = m.sb("gidx", [P, NCOL], U32)
        C.dloc = m.sb("dloc", [P, NCOL])

        def dram(name, shape, dt=F32):
            return nc.dram_tensor(name, shape, dt).ap()

        S.recs = dram("recs_d", [NSLOT + EC, REC])
        S.bucket, S.bucket2 = dram("bucket_d", [NG], I32), dram("bucket2_d", [NG], I32)
        S.xn, S.xn1, S.xn2, S.xn3, S.x1, S.x2, S.y = (
            dram(f"{n}_d", [NPAD, D]) for n in ("xn", "xn1", "xn2", "xn3", "x1", "x2", "y"))
        S.xnT, S.xT = dram("xnT_d", [D, NPAD]), dram("xT_d", [D, NPAD])
        S.p, S.q = dram("p_d", [NPAD, HID]), dram("q_d", [NPAD, HID])
        S.deg, S.route = dram("deg_d", [NPAD]), dram("route_d", [NPAD])

        stage_constants(nc, C)
        stage_prepare(nc, C, A, S)
        with ExitStack() as edge_ctx:
            e = Mem(nc, edge_ctx)
            C.agg = e.sb("agg", [P, NT, HID])
            C.deg_src = e.sb("deg_src", [P, NT])
            stage_edge_network(nc, C, A, S)
            stage_update(nc, C, A, S)
        stage_experts(nc, C, A, S)
        with ExitStack() as sage_ctx:
            e = Mem(nc, sage_ctx)
            C.nbr = e.sb("nbr", [P, NT, D + 2])
            C.z = e.sb("z", [P, NT, D])
            for layer in range(2):
                stage_project(nc, C, A, S, layer)
                stage_neighbours(nc, C, A, S, layer)
            stage_last(nc, C, A, S, out)


_INS = {"mW1": "L0_gnn_mW1", "mb1": "L0_gnn_mb1", "mW2": "L0_gnn_mW2", "mb2": "L0_gnn_mb2", "uW1": "L0_gnn_uW1",
        "ub1": "L0_gnn_ub1", "uW2": "L0_gnn_uW2", "ub2": "L0_gnn_ub2", "sW1": "L0_ffn_sW1", "sb1": "L0_ffn_sb1",
        "sW2": "L0_ffn_sW2", "sb2": "L0_ffn_sb2", "sW3": "L0_ffn_sW3", "sb3": "L0_ffn_sb3", "eW1": "L0_ffn_eW1",
        "eb1": "L0_ffn_eb1", "eW2": "L0_ffn_eW2", "eb2": "L0_ffn_eb2", "eW3": "L0_ffn_eW3", "eb3": "L0_ffn_eb3",
        "gW": "L0_ffn_gW", "gb": "L0_ffn_gb", "W_l1": "L1_gnn_W_l1", "b1": "L1_gnn_b1", "W_r1": "L1_gnn_W_r1",
        "W_l2": "L1_gnn_W_l2", "b2": "L1_gnn_b2", "W_r2": "L1_gnn_W_r2", "wr": "L1_ffn_wr", "br": "L1_ffn_br",
        "w1": "L1_ffn_w1", "b1f": "L1_ffn_b1", "w2": "L1_ffn_w2", "b2f": "L1_ffn_b2"}


def kernel(**inputs):
    import numpy as _np
    import concourse.bacc as _bacc
    from concourse import mybir as _mybir
    from concourse.bass_utils import run_bass_kernel_spmd as _run

    def padded(name, rows, fill):
        a = _np.asarray(inputs[name])
        whole = _np.full((rows,) + a.shape[1:], fill, a.dtype)
        whole[:a.shape[0]] = a
        return whole

    host = {"x": padded("x", NPAD, 0), "src": padded("src", EPAD, NPAD), "dst": padded("dst", EPAD, NPAD),
            "edge_attr": padded("edge_attr_16", EPAD, 0)}
    for short, name in _INS.items():
        host[short] = _np.ascontiguousarray(inputs[name])
    nc = _bacc.Bacc("TRN2", target_bir_lowering=False, num_devices=1)
    A, arrays = Names(), {}
    for short, a in host.items():
        arrays[f"in_{short}"] = a
        setattr(A, short, nc.dram_tensor(f"in_{short}", a.shape, _mybir.dt.from_np(a.dtype), kind="ExternalInput").ap())
    out = nc.dram_tensor("out_0", (NPAD, D), F32, kind="ExternalOutput").ap()
    build(nc, A, out)
    r = _run(nc, [arrays], core_ids=[0])
    return r.results[0]["out_0"][:N_NODES]
```
